# Optimizing a Trainium2 kernel written in Bass

```python
import numpy as np
import jax
import jax.numpy as jnp

def _softmax(x, axis=-1):
    return jax.nn.softmax(x, axis=axis)

def _gelu(x):
    return jax.nn.gelu(x, approximate=True)

def _silu(x):
    return jax.nn.silu(x)

def _sigmoid(x):
    return jax.nn.sigmoid(x)

def _layernorm(x, axis=-1, eps=1e-05):
    m = jnp.mean(x, axis=axis, keepdims=True)
    v = jnp.var(x, axis=axis, keepdims=True)
    return (x - m) / jnp.sqrt(v + eps)

def _scatter_add(tgt, idx, src, axis=0):
    return tgt.at[idx].add(src)

def _segment_sum(src, seg, n):
    return jax.ops.segment_sum(src, seg, n)
kernel_name = 'mk_decoder_preln_d2_seqx_r8_d7836f'

def setup_inputs(seed: int=0):
    np.random.seed(seed)
    _w = jnp.asarray

    def _rec_inputs():
        import jax
        import jax.numpy as jnp
        _rk = jax.random.key(seed)
        x = -0.0003929 + 0.9999 * jax.random.normal(jax.random.fold_in(_rk, 1), (16, 128, 128), jnp.float32)
        _lenS = 128 - jax.random.randint(jax.random.fold_in(_rk, 7), (16,), 0, max(1, 128 // 4) + 1, jnp.int32)
        _lenS2 = 120 - jax.random.randint(jax.random.fold_in(_rk, 8), (16,), 0, max(1, 120 // 4) + 1, jnp.int32)
        _ctx_768P = jax.random.normal(jax.random.fold_in(_rk, 11), (16, 16, 96), jnp.float32)
        _ctx_768c = jax.random.dirichlet(jax.random.fold_in(_rk, 511), 0.3 * jnp.ones((16,), jnp.float32), (16, 120))
        _ctx_768t = jnp.einsum('bsk,bkd->bsd', _ctx_768c, _ctx_768P)
        _ctx_768t = _ctx_768t * jax.lax.rsqrt(jnp.mean(jnp.square(_ctx_768t)) + 1e-12) * 0.953939
        ctx_768 = -0.00055796 + 0.999787 * (_ctx_768t + 0.3 * jax.random.normal(jax.random.fold_in(_rk, 611), (16, 120, 96), jnp.float32))
        return (x, ctx_768)
    x, ctx_768 = _rec_inputs()

    def _L0_attn_setup():
        import math
        import jax, jax.numpy as jnp
        import numpy as np
        B, T, D_MODEL, N_HEADS = (2, 256, 128, 16)
        HEAD_DIM = D_MODEL // N_HEADS

        def _alibi_slopes(n_heads: int) -> np.ndarray:

            def pow2(n):
                start = 2.0 ** (-(8.0 / n))
                return [start * start ** i for i in range(n)]
            if math.log2(n_heads).is_integer():
                s = pow2(n_heads)
            else:
                cp = 2 ** math.floor(math.log2(n_heads))
                base = pow2(cp)
                extra = pow2(2 * cp)[1::2]
                s = base + extra[:n_heads - cp]
            return np.asarray(s, dtype=np.float32)
        SLOPES = jnp.asarray(_alibi_slopes(N_HEADS))
        key = jax.random.key(seed)
        k1, k2, k3 = jax.random.split(key, 3)
        x = jax.random.normal(k1, (B, T, D_MODEL), dtype=jnp.float32)
        Wqkv = jax.random.normal(k2, (D_MODEL, 3 * D_MODEL), dtype=jnp.float32) * 0.02
        Wout = jax.random.normal(k3, (D_MODEL, D_MODEL), dtype=jnp.float32) * 0.02
        return {'x': x, 'Wqkv': Wqkv, 'Wout': Wout}
    _L0_attn_all = _L0_attn_setup()
    _L0_attn_in = {k: v for k, v in _L0_attn_all.items() if k in ('Wqkv', 'Wout')}
    del _L0_attn_all

    def _L0_xattn_setup():
        import jax, jax.numpy as jnp
        import numpy as np
        IMAGE_DIM = 128
        TEXT_DIM = 96
        NUM_HEADS = 16
        HEAD_DIM = IMAGE_DIM // NUM_HEADS
        key = jax.random.key(seed)
        ks = jax.random.split(key, 14)
        B, N, M = (4, 512, 64)
        s_img = 1.0 / np.sqrt(IMAGE_DIM)
        s_txt = 1.0 / np.sqrt(TEXT_DIM)
        s_ff = 1.0 / np.sqrt(2 * IMAGE_DIM)
        return {'x': jax.random.normal(ks[0], (B, N, IMAGE_DIM), jnp.float32), 'y': jax.random.normal(ks[1], (B, M, TEXT_DIM), jnp.float32), 'Wq': jax.random.normal(ks[2], (IMAGE_DIM, IMAGE_DIM), jnp.float32) * s_img, 'bq': jax.random.normal(ks[3], (IMAGE_DIM,), jnp.float32) * s_img, 'Wk': jax.random.normal(ks[4], (TEXT_DIM, IMAGE_DIM), jnp.float32) * s_txt, 'bk': jax.random.normal(ks[5], (IMAGE_DIM,), jnp.float32) * s_txt, 'Wv': jax.random.normal(ks[6], (TEXT_DIM, IMAGE_DIM), jnp.float32) * s_txt, 'bv': jax.random.normal(ks[7], (IMAGE_DIM,), jnp.float32) * s_txt, 'W1': jax.random.normal(ks[8], (IMAGE_DIM, 2 * IMAGE_DIM), jnp.float32) * s_img, 'b1': jax.random.normal(ks[9], (2 * IMAGE_DIM,), jnp.float32) * s_img, 'W2': jax.random.normal(ks[10], (2 * IMAGE_DIM, IMAGE_DIM), jnp.float32) * s_ff, 'b2': jax.random.normal(ks[11], (IMAGE_DIM,), jnp.float32) * s_ff}
    _L0_xattn_all = _L0_xattn_setup()
    _L0_xattn_in = {k: v for k, v in _L0_xattn_all.items() if k in ('Wq', 'bq', 'Wk', 'bk', 'Wv', 'bv', 'W1', 'b1', 'W2', 'b2')}
    del _L0_xattn_all

    def _L0_ffn_setup():
        import jax, jax.numpy as jnp
        import numpy as np
        C = 1.0
        EPS = 1e-06
        DIM = 128
        INTER = 64
        N_EXP = 16
        TOPK = 2
        SH_INTER = 2 * INTER
        B, S = (1, 64)
        ROUTE_SCALE = 1.0

        def _time(space):
            return jnp.sqrt(jnp.clip(jnp.sum(space * space, -1, keepdims=True) + C, EPS))

        def _llinear(x, W, b):
            s = x @ W.T + b
            return jnp.concatenate([_time(s), s], axis=-1)

        def _lmlp(x, W1, b1, W3, b3, W2, b2):
            a = jax.nn.silu(_llinear(x, W1, b1)[..., 1:])
            s = a * _llinear(x, W3, b3)[..., 1:]
            h = jnp.concatenate([_time(s), s], axis=-1)
            return _llinear(h, W2, b2)

        def _lresnet(x, y, w):
            z = x + w * y
            inner = -z[..., :1] ** 2 + jnp.sum(z[..., 1:] ** 2, -1, keepdims=True)
            return jnp.sqrt(C) * z / jnp.sqrt(jnp.clip(-inner, EPS))
        key = jax.random.key(seed)
        ks = jax.random.split(key, 16)
        sc = 0.02
        xs = jax.random.normal(ks[0], (B, S, DIM - 1), jnp.float32)
        x = jnp.concatenate([jnp.sqrt(jnp.sum(xs ** 2, -1, keepdims=True) + C), xs], -1)
        f32 = jnp.float32
        return {'x': x, 'gate_w': jax.random.normal(ks[1], (N_EXP, DIM), f32) * sc, 'We1': jax.random.normal(ks[2], (N_EXP, INTER - 1, DIM), f32) * sc, 'be1': jnp.zeros((N_EXP, INTER - 1), f32), 'We3': jax.random.normal(ks[3], (N_EXP, INTER - 1, DIM), f32) * sc, 'be3': jnp.zeros((N_EXP, INTER - 1), f32), 'We2': jax.random.normal(ks[4], (N_EXP, DIM - 1, INTER), f32) * sc, 'be2': jnp.zeros((N_EXP, DIM - 1), f32), 'Ws1': jax.random.normal(ks[5], (SH_INTER - 1, DIM), f32) * sc, 'bs1': jnp.zeros((SH_INTER - 1,), f32), 'Ws3': jax.random.normal(ks[6], (SH_INTER - 1, DIM), f32) * sc, 'bs3': jnp.zeros((SH_INTER - 1,), f32), 'Ws2': jax.random.normal(ks[7], (DIM - 1, SH_INTER), f32) * sc, 'bs2': jnp.zeros((DIM - 1,), f32)}
    _L0_ffn_all = _L0_ffn_setup()
    _L0_ffn_in = {k: v for k, v in _L0_ffn_all.items() if k in ('gate_w', 'We1', 'be1', 'We3', 'be3', 'We2', 'be2', 'Ws1', 'bs1', 'Ws3', 'bs3', 'Ws2', 'bs2')}
    del _L0_ffn_all

    def _L1_attn_setup():
        import jax, jax.numpy as jnp
        import numpy as np
        H = 128
        NH = 16
        HD = H // NH
        B, S = (2, 256)
        key = jax.random.key(seed)
        ks = jax.random.split(key, 6)
        std = 0.02
        x = jax.random.normal(ks[0], (B, S, H), dtype=jnp.float32)
        w_qkv = jax.random.normal(ks[1], (3 * H, H), dtype=jnp.float32) * std
        b_qkv = jnp.zeros((3 * H,), dtype=jnp.float32)
        ln_g = jnp.ones((H,), dtype=jnp.float32)
        ln_b = jnp.zeros((H,), dtype=jnp.float32)
        w_ent = jax.random.normal(ks[2], (1, H), dtype=jnp.float32) * std
        b_ent = jnp.zeros((1,), dtype=jnp.float32)
        w_out = jax.random.normal(ks[3], (H, H), dtype=jnp.float32) * std
        b_out = jnp.zeros((H,), dtype=jnp.float32)
        return {'x': x, 'ln_g': ln_g, 'ln_b': ln_b, 'w_qkv': w_qkv, 'b_qkv': b_qkv, 'w_ent': w_ent, 'b_ent': b_ent, 'w_out': w_out, 'b_out': b_out}
    _L1_attn_all = _L1_attn_setup()
    _L1_attn_in = {k: v for k, v in _L1_attn_all.items() if k in ('ln_g', 'ln_b', 'w_qkv', 'b_qkv', 'w_ent', 'b_ent', 'w_out', 'b_out')}
    del _L1_attn_all

    def _L1_xattn_setup():
        import jax, jax.numpy as jnp
        import numpy as np
        HEADS = 16
        DIM_HEAD = 64
        QUERY_DIM = 128
        CONTEXT_DIM = 96
        INNER = HEADS * DIM_HEAD
        SCALE = DIM_HEAD ** (-0.5)
        key = jax.random.key(seed)
        ks = jax.random.split(key, 7)
        B, Sq, Skv = (4, 256, 256)
        x = jax.random.normal(ks[0], (B, Sq, QUERY_DIM), dtype=jnp.float32)
        context = jax.random.normal(ks[1], (B, Skv, CONTEXT_DIM), dtype=jnp.float32)
        w_q = jax.random.normal(ks[2], (QUERY_DIM, INNER), dtype=jnp.float32) / np.sqrt(QUERY_DIM)
        w_k = jax.random.normal(ks[3], (CONTEXT_DIM, INNER), dtype=jnp.float32) / np.sqrt(CONTEXT_DIM)
        w_v = jax.random.normal(ks[4], (CONTEXT_DIM, INNER), dtype=jnp.float32) / np.sqrt(CONTEXT_DIM)
        w_o = jax.random.normal(ks[5], (INNER, QUERY_DIM), dtype=jnp.float32) / np.sqrt(INNER)
        b_o = jax.random.normal(ks[6], (QUERY_DIM,), dtype=jnp.float32) * 0.02
        return {'x': x, 'context': context, 'w_q': w_q, 'w_k': w_k, 'w_v': w_v, 'w_o': w_o, 'b_o': b_o}
    _L1_xattn_all = _L1_xattn_setup()
    _L1_xattn_in = {k: v for k, v in _L1_xattn_all.items() if k in ('w_q', 'w_k', 'w_v', 'w_o', 'b_o')}
    del _L1_xattn_all

    def _L1_ffn_setup():
        import jax, jax.numpy as jnp
        import numpy as np
        H = 128
        I = 512
        E = 4
        LN_EPS = 1e-12

        def _layer_norm(x, gamma, beta, eps=LN_EPS):
            mu = jnp.mean(x, axis=-1, keepdims=True)
            var = jnp.mean(jnp.square(x - mu), axis=-1, keepdims=True)
            return (x - mu) * jax.lax.rsqrt(var + eps) * gamma + beta
        key = jax.random.key(seed)
        ks = jax.random.split(key, 8)
        B, S = (4, 64)
        scale = 0.02
        return {'hidden_states': jax.random.normal(ks[0], (B, S, H), jnp.float32), 'W_router': jax.random.normal(ks[1], (H, E), jnp.float32) * scale, 'W1': jax.random.normal(ks[2], (E, H, I), jnp.float32) * scale, 'b1': jax.random.normal(ks[3], (E, I), jnp.float32) * scale, 'Wo': jax.random.normal(ks[4], (I, H), jnp.float32) * scale, 'bo': jax.random.normal(ks[5], (H,), jnp.float32) * scale, 'ln_gamma': jnp.ones((H,), jnp.float32), 'ln_beta': jnp.zeros((H,), jnp.float32)}
    _L1_ffn_all = _L1_ffn_setup()
    _L1_ffn_in = {k: v for k, v in _L1_ffn_all.items() if k in ('W_router', 'W1', 'b1', 'Wo', 'bo', 'ln_gamma', 'ln_beta')}
    del _L1_ffn_all
    return {'x': x, 'ctx_768': ctx_768, 'L0_attn_Wqkv': _L0_attn_in['Wqkv'], 'L0_attn_Wout': _L0_attn_in['Wout'], 'L0_xattn_Wq': _L0_xattn_in['Wq'], 'L0_xattn_bq': _L0_xattn_in['bq'], 'L0_xattn_Wk': _L0_xattn_in['Wk'], 'L0_xattn_bk': _L0_xattn_in['bk'], 'L0_xattn_Wv': _L0_xattn_in['Wv'], 'L0_xattn_bv': _L0_xattn_in['bv'], 'L0_xattn_W1': _L0_xattn_in['W1'], 'L0_xattn_b1': _L0_xattn_in['b1'], 'L0_xattn_W2': _L0_xattn_in['W2'], 'L0_xattn_b2': _L0_xattn_in['b2'], 'L0_ffn_gate_w': _L0_ffn_in['gate_w'], 'L0_ffn_We1': _L0_ffn_in['We1'], 'L0_ffn_be1': _L0_ffn_in['be1'], 'L0_ffn_We3': _L0_ffn_in['We3'], 'L0_ffn_be3': _L0_ffn_in['be3'], 'L0_ffn_We2': _L0_ffn_in['We2'], 'L0_ffn_be2': _L0_ffn_in['be2'], 'L0_ffn_Ws1': _L0_ffn_in['Ws1'], 'L0_ffn_bs1': _L0_ffn_in['bs1'], 'L0_ffn_Ws3': _L0_ffn_in['Ws3'], 'L0_ffn_bs3': _L0_ffn_in['bs3'], 'L0_ffn_Ws2': _L0_ffn_in['Ws2'], 'L0_ffn_bs2': _L0_ffn_in['bs2'], 'L1_attn_ln_g': _L1_attn_in['ln_g'], 'L1_attn_ln_b': _L1_attn_in['ln_b'], 'L1_attn_w_qkv': _L1_attn_in['w_qkv'], 'L1_attn_b_qkv': _L1_attn_in['b_qkv'], 'L1_attn_w_ent': _L1_attn_in['w_ent'], 'L1_attn_b_ent': _L1_attn_in['b_ent'], 'L1_attn_w_out': _L1_attn_in['w_out'], 'L1_attn_b_out': _L1_attn_in['b_out'], 'L1_xattn_w_q': _L1_xattn_in['w_q'], 'L1_xattn_w_k': _L1_xattn_in['w_k'], 'L1_xattn_w_v': _L1_xattn_in['w_v'], 'L1_xattn_w_o': _L1_xattn_in['w_o'], 'L1_xattn_b_o': _L1_xattn_in['b_o'], 'L1_ffn_W_router': _L1_ffn_in['W_router'], 'L1_ffn_W1': _L1_ffn_in['W1'], 'L1_ffn_b1': _L1_ffn_in['b1'], 'L1_ffn_Wo': _L1_ffn_in['Wo'], 'L1_ffn_bo': _L1_ffn_in['bo'], 'L1_ffn_ln_gamma': _L1_ffn_in['ln_gamma'], 'L1_ffn_ln_beta': _L1_ffn_in['ln_beta']}

def reference(x, ctx_768, L0_attn_Wqkv, L0_attn_Wout, L0_xattn_Wq, L0_xattn_bq, L0_xattn_Wk, L0_xattn_bk, L0_xattn_Wv, L0_xattn_bv, L0_xattn_W1, L0_xattn_b1, L0_xattn_W2, L0_xattn_b2, L0_ffn_gate_w, L0_ffn_We1, L0_ffn_be1, L0_ffn_We3, L0_ffn_be3, L0_ffn_We2, L0_ffn_be2, L0_ffn_Ws1, L0_ffn_bs1, L0_ffn_Ws3, L0_ffn_bs3, L0_ffn_Ws2, L0_ffn_bs2, L1_attn_ln_g, L1_attn_ln_b, L1_attn_w_qkv, L1_attn_b_qkv, L1_attn_w_ent, L1_attn_b_ent, L1_attn_w_out, L1_attn_b_out, L1_xattn_w_q, L1_xattn_w_k, L1_xattn_w_v, L1_xattn_w_o, L1_xattn_b_o, L1_ffn_W_router, L1_ffn_W1, L1_ffn_b1, L1_ffn_Wo, L1_ffn_bo, L1_ffn_ln_gamma, L1_ffn_ln_beta):
    import jax
    import jax.numpy as jnp

    def _L0_attn_ref(x, Wqkv, Wout):
        import math
        import jax, jax.numpy as jnp
        import numpy as np
        B, T, D_MODEL, N_HEADS = (2, 256, 128, 16)
        HEAD_DIM = D_MODEL // N_HEADS

        def _alibi_slopes(n_heads: int) -> np.ndarray:

            def pow2(n):
                start = 2.0 ** (-(8.0 / n))
                return [start * start ** i for i in range(n)]
            if math.log2(n_heads).is_integer():
                s = pow2(n_heads)
            else:
                cp = 2 ** math.floor(math.log2(n_heads))
                base = pow2(cp)
                extra = pow2(2 * cp)[1::2]
                s = base + extra[:n_heads - cp]
            return np.asarray(s, dtype=np.float32)
        SLOPES = jnp.asarray(_alibi_slopes(N_HEADS))
        Bc, Tc, Dc = x.shape
        qkv = x @ Wqkv
        q, k, v = jnp.split(qkv, 3, axis=-1)
        q = q.reshape(Bc, Tc, N_HEADS, HEAD_DIM)
        k = k.reshape(Bc, Tc, N_HEADS, HEAD_DIM)
        v = v.reshape(Bc, Tc, N_HEADS, HEAD_DIM)
        scale = 1.0 / math.sqrt(HEAD_DIM)
        logits = jnp.einsum('bihd,bjhd->bhij', q, k) * scale
        pos = jnp.arange(Tc, dtype=jnp.float32)
        rel = pos[None, :] - pos[:, None]
        logits = logits + SLOPES[None, :, None, None] * rel[None, None, :, :]
        causal = pos[:, None] >= pos[None, :]
        logits = jnp.where(causal[None, None, :, :], logits, -jnp.inf)
        attn = jax.nn.softmax(logits, axis=-1)
        out = jnp.einsum('bhij,bjhd->bihd', attn, v).reshape(Bc, Tc, Dc)
        return out @ Wout

    def _L0_xattn_ref(x, y, Wq, bq, Wk, bk, Wv, bv, W1, b1, W2, b2):
        import jax, jax.numpy as jnp
        import numpy as np
        IMAGE_DIM = 128
        TEXT_DIM = 96
        NUM_HEADS = 16
        HEAD_DIM = IMAGE_DIM // NUM_HEADS
        B, N, _ = x.shape
        M = y.shape[1]
        q = (x @ Wq + bq).reshape(B, N, NUM_HEADS, HEAD_DIM)
        k = (y @ Wk + bk).reshape(B, M, NUM_HEADS, HEAD_DIM)
        v = (y @ Wv + bv).reshape(B, M, NUM_HEADS, HEAD_DIM)
        scale = 1.0 / np.sqrt(HEAD_DIM)
        scores = jnp.einsum('bnhd,bmhd->bhnm', q, k) * scale
        attn = jax.nn.softmax(scores, axis=-1)
        out = jnp.einsum('bhnm,bmhd->bnhd', attn, v).reshape(B, N, IMAGE_DIM)
        h = jax.nn.relu(out @ W1 + b1)
        return h @ W2 + b2

    def _L0_ffn_ref(x, gate_w, We1, be1, We3, be3, We2, be2, Ws1, bs1, Ws3, bs3, Ws2, bs2):
        import jax, jax.numpy as jnp
        import numpy as np
        C = 1.0
        EPS = 1e-06
        DIM = 128
        INTER = 64
        N_EXP = 16
        TOPK = 2
        SH_INTER = 2 * INTER
        B, S = (1, 64)
        ROUTE_SCALE = 1.0

        def _time(space):
            return jnp.sqrt(jnp.clip(jnp.sum(space * space, -1, keepdims=True) + C, EPS))

        def _llinear(x, W, b):
            s = x @ W.T + b
            return jnp.concatenate([_time(s), s], axis=-1)

        def _lmlp(x, W1, b1, W3, b3, W2, b2):
            a = jax.nn.silu(_llinear(x, W1, b1)[..., 1:])
            s = a * _llinear(x, W3, b3)[..., 1:]
            h = jnp.concatenate([_time(s), s], axis=-1)
            return _llinear(h, W2, b2)

        def _lresnet(x, y, w):
            z = x + w * y
            inner = -z[..., :1] ** 2 + jnp.sum(z[..., 1:] ** 2, -1, keepdims=True)
            return jnp.sqrt(C) * z / jnp.sqrt(jnp.clip(-inner, EPS))
        shape = x.shape
        xt = x.reshape(-1, DIM)
        T = xt.shape[0]
        scores = jax.nn.softmax((xt @ gate_w.T).astype(jnp.float32), axis=-1)
        top_w, top_i = jax.lax.top_k(scores, TOPK)
        weights = (top_w * ROUTE_SCALE).astype(x.dtype)
        rows = jnp.arange(T)[:, None]
        w_te = jnp.zeros((T, N_EXP), x.dtype).at[rows, top_i].set(weights)
        hit_te = jnp.zeros((T, N_EXP), bool).at[rows, top_i].set(True)
        y0 = jnp.concatenate([jnp.full((T, 1), jnp.sqrt(C), x.dtype), jnp.zeros((T, DIM - 1), x.dtype)], -1)

        def step(y, packed):
            W1, b1, W3, b3, W2, b2, wt, hit = packed
            out = _lmlp(xt, W1, b1, W3, b3, W2, b2)
            z = _lresnet(y, out, wt[:, None])
            return (jnp.where(hit[:, None], z, y), None)
        y, _ = jax.lax.scan(step, y0, (We1, be1, We3, be3, We2, be2, w_te.T, hit_te.T))
        z = _lmlp(xt, Ws1, bs1, Ws3, bs3, Ws2, bs2)
        out = _lresnet(y, z, 1.0)
        return out.reshape(shape)

    def _L1_attn_ref(x, ln_g, ln_b, w_qkv, b_qkv, w_ent, b_ent, w_out, b_out):
        import jax, jax.numpy as jnp
        import numpy as np
        H = 128
        NH = 16
        HD = H // NH
        B, S = (2, 256)
        b, s, h = x.shape
        scale = 1.0 / jnp.sqrt(jnp.float32(HD))
        TEMP = 0.1
        mu = jnp.mean(x, axis=-1, keepdims=True)
        var = jnp.mean(jnp.square(x - mu), axis=-1, keepdims=True)
        xn = (x - mu) / jnp.sqrt(var + 1e-06) * ln_g + ln_b
        qkv = xn @ w_qkv.T + b_qkv
        qkv = qkv.reshape(b, s, 3, NH, HD).transpose(2, 0, 3, 1, 4)
        q, k, v = (qkv[0], qkv[1], qkv[2])
        scores = jnp.einsum('bhqd,bhkd->bhqk', q, k) * scale
        causal = jnp.tril(jnp.ones((s, s), dtype=bool))
        scores = jnp.where(causal[None, None], scores, -jnp.inf)
        probs = jax.nn.softmax(scores / TEMP, axis=-1)
        gate = jax.nn.sigmoid(xn @ w_ent.T + b_ent)
        gate = jnp.clip(gate, 0.1, 2.0)[:, None, None, :, 0]
        probs = probs * gate
        out = jnp.einsum('bhqk,bhkd->bhqd', probs, v)
        out = out.transpose(0, 2, 1, 3).reshape(b, s, h)
        return (out @ w_out.T + b_out) * 0.1

    def _L1_xattn_ref(x, context, w_q, w_k, w_v, w_o, b_o):
        import jax, jax.numpy as jnp
        import numpy as np
        HEADS = 16
        DIM_HEAD = 64
        QUERY_DIM = 128
        CONTEXT_DIM = 96
        INNER = HEADS * DIM_HEAD
        SCALE = DIM_HEAD ** (-0.5)
        B, Sq, _ = x.shape
        Skv = context.shape[1]
        q = (x @ w_q).reshape(B, Sq, HEADS, DIM_HEAD).transpose(0, 2, 1, 3)
        k = (context @ w_k).reshape(B, Skv, HEADS, DIM_HEAD).transpose(0, 2, 1, 3)
        v = (context @ w_v).reshape(B, Skv, HEADS, DIM_HEAD).transpose(0, 2, 1, 3)
        sim = jnp.einsum('bhid,bhjd->bhij', q, k) * SCALE
        attn = jax.nn.softmax(sim, axis=-1)
        out = jnp.einsum('bhij,bhjd->bhid', attn, v)
        out = out.transpose(0, 2, 1, 3).reshape(B, Sq, INNER)
        return out @ w_o + b_o

    def _L1_ffn_ref(hidden_states, W_router, W1, b1, Wo, bo, ln_gamma, ln_beta):
        import jax, jax.numpy as jnp
        import numpy as np
        H = 128
        I = 512
        E = 4
        LN_EPS = 1e-12

        def _layer_norm(x, gamma, beta, eps=LN_EPS):
            mu = jnp.mean(x, axis=-1, keepdims=True)
            var = jnp.mean(jnp.square(x - mu), axis=-1, keepdims=True)
            return (x - mu) * jax.lax.rsqrt(var + eps) * gamma + beta
        B, S, _ = hidden_states.shape
        x = hidden_states.reshape(-1, H)
        logits = x @ W_router
        expert_idx = jnp.argmax(logits, axis=-1)
        h = jnp.einsum('th,ehi->tei', x, W1) + b1
        h = jax.nn.gelu(h, approximate=False)
        onehot = jax.nn.one_hot(expert_idx, E, dtype=x.dtype)
        intermediate = jnp.einsum('te,tei->ti', onehot, h)
        y = intermediate @ Wo + bo + x
        y = _layer_norm(y, ln_gamma, ln_beta)
        return y.reshape(B, S, H)
    x = x + _L0_attn_ref(_layernorm(x, axis=-1), L0_attn_Wqkv, L0_attn_Wout)
    x = x + _L0_xattn_ref(_layernorm(x, axis=-1), ctx_768, L0_xattn_Wq, L0_xattn_bq, L0_xattn_Wk, L0_xattn_bk, L0_xattn_Wv, L0_xattn_bv, L0_xattn_W1, L0_xattn_b1, L0_xattn_W2, L0_xattn_b2)
    x = x + _L0_ffn_ref(_layernorm(x, axis=-1), L0_ffn_gate_w, L0_ffn_We1, L0_ffn_be1, L0_ffn_We3, L0_ffn_be3, L0_ffn_We2, L0_ffn_be2, L0_ffn_Ws1, L0_ffn_bs1, L0_ffn_Ws3, L0_ffn_bs3, L0_ffn_Ws2, L0_ffn_bs2)
    x = x + _L1_attn_ref(_layernorm(x, axis=-1), L1_attn_ln_g, L1_attn_ln_b, L1_attn_w_qkv, L1_attn_b_qkv, L1_attn_w_ent, L1_attn_b_ent, L1_attn_w_out, L1_attn_b_out)
    x = x + _L1_xattn_ref(_layernorm(x, axis=-1), ctx_768, L1_xattn_w_q, L1_xattn_w_k, L1_xattn_w_v, L1_xattn_w_o, L1_xattn_b_o)
    x = x + _L1_ffn_ref(_layernorm(x, axis=-1), L1_ffn_W_router, L1_ffn_W1, L1_ffn_b1, L1_ffn_Wo, L1_ffn_bo, L1_ffn_ln_gamma, L1_ffn_ln_beta)
    return x

_drawn_inputs = setup_inputs


def setup_inputs(seed=0):
    import zlib

    import numpy as np

    out = dict(_drawn_inputs(seed))
    spreads = {'L0_ffn_be1': (0.0, 2.0),
     'L0_ffn_be3': (0.0, 2.0),
     'L0_ffn_be2': (0.0, 2.0),
     'L0_ffn_bs1': (0.0, 0.8),
     'L0_ffn_bs3': (0.0, 0.8),
     'L0_ffn_bs2': (0.0, 0.8),
     'L1_attn_ln_g': (1.0, 0.6),
     'L1_attn_ln_b': (0.0, 0.8),
     'L1_attn_b_qkv': (0.0, 0.8),
     'L1_attn_b_out': (0.0, 0.8),
     'L1_ffn_ln_gamma': (1.0, 0.2),
     'L1_ffn_ln_beta': (0.0, 0.1)}
    factors = {'L0_attn_Wqkv': 4.003,
     'L0_attn_Wout': 3.988,
     'L0_xattn_bq': 4.118,
     'L0_xattn_bk': 64.0,
     'L0_ffn_gate_w': 8.0,
     'L0_ffn_We1': 8.0,
     'L0_ffn_We3': 8.0,
     'L0_ffn_We2': 8.0,
     'L0_ffn_Ws1': 8.0,
     'L0_ffn_Ws3': 8.0,
     'L0_ffn_Ws2': 6.379,
     'L1_attn_w_qkv': 8.0,
     'L1_attn_w_ent': 8.0,
     'L1_attn_w_out': 8.0,
     'L1_xattn_b_o': 3.106,
     'L1_ffn_W_router': 2.676,
     'L1_ffn_b1': 29.996,
     'L1_ffn_bo': 5.052}
    for name, (base, spread) in spreads.items():
        noise = np.random.default_rng([zlib.crc32(name.encode()), seed]).standard_normal(out[name].shape)
        drawn = base * np.exp(spread * noise) if base else spread * noise
        out[name] = jnp.asarray(drawn.astype(out[name].dtype))
    for name, factor in factors.items():
        out[name] = (out[name] * factor).astype(out[name].dtype)
    return out
```

```python
from contextlib import ExitStack

import numpy as np

import concourse.bass as bass
from concourse import mybir

F32 = mybir.dt.float32
BF16 = mybir.dt.bfloat16
U32 = mybir.dt.uint32
ACT = mybir.ActivationFunctionType
ALU = mybir.AluOpType
AX = mybir.AxisListType

B, T, D = 16, 128, 128
C, CD = 120, 96
H, HD = 16, 8
LHD = 64
NE, EI = 16, 64
NF, FI = 4, 512
SLOTS = 2
STEPS = B // SLOTS
UNITS = H // 4
NEG = -1.0e30

WEIGHTS = [
    [("q", D), ("k", D), ("v", D), ("o", D)],
    [("q", D), ("k", D), ("v", D), ("m1", 2 * D), ("m2", 2 * D)],
    [("gate", NE), ("s1", D), ("s3", D), ("w1", NE * EI), ("w3", NE * EI), ("w2", NE * EI), ("s2", D), ("s2t", D)],
    [("q", D), ("k", D), ("v", D), ("ent", 2), ("o", D), ("g", 1), ("b", 1)],
    [("q", H * LHD), ("k", H * LHD), ("v", H * LHD), ("o", H * LHD)],
    [("r", NF), ("w1", NF * FI), ("o", FI), ("g", D), ("b", D)],
]
ROWS = [("xq", D), ("xm1", 2 * D), ("xm2", D), ("s1", D), ("s3", D), ("s2", D), ("e1", NE * EI), ("e3", NE * EI),
        ("eA", D), ("eB", D), ("tA", D), ("tB", D),
        ("q", D), ("k", D), ("v", D), ("ent", 2), ("ao", D), ("lo", D), ("fo", D), ("f1", FI)]
CONST16 = [("ident", 128), ("causal", T), ("ones", 128), ("alibi_q", T), ("alibi_k", H * T), ("sel", 16 * 128)]
CONST32 = [("ident", 128), ("head", 4), ("iota", NE), ("iota_up", NE), ("origin", D), ("pair", 2), ("ones", 2)]


def columns(table):
    at, out = 0, {}
    for name, n in table:
        out[name] = slice(at, at + n)
        at += n
    return out, at


EVENTS = {
    "x_loaded": 1, "ctx_loaded": 1, "x_taken": 1, "out_ready": 1,
    "var": 8, "rstd": 8, "xn": 8, "xflip": 6, "xT": 6,
    "qkv": 3, "qv": 3, "kx": 3,
    "scores": 16, "shifted": 16, "flipped": 16, "probs": 16, "mixed": 16,
    "onorm": 7, "oflip": 4, "oT": 4, "y": 5, "mlp": 1, "mlp_act": 1, "gate": 1, "gate_exp": 1, "key_gate": 1,
    "logits": 2, "top": 1, "gexp": 1, "masks": 1, "mflip": 1, "maskT": 1,
    "shared_silu": 1, "shared": 1, "h1": 1, "h3": 1, "silu": 1, "hidden": 1, "square": 1,
    "spreadA": 1, "spreadB": 1, "hA": 1, "hB": 1, "norms": 1, "experts": 1,
    "time_in": 1, "time": 1, "time_part": 1, "otime_in": 1, "otime": 1, "inner": 3, "rescale": 3,
    "lq": 1, "lqs": 1, "lk": 1, "lks": 1, "lv": 1, "lvs": 1,
    "flogits": 1, "fmasked": 1, "fflip": 1, "fT": 1, "fh": 1, "fact": 1,
}
DVE_LINKS = 67
POOL_LINKS = 10


def decoder(nc, x, ctx, wts, rows, c16, c32, out):
    wcol = [columns(t) for t in WEIGHTS]
    rcol, nrows = columns(ROWS)
    ccol, n16 = columns(CONST16)
    fcol, n32 = columns(CONST32)

    with ExitStack() as stack:
        def sb(name, shape, dt=F32):
            return stack.enter_context(nc.sbuf_tensor(name, shape, dt))

        def per_slot(name, shape, dt=F32):
            return [sb(f"{name}{s}", shape, dt) for s in range(SLOTS)]

        bank = [[stack.enter_context(nc.psum_tensor(f"bank{s}_{b}", [128, 512], F32)) for b in range(4)]
                for s in range(SLOTS)]
        ev = {n: [stack.enter_context(nc.semaphore(f"{n}_{s}")) for s in range(SLOTS)] for n in EVENTS}
        dve_order = [stack.enter_context(nc.semaphore(f"dve_order{s}")) for s in range(SLOTS)]
        pool_order = [stack.enter_context(nc.semaphore(f"pool_order{s}")) for s in range(SLOTS)]
        out_free = [stack.enter_context(nc.semaphore(f"out_free{s}")) for s in range(SLOTS)]
        w_loaded = [stack.enter_context(nc.semaphore(f"w_loaded{i}")) for i in range(6)]
        const_loaded = stack.enter_context(nc.semaphore("const_loaded"))
        rows_loaded = stack.enter_context(nc.semaphore("rows_loaded"))
        cleared = stack.enter_context(nc.semaphore("cleared"))
        parts_step = stack.enter_context(nc.semaphore("parts_step"))
        parts_ready = stack.enter_context(nc.semaphore("parts_ready"))

        W = [sb(f"weights{i}", [128, wcol[i][1]]) for i in range(6)]
        K16 = sb("const16", [128, n16], BF16)
        K32 = sb("const32", [128, n32])
        raw = sb("raw_rows", [128, nrows])
        part = sb("row_parts", [128, nrows], BF16)
        low = sb("row_low", [128, nrows], BF16)
        powers = sb("powers", [128, 8])

        def w(i, name, rows_=128):
            return W[i][0:rows_, wcol[i][0][name]]

        def k16(name):
            return K16[:, ccol[name]]

        def k32(name, p=128):
            return K32[0:p, fcol[name]]

        def row(name):
            return part[:, rcol[name]]

        x_in = per_slot("x_in", [128, D])
        ctx_in = per_slot("ctx_in", [CD + 1, C])
        res = per_slot("res", [128, D])
        x_out = per_slot("x_out", [128, D])
        stats = per_slot("stats", [128, 6])
        mv = per_slot("mean_var", [128, 2])
        rstd = per_slot("rstd", [128, 2])
        pad = per_slot("pad", [128, 1])
        xn = per_slot("xn", [128, D])
        xT = per_slot("xT", [128, T])
        xl = per_slot("xl", [128, D])
        qq = per_slot("q_quadrants", [128, UNITS * T])
        kx = per_slot("k_heads", [128, 4 * T])
        vv = per_slot("v_ones", [128, H * (HD + 1)])
        top = per_slot("top", [128, 4])
        shifted = per_slot("shifted", [128, 2 * 512])
        probs = per_slot("probs", [128, 2 * 512])
        rsum = per_slot("rsum", [128, H])
        o = per_slot("o", [128, D])
        oT = per_slot("oT", [128, D])
        mh = per_slot("mlp_hidden", [128, 2 * D])
        gate = per_slot("gate", [128, 2])
        lg = per_slot("lg", [128, NE])
        pr = per_slot("pr", [128, NE])
        sm = per_slot("small", [128, 32])
        best = per_slot("best", [128, 8])
        at_best = per_slot("at_best", [128, 8], U32)
        mk = per_slot("masks", [128, 128], BF16)
        mT = per_slot("masksT", [128, T], BF16)
        big = per_slot("big", [128, 4 * 1024])
        wide = per_slot("wide", [128, 2048])
        sh = per_slot("shared", [128, 3 * 128])
        lv = per_slot("lv", [128, H * (LHD + 1)])
        oe = per_slot("experts_out", [128, 3 * D])
        tw = per_slot("time_part", [128, 2 * D])
        z = per_slot("z", [128, D])
        yy = per_slot("y_state", [128, D])
        junk = per_slot("junk", [128, D])

        def nth(it, name, k=0, by=1):
            return it * (EVENTS[name] * by) + (k + 1) * by

        b = bank
        block = stack.enter_context(nc.Block())

        @block.sync
        def _(sp):
            for s in range(SLOTS):
                sp.dma_start(x_in[s][:, :], x[s]).then_inc(ev["x_loaded"][s], 16)
            sp.dma_start(K32[:, :], c32).then_inc(const_loaded, 16)
            sp.dma_start(W[0][:, :], wts[0]).then_inc(w_loaded[0], 16)
            sp.dma_start(K16[:, :], c16).then_inc(const_loaded, 16)
            for s in range(SLOTS):
                sp.dma_start(ctx_in[s][:, :], ctx[s]).then_inc(ev["ctx_loaded"][s], 16)
            for p in range(3):
                sp.dma_start(raw[32 * p:32 * p + 32, :], rows).then_inc(rows_loaded, 16)
            for i in range(1, 6):
                sp.dma_start(W[i][:, :], wts[i]).then_inc(w_loaded[i], 16)

            def store(it):
                for s in range(SLOTS):
                    sp.wait_ge(ev["out_ready"][s], nth(it, "out_ready"))
                    sp.dma_start(out[bass.ds(SLOTS * it + s, 1)].rearrange("b t d -> (b t) d"), x_out[s][:, :])\
                        .then_inc(out_free[s], 16)

            with sp.Fori(0, STEPS - 1) as it:
                for s in range(SLOTS):
                    sp.wait_ge(ev["x_taken"][s], nth(it, "x_taken"))
                    sp.dma_start(x_in[s][:, :], x[bass.ds(SLOTS * it + SLOTS + s, 1)].rearrange("b t d -> (b t) d"))\
                        .then_inc(ev["x_loaded"][s], 16)
                for s in range(SLOTS):
                    sp.wait_ge(ev["lv"][s], nth(it, "lv"))
                    sp.dma_start(ctx_in[s][:, :], ctx[bass.ds(SLOTS * it + SLOTS + s, 1)].rearrange("b t d -> (b t) d"))\
                        .then_inc(ev["ctx_loaded"][s], 16)
                store(it)
            for s in range(SLOTS):
                sp.wait_ge(ev["out_ready"][s], STEPS)
                sp.dma_start(out[SLOTS * (STEPS - 1) + s], x_out[s][:, :]).then_inc(out_free[s], 16)
            for s in range(SLOTS):
                sp.wait_ge(out_free[s], 16 * (STEPS + 1))

        @block.gpsimd
        def _(pool):
            for j, value in enumerate([-0.5, 0.5, 1e-5, 1e-6, 1e-12, 1.0, 1.0, 1.0]):
                pool.memset(powers[:, j:j + 1], value).then_inc(cleared, 1)
            for s in range(SLOTS):
                pool.memset(qq[s][:, :], 0.0).then_inc(cleared, 1)
                pool.memset(vv[s][:, :], 1.0).then_inc(cleared, 1)
                pool.memset(mk[s][:, :], 0.0).then_inc(cleared, 1)
                pool.memset(lv[s][:, :], 1.0).then_inc(cleared, 1)
                pool.memset(x_out[s][:, :], 0.0).then_inc(out_free[s], 16)
            half = powers[:, 1:2]
            minus_half = powers[:, 0:1]
            epsilon = {1e-5: powers[:, 2:3], 1e-6: powers[:, 3:4], 1e-12: powers[:, 4:5]}
            pool.wait_ge(cleared, CLEARED)
            with pool.Fori(0, STEPS) as it:
                n = [0] * SLOTS

                def link(ins, s):
                    n[s] += 1
                    ins.then_inc(pool_order[s], 1)
                    pool.wait_ge(pool_order[s], it * POOL_LINKS + n[s])

                def ln(k, eps):
                    for s in range(SLOTS):
                        pool.wait_ge(ev["var"][s], nth(it, "var", k))
                        link(pool.tensor_tensor(rstd[s][:, 1:2], mv[s][:, 1:2], epsilon[eps], ALU.add), s)
                        pool.tensor_tensor(rstd[s][:, 0:1], rstd[s][:, 1:2], minus_half, ALU.pow)\
                            .then_inc(ev["rstd"][s], 1)

                def time(source, done, src, dst):
                    for s in range(SLOTS):
                        pool.wait_ge(ev[source][s], nth(it, source))
                        link(pool.tensor_tensor(sm[s][:, 12:15], sm[s][:, src], powers[:, 5:8], ALU.add), s)
                        pool.tensor_tensor(sm[s][:, dst], sm[s][:, 12:15], half.to_broadcast([128, 3]), ALU.pow)\
                            .then_inc(ev[done][s], 1)

                ln(0, 1e-5)
                ln(1, 1e-5)
                ln(2, 1e-5)
                time("time_in", "time", slice(0, 3), slice(3, 6))
                time("otime_in", "otime", slice(6, 9), slice(9, 12))
                for k in range(3):
                    for s in range(SLOTS):
                        pool.wait_ge(ev["inner"][s], nth(it, "inner", k))
                        pool.tensor_tensor(sm[s][:, 18:19], sm[s][:, 17:18], minus_half, ALU.pow)\
                            .then_inc(ev["rescale"][s], 1)
                ln(3, 1e-5)
                ln(4, 1e-6)
                ln(5, 1e-5)
                ln(6, 1e-5)
                ln(7, 1e-12)
                assert n == [POOL_LINKS] * SLOTS, n

        @block.scalar
        def _(act):
            act.wait_ge(cleared, CLEARED)
            act.wait_ge(w_loaded[3], 16)
            with act.Fori(0, STEPS) as it:
                def flip_out(k):
                    for s in range(SLOTS):
                        act.wait_ge(ev["xflip"][s], nth(it, "xflip", k))
                        if k == 3:
                            act.activation(xT[s][:, :], b[s][3][:, 0:T], ACT.Identity, bias=w(3, "b"), scale=w(3, "g"))\
                                .then_inc(ev["xT"][s], 1)
                        else:
                            act.activation(xT[s][:, :], b[s][3][:, 0:T], ACT.Copy).then_inc(ev["xT"][s], 1)

                def qv_out(a, keys):
                    for s in range(SLOTS):
                        act.wait_ge(ev["qkv"][s], nth(it, "qkv", a))
                        if a == 2:
                            act.activation(gate[s][:, 0:1], b[s][3][:, 384:385], ACT.Exp, scale=-1.0)\
                                .then_inc(ev["gate_exp"][s], 1)
                        for i in range(UNITS):
                            act.activation(qq[s][32 * i:32 * i + 32, T * i:T * i + T],
                                           b[s][3][32 * i:32 * i + 32, 128:256], ACT.Copy)
                        if a == 2:
                            act.wait_ge(ev["key_gate"][s], nth(it, "key_gate"))
                        act.activation(vv[s][0:keys, :].rearrange("p (h d) -> p h d", d=HD + 1)[:, :, 0:HD],
                                       b[s][3][0:keys, 256:384].rearrange("p (h d) -> p h d", d=HD), ACT.Copy,
                                       scale=gate[s][:, 1:2] if a == 2 else 1.0).then_inc(ev["qv"][s], 1)

                def exps(a, keys, scale):
                    for i in range(UNITS):
                        for s in range(SLOTS):
                            act.wait_ge(ev["flipped"][s], nth(it, "flipped", 4 * a + i))
                            if i >= 2:
                                act.wait_ge(ev["mixed"][s], nth(it, "mixed", 4 * a + i - 2))
                            act.activation(probs[s][0:keys, 512 * (i % 2):512 * (i % 2) + 512], b[s][2][0:keys, :],
                                           ACT.Exp, scale=scale).then_inc(ev["probs"][s], 1)

                def o_out(a):
                    for s in range(SLOTS):
                        act.wait_ge(ev["oflip"][s], nth(it, "oflip", a))
                        act.activation(oT[s][:, :], b[s][3][:, 256:384], ACT.Copy).then_inc(ev["oT"][s], 1)

                flip_out(0)
                qv_out(0, T)
                exps(0, T, HD ** -0.5)
                o_out(0)
                flip_out(1)
                qv_out(1, C)
                exps(1, C, HD ** -0.5)
                o_out(1)
                for s in range(SLOTS):
                    act.wait_ge(ev["mlp"][s], nth(it, "mlp"))
                    act.activation(mh[s][:, :], b[s][3][:, 0:2 * D], ACT.Relu).then_inc(ev["mlp_act"][s], 1)
                flip_out(2)
                for s in range(SLOTS):
                    act.wait_ge(ev["gate"][s], nth(it, "gate"))
                    act.activation(lg[s][:, :], b[s][3][:, 128:128 + NE], ACT.Copy).then_inc(ev["logits"][s], 1)
                for s in range(SLOTS):
                    act.wait_ge(ev["top"][s], nth(it, "top"))
                    act.activation(pr[s][:, :], lg[s][:, :], ACT.Exp, bias=sm[s][:, 19:20],
                                   accum_out=sm[s][:, 20:21]).then_inc(ev["gexp"][s], 1)
                for s in range(SLOTS):
                    act.activation(sh[s][:, 0:128], b[s][3][:, 256:384], ACT.Silu).then_inc(ev["shared_silu"][s], 1)
                for s in range(SLOTS):
                    act.wait_ge(ev["h1"][s], nth(it, "h1"))
                    act.activation(big[s][:, 0:512], b[s][0][:, :], ACT.Silu)
                    act.activation(big[s][:, 512:1024], b[s][1][:, :], ACT.Silu).then_inc(ev["silu"][s], 1)
                for s in range(SLOTS):
                    act.wait_ge(ev["mflip"][s], nth(it, "mflip"))
                    act.activation(mT[s][:, :], b[s][3][:, 128:192].bitcast(BF16), ACT.Copy)\
                        .then_inc(ev["maskT"][s], 1)
                for s in range(SLOTS):
                    act.wait_ge(ev["hidden"][s], nth(it, "hidden"))
                    act.activation(sh[s][:, 256:384], sh[s][:, 128:256], ACT.Square)
                    act.activation(wide[s][:, 0:1024], big[s][:, 1024:2048], ACT.Square).then_inc(ev["square"][s], 1)
                for s in range(SLOTS):
                    act.wait_ge(ev["experts"][s], nth(it, "experts"))
                    act.wait_ge(ev["time"][s], nth(it, "time"))
                    act.activation(tw[s][:, 0:D], b[s][1][:, 256:384], ACT.Copy, scale=sm[s][:, 3:4])
                    act.activation(tw[s][:, D:2 * D], b[s][1][:, 384:512], ACT.Copy, scale=sm[s][:, 4:5])\
                        .then_inc(ev["time_part"][s], 1)
                flip_out(3)
                qv_out(2, T)
                exps(2, T, HD ** -0.5 / 0.1)
                o_out(2)
                flip_out(4)
                for s in range(SLOTS):
                    act.wait_ge(ev["lq"][s], nth(it, "lq"))
                    act.activation(big[s][:, 0:512], b[s][0][:, :], ACT.Copy)
                    act.activation(big[s][:, 512:1024], b[s][1][:, :], ACT.Copy).then_inc(ev["lqs"][s], 1)
                for s in range(SLOTS):
                    act.wait_ge(ev["lv"][s], nth(it, "lv"))
                    for j in range(2):
                        ins = act.activation(
                            lv[s][0:C, :].rearrange("p (h d) -> p h d", d=LHD + 1)[:, 8 * j:8 * j + 8, 0:LHD],
                            b[s][j][0:C, :].rearrange("p (h d) -> p h d", d=LHD), ACT.Copy)
                    ins.then_inc(ev["lvs"][s], 1)
                exps(3, C, LHD ** -0.5)
                for s in range(SLOTS):
                    act.wait_ge(ev["oflip"][s], nth(it, "oflip", 3))
                    act.activation(big[s][:, 2048:2560], b[s][0][:, :], ACT.Copy)
                    act.activation(big[s][:, 2560:3072], b[s][1][:, :], ACT.Copy).then_inc(ev["oT"][s], 1)
                flip_out(5)
                for s in range(SLOTS):
                    act.wait_ge(ev["flogits"][s], nth(it, "flogits"))
                    act.activation(lg[s][:, 0:NF], b[s][3][:, 128:128 + NF], ACT.Copy).then_inc(ev["logits"][s], 1)
                for s in range(SLOTS):
                    act.wait_ge(ev["fflip"][s], nth(it, "fflip"))
                    act.activation(big[s][:, 0:512], b[s][2][:, :], ACT.Copy)
                    act.activation(mT[s][:, :], b[s][3][:, 128:192].bitcast(BF16), ACT.Copy).then_inc(ev["fT"][s], 1)
                for s in range(SLOTS):
                    act.wait_ge(ev["fh"][s], nth(it, "fh"))
                    act.activation(big[s][:, 512:1024], b[s][0][:, :], ACT.Gelu).then_inc(ev["fact"][s], 1)

        @block.vector
        def _(dve):
            for j in range(2):
                dve.memset(raw[96:128, :] if j == 0 else pad[0][:, :], 0.0).then_inc(parts_step, 1)
            dve.wait_ge(rows_loaded, 48)
            dve.wait_ge(parts_step, 2)
            step = 2
            for p in range(3):
                dve.tensor_copy(part[:, :] if p == 0 else low[:, :], raw[:, :]).then_inc(parts_step, 1)
                step += 1
                dve.wait_ge(parts_step, step)
                if p > 0:
                    dve.tensor_copy(part[32 * p:32 * p + 32, :], low[32 * p:32 * p + 32, :]).then_inc(parts_step, 1)
                    step += 1
                    dve.wait_ge(parts_step, step)
                if p < 2:
                    dve.tensor_tensor(raw[:, :], raw[:, :], part[:, :] if p == 0 else low[:, :], ALU.subtract)\
                        .then_inc(parts_step, 1)
                    step += 1
                    dve.wait_ge(parts_step, step)
            dve.tensor_copy(pad[0][:, :], raw[:, 0:1]).then_inc(parts_ready, 1)
            dve.wait_ge(cleared, CLEARED)
            dve.wait_ge(const_loaded, 32)
            dve.wait_ge(w_loaded[2], 16)
            dve.wait_ge(w_loaded[5], 16)

            with dve.Fori(0, STEPS) as it:
                n = [0] * SLOTS

                def link(ins, s):
                    n[s] += 1
                    ins.then_inc(dve_order[s], 1)
                    dve.wait_ge(dve_order[s], it * DVE_LINKS + n[s])

                def hold(s):
                    dve.memset(pad[s][:, :], 0.0)

                def ln(k, src, dst):
                    for s in range(SLOTS):
                        if k == 0:
                            dve.wait_ge(ev["x_loaded"][s], nth(it, "x_loaded", 0, 16))
                        link(dve.bn_stats(stats[s][:, :], src[s][:, :]), s)
                        hold(s)
                        dve.bn_aggr(mv[s][:, :], stats[s][:, :]).then_inc(ev["var"][s], 1)
                    for s in range(SLOTS):
                        dve.wait_ge(ev["rstd"][s], nth(it, "rstd", k))
                        dve.tensor_scalar(dst[s][:, :], src[s][:, :], mv[s][:, 0:1], rstd[s][:, 0:1],
                                          ALU.subtract, ALU.mult).then_inc(ev["xn"][s], 1)

                def k_heads(a, keys):
                    for s in range(SLOTS):
                        dve.wait_ge(ev["qkv"][s], nth(it, "qkv", a))
                        dve.tensor_tensor(kx[s][:, 0:4 * keys].rearrange("p (j t) -> p j t", j=4),
                                          b[s][2][:, 0:keys].unsqueeze(1).to_broadcast([128, 4, keys]),
                                          k32("head").unsqueeze(2).to_broadcast([128, 4, keys]), ALU.mult)\
                            .then_inc(ev["kx"][s], 1)

                def shifts(a, keys):
                    for i in range(UNITS):
                        for s in range(SLOTS):
                            dve.wait_ge(ev["scores"][s], nth(it, "scores", 4 * a + i))
                            sc = b[s][i % 2][:, 0:4 * keys].rearrange("p (j t) -> p j t", j=4)
                            link(dve.tensor_reduce(top[s][:, :], sc, AX.X, ALU.max), s)
                            if i >= 2:
                                dve.wait_ge(ev["flipped"][s], nth(it, "flipped", 4 * a + i - 2))
                            dve.tensor_tensor(
                                shifted[s][:, 512 * (i % 2):512 * (i % 2) + 4 * keys].rearrange("p (j t) -> p j t", j=4),
                                sc, top[s][:, :].unsqueeze(2).to_broadcast([128, 4, keys]), ALU.subtract)\
                                .then_inc(ev["shifted"][s], 1)

                def o_norm(a):
                    for s in range(SLOTS):
                        dve.wait_ge(ev["mixed"][s], nth(it, "mixed", 4 * a + 3))
                        m = b[s][3][:, 0:H * (HD + 1)].rearrange("p (h d) -> p h d", d=HD + 1)
                        link(dve.reciprocal(rsum[s][:, :], m[:, :, HD]), s)
                        dve.tensor_tensor(o[s][:, :].rearrange("p (h d) -> p h d", d=HD), m[:, :, 0:HD],
                                          rsum[s][:, :].unsqueeze(2).to_broadcast([128, H, HD]), ALU.mult)\
                            .then_inc(ev["onorm"][s], 1)

                ln(0, x_in, xn)
                k_heads(0, T)
                shifts(0, T)
                o_norm(0)
                for s in range(SLOTS):
                    dve.wait_ge(ev["y"][s], nth(it, "y", 0))
                    link(dve.tensor_tensor(res[s][:, :], b[s][3][:, 384:512], x_in[s][:, :], ALU.add), s)
                    dve.memset(pad[s][:, :], 0.0).then_inc(ev["x_taken"][s], 1)
                ln(1, res, xn)
                k_heads(1, C)
                shifts(1, C)
                o_norm(1)
                for s in range(SLOTS):
                    dve.wait_ge(ev["y"][s], nth(it, "y", 1))
                    link(dve.tensor_tensor(res[s][:, :], b[s][3][:, 384:512], res[s][:, :], ALU.add), s)
                ln(2, res, xn)
                for s in range(SLOTS):
                    dve.wait_ge(ev["logits"][s], nth(it, "logits", 0))
                    link(dve.tensor_reduce(sm[s][:, 16:17], lg[s][:, :], AX.X, ALU.max), s)
                    dve.tensor_scalar(sm[s][:, 19:20], sm[s][:, 16:17], -1.0, None, ALU.mult).then_inc(ev["top"][s], 1)
                for s in range(SLOTS):
                    dve.wait_ge(ev["shared_silu"][s], nth(it, "shared_silu"))
                    dve.tensor_tensor(sh[s][:, 128:256], b[s][3][:, 384:512], sh[s][:, 0:128], ALU.mult)\
                        .then_inc(ev["shared"][s], 1)
                for s in range(SLOTS):
                    dve.wait_ge(ev["gexp"][s], nth(it, "gexp"))
                    link(dve.reciprocal(sm[s][:, 21:22], sm[s][:, 20:21]), s)
                    link(dve.tensor_scalar(pr[s][:, :], pr[s][:, :], sm[s][:, 21:22], None, ALU.mult), s)
                    hold(s)
                    link(dve.max(best[s][:, :], pr[s][:, :]), s)
                    hold(s)
                    link(dve.max_index(at_best[s][:, :], best[s][:, :], pr[s][:, :]), s)
                    link(dve.tensor_copy(sm[s][:, 22:24], at_best[s][:, 0:2]), s)
                    dve.tensor_tensor(sm[s][:, 24:25], sm[s][:, 22:23], sm[s][:, 23:24], ALU.min)
                    link(dve.tensor_tensor(sm[s][:, 25:26], sm[s][:, 22:23], sm[s][:, 23:24], ALU.max), s)
                    m = mk[s][:, :].rearrange("p (a c) -> p a c", a=4)
                    for j in range(2):
                        ins = dve.tensor_scalar(m[:, 0:3, NE * j:NE * j + NE],
                                                k32("iota").unsqueeze(1).to_broadcast([128, 3, NE]),
                                                sm[s][:, 24 + j:25 + j], None, ALU.is_equal)
                    ins.then_inc(ev["masks"][s], 1)
                    dve.wait_ge(ev["masks"][s], nth(it, "masks"))
                    for j in range(2):
                        ins = dve.tensor_tensor_reduce(out=junk[s][:, NE * j:NE * j + NE], in0=mk[s][:, NE * j:NE * j + NE],
                                                       in1=pr[s][:, :], scale=1.0, scalar=0.0, op0=ALU.mult, op1=ALU.add,
                                                       accum_out=sm[s][:, 26 + j:27 + j])
                    link(ins, s)
                for s in range(SLOTS):
                    dve.wait_ge(ev["silu"][s], nth(it, "silu"))
                    dve.wait_ge(ev["h3"][s], nth(it, "h3"))
                    dve.tensor_tensor(big[s][:, 1024:1536], b[s][2][:, :], big[s][:, 0:512], ALU.mult)
                    dve.tensor_tensor(big[s][:, 1536:2048], b[s][3][:, :], big[s][:, 512:1024], ALU.mult)\
                        .then_inc(ev["hidden"][s], 1)
                for j, (spread, done) in enumerate([("spreadA", "hA"), ("spreadB", "hB")]):
                    for s in range(SLOTS):
                        dve.wait_ge(ev["hidden"][s], nth(it, "hidden"))
                        dve.wait_ge(ev[spread][s], nth(it, spread))
                        for c in range(2):
                            ins = dve.tensor_tensor(big[s][:, 2048 + 1024 * j + 512 * c:2560 + 1024 * j + 512 * c],
                                                    b[s][2 * j + c][:, :], big[s][:, 1024 + 512 * c:1536 + 512 * c],
                                                    ALU.mult)
                        ins.then_inc(ev[done][s], 1)
                for s in range(SLOTS):
                    dve.wait_ge(ev["norms"][s], nth(it, "norms"))
                    for j in range(2):
                        dve.tensor_tensor_reduce(out=junk[s][:, NE * j + 32:NE * j + 32 + NE], in0=b[s][0][:, 0:NE],
                                                 in1=mk[s][:, NE * j:NE * j + NE], scale=1.0, scalar=0.0,
                                                 op0=ALU.mult, op1=ALU.add, accum_out=sm[s][:, j:j + 1])
                    dve.tensor_copy(sm[s][:, 2:3], b[s][0][:, NE:NE + 1]).then_inc(ev["time_in"][s], 1)
                for s in range(SLOTS):
                    dve.wait_ge(ev["time_part"][s], nth(it, "time_part"))
                    dve.tensor_tensor(oe[s][:, 0:2 * D], b[s][1][:, 0:2 * D], tw[s][:, :], ALU.add)
                    link(dve.scalar_tensor_tensor(oe[s][:, 2 * D:3 * D], w(2, "s2t"), sm[s][:, 5:6], b[s][0][:, 128:256],
                                                  ALU.mult, ALU.add), s)
                    for j in range(3):
                        ins = dve.tensor_tensor_reduce(out=(junk[s][:, :], z[s][:, :], yy[s][:, :])[j],
                                                       in0=oe[s][:, D * j:D * j + D], in1=oe[s][:, D * j:D * j + D],
                                                       scale=1.0, scalar=0.0, op0=ALU.mult, op1=ALU.add,
                                                       accum_out=sm[s][:, 6 + j:7 + j])
                    ins.then_inc(ev["otime_in"][s], 1)
                for s in range(SLOTS):
                    dve.wait_ge(ev["otime"][s], nth(it, "otime"))
                    link(dve.tensor_copy(oe[s][:, :].rearrange("p (j d) -> p j d", j=3)[:, :, 0], sm[s][:, 9:12]), s)
                for k in range(3):
                    for s in range(SLOTS):
                        y_now = k32("origin") if k == 0 else yy[s][:, :]
                        weight = sm[s][:, 26 + k:27 + k] if k < 2 else 1.0
                        link(dve.scalar_tensor_tensor(z[s][:, :], oe[s][:, D * k:D * k + D], weight, y_now,
                                                      ALU.mult, ALU.add), s)
                        link(dve.tensor_tensor_reduce(out=junk[s][:, 1:D], in0=z[s][:, 1:D], in1=z[s][:, 1:D], scale=1.0,
                                                      scalar=0.0, op0=ALU.mult, op1=ALU.add,
                                                      accum_out=sm[s][:, 15:16]), s)
                        link(dve.scalar_tensor_tensor(sm[s][:, 16:17], z[s][:, 0:1], z[s][:, 0:1], sm[s][:, 15:16],
                                                      ALU.mult, ALU.subtract), s)
                        dve.tensor_scalar(sm[s][:, 17:18], sm[s][:, 16:17], 1e-6, None, ALU.max)\
                            .then_inc(ev["inner"][s], 1)
                    for s in range(SLOTS):
                        dve.wait_ge(ev["rescale"][s], nth(it, "rescale", k))
                        if k < 2:
                            link(dve.tensor_scalar(yy[s][:, :], z[s][:, :], sm[s][:, 18:19], None, ALU.mult), s)
                        else:
                            link(dve.scalar_tensor_tensor(res[s][:, :], z[s][:, :], sm[s][:, 18:19], res[s][:, :],
                                                          ALU.mult, ALU.add), s)
                ln(3, res, xl)
                for s in range(SLOTS):
                    dve.wait_ge(ev["xn"][s], nth(it, "xn", 3))
                ln(4, xl, xn)
                k_heads(2, T)
                for s in range(SLOTS):
                    dve.wait_ge(ev["gate_exp"][s], nth(it, "gate_exp"))
                    link(dve.tensor_scalar(gate[s][:, 1:2], gate[s][:, 0:1], 1.0, None, ALU.add), s)
                    link(dve.reciprocal(gate[s][:, 0:1], gate[s][:, 1:2]), s)
                    dve.tensor_scalar(gate[s][:, 1:2], gate[s][:, 0:1], 0.1, 2.0, ALU.max, ALU.min)\
                        .then_inc(ev["key_gate"][s], 1)
                shifts(2, T)
                o_norm(2)
                for s in range(SLOTS):
                    dve.wait_ge(ev["y"][s], nth(it, "y", 2))
                    link(dve.scalar_tensor_tensor(res[s][:, :], b[s][3][:, 384:512], 0.1, res[s][:, :],
                                                  ALU.mult, ALU.add), s)
                ln(5, res, xn)
                for s in range(SLOTS):
                    dve.wait_ge(ev["lk"][s], nth(it, "lk"))
                    k4 = wide[s][:, 0:1920].rearrange("p (c e t) -> p c e t", c=8, e=2)
                    for c in range(2):
                        src = b[s][2 + c][:, 0:480].rearrange("p (c t) -> p c t", c=4)
                        for e in range(2):
                            ins = dve.tensor_scalar(
                                k4[:, 4 * c:4 * c + 4, e, :], src,
                                k32("pair")[:, e:e + 1], None, ALU.mult)
                    ins.then_inc(ev["lks"][s], 1)
                for i in range(UNITS + 1):
                    if i < UNITS:
                        for s in range(SLOTS):
                            dve.wait_ge(ev["scores"][s], nth(it, "scores", 12 + i))
                            sc = b[s][i % 2][:, 0:4 * C].rearrange("p (j t) -> p j t", j=4)
                            link(dve.tensor_reduce(top[s][:, :], sc, AX.X, ALU.max), s)
                            if i >= 2:
                                dve.wait_ge(ev["flipped"][s], nth(it, "flipped", 12 + i - 2))
                            dve.tensor_tensor(
                                shifted[s][:, 512 * (i % 2):512 * (i % 2) + 4 * C].rearrange("p (j t) -> p j t", j=4),
                                sc, top[s][:, :].unsqueeze(2).to_broadcast([128, 4, C]), ALU.subtract)\
                                .then_inc(ev["shifted"][s], 1)
                    if i >= 1:
                        for s in range(SLOTS):
                            dve.wait_ge(ev["mixed"][s], nth(it, "mixed", 12 + i - 1))
                            m = b[s][3][:, 0:4 * (LHD + 1)].rearrange("p (h d) -> p h d", d=LHD + 1)
                            link(dve.reciprocal(rsum[s][:, 0:4], m[:, :, LHD]), s)
                            dve.tensor_tensor(
                                big[s][:, 1024 + 256 * (i - 1):1024 + 256 * i].rearrange("p (h d) -> p h d", d=LHD),
                                m[:, :, 0:LHD], rsum[s][:, 0:4].unsqueeze(2).to_broadcast([128, 4, LHD]), ALU.mult)\
                                .then_inc(ev["onorm"][s], 1)
                for s in range(SLOTS):
                    dve.wait_ge(ev["y"][s], nth(it, "y", 3))
                    link(dve.tensor_tensor(res[s][:, :], b[s][3][:, 384:512], res[s][:, :], ALU.add), s)
                ln(6, res, xn)
                for s in range(SLOTS):
                    dve.wait_ge(ev["logits"][s], nth(it, "logits", 1))
                    link(dve.tensor_reduce(sm[s][:, 16:17], lg[s][:, 0:NF], AX.X, ALU.max), s)
                    link(dve.tensor_scalar(sm[s][:, 19:23], lg[s][:, 0:NF], sm[s][:, 16:17], None, ALU.is_equal), s)
                    link(dve.scalar_tensor_tensor(sm[s][:, 24:28], sm[s][:, 19:23], -float(NE), k32("iota_up")[:, 0:NF],
                                                  ALU.mult, ALU.add), s)
                    link(dve.tensor_reduce(sm[s][:, 16:17], sm[s][:, 24:28], AX.X, ALU.min), s)
                    link(dve.tensor_scalar(sm[s][:, 19:23], k32("iota")[:, 0:NF], sm[s][:, 16:17], None, ALU.is_equal), s)
                    m = mk[s][:, :].rearrange("p (a c) -> p a c", a=4)
                    dve.tensor_copy(m[:, 0:3, 0:NF], sm[s][:, 19:23].unsqueeze(1).to_broadcast([128, 3, NF]))
                    dve.tensor_tensor(big[s][:, 3072:3584].rearrange("p (e d) -> p e d", e=NF),
                                      xn[s][:, :].unsqueeze(1).to_broadcast([128, NF, D]),
                                      sm[s][:, 19:23].unsqueeze(2).to_broadcast([128, NF, D]), ALU.mult)\
                        .then_inc(ev["fmasked"][s], 1)
                for s in range(SLOTS):
                    dve.wait_ge(ev["y"][s], nth(it, "y", 4))
                    link(dve.tensor_tensor(z[s][:, :], b[s][3][:, 384:512], xn[s][:, :], ALU.add), s)
                ln(7, z, yy)
                for s in range(SLOTS):
                    dve.wait_ge(ev["xn"][s], nth(it, "xn", 7))
                    link(dve.tensor_tensor(z[s][:, :], yy[s][:, :], w(5, "g"), ALU.mult), s)
                    link(dve.tensor_tensor(yy[s][:, :], z[s][:, :], w(5, "b"), ALU.add), s)
                    dve.wait_ge(out_free[s], it * 16 + 16)
                    dve.tensor_tensor(x_out[s][:, :], yy[s][:, :], res[s][:, :], ALU.add).then_inc(ev["out_ready"][s], 1)
                assert n == [DVE_LINKS] * SLOTS, n

        @block.tensor
        def _(pe):
            ident = k32("ident")
            for i in range(6):
                pe.wait_ge(w_loaded[i], 16)
            pe.wait_ge(const_loaded, 32)
            pe.wait_ge(parts_ready, 1)
            pe.wait_ge(cleared, CLEARED)

            with pe.Fori(0, STEPS) as it:
                def flip(k):
                    for s in range(SLOTS):
                        pe.wait_ge(ev["xn"][s], nth(it, "xn", (0, 1, 2, 4, 5, 6)[k]))
                        pe.transpose(b[s][3][:, 0:T], xn[s][:, :], ident).then_inc(ev["xflip"][s], 1)

                def project(a, i, keys):
                    for s in range(SLOTS):
                        pe.wait_ge(ev["xT"][s], nth(it, "xT", (0, 1, 3)[a]))
                        kvT, depth = xT[s][:, :], 128
                        if a == 1:
                            pe.wait_ge(ev["ctx_loaded"][s], nth(it, "ctx_loaded", 0, 16))
                            kvT, depth = ctx_in[s][:, :], CD + 1
                        pe.matmul(b[s][2][:, 0:keys], w(i, "k", depth), kvT, start=True, stop=(a != 2))
                        if a == 2:
                            pe.matmul(b[s][2][:, 0:keys], row("k"), k16("ones"), start=False, stop=True)
                        pe.matmul(b[s][3][:, 128:256], w(i, "q"), xT[s][:, :], start=True, stop=(a == 0))
                        if a > 0:
                            pe.matmul(b[s][3][:, 128:256], row(("", "xq", "q")[a]), k16("ones"), start=False, stop=True)
                        wv = w(i, "v", depth)
                        if a == 2:
                            wv = W[i][:, wcol[i][0]["v"].start:wcol[i][0]["ent"].stop]
                        last = pe.matmul(b[s][3][0:keys, 256:256 + wv.shape[1]], kvT, wv, start=True, stop=(a != 2))
                        if a == 2:
                            last = pe.matmul(b[s][3][:, 256:386], k16("ones"),
                                             part[:, rcol["v"].start:rcol["ent"].stop], start=False, stop=True)
                        last.then_inc(ev["qkv"][s], 1)

                def attend(a, keys, v, depth):
                    for i in range(UNITS + 2):
                        if i < UNITS:
                            for s in range(SLOTS):
                                if i == 0:
                                    if a < 3:
                                        pe.wait_ge(ev["kx"][s], nth(it, "kx", a))
                                        pe.wait_ge(ev["qv"][s], nth(it, "qv", a))
                                    else:
                                        pe.wait_ge(ev["lvs"][s], nth(it, "lvs"))
                                        pe.wait_ge(ev["lks"][s], nth(it, "lks"))
                                if i >= 2:
                                    pe.wait_ge(ev["shifted"][s], nth(it, "shifted", 4 * a + i - 2))
                                sc = b[s][i % 2]
                                if a == 3:
                                    for c in range(2):
                                        last = pe.matmul(sc[:, 240 * c:240 * c + 240],
                                                         big[s][:, 128 * (2 * i + c):128 * (2 * i + c) + 128],
                                                         wide[s][:, 240 * (2 * i + c):240 * (2 * i + c) + 240],
                                                         start=True, stop=True)
                                else:
                                    last = pe.matmul(sc[:, 0:4 * keys], qq[s][:, T * i:T * i + T], kx[s][:, 0:4 * keys],
                                                     start=True, stop=(a == 1))
                                    if a != 1:
                                        last = pe.matmul(sc[:, :], k16("ident"),
                                                         k16("causal").unsqueeze(1).to_broadcast([128, 4, T]),
                                                         start=False, stop=(a == 2))
                                    if a == 0:
                                        last = pe.matmul(sc[:, :], k16("alibi_q"),
                                                         k16("alibi_k")[:, 4 * T * i:4 * T * i + 4 * T],
                                                         start=False, stop=True)
                                last.then_inc(ev["scores"][s], 1)
                        if 1 <= i <= UNITS:
                            for s in range(SLOTS):
                                pe.wait_ge(ev["shifted"][s], nth(it, "shifted", 4 * a + i - 1))
                                if i >= 2:
                                    pe.wait_ge(ev["probs"][s], nth(it, "probs", 4 * a + i - 2))
                                at = 512 * ((i - 1) % 2)
                                for j in range(4):
                                    last = pe.transpose(b[s][2][0:keys, T * j:T * j + T],
                                                        shifted[s][:, at + keys * j:at + keys * j + keys], ident)
                                last.then_inc(ev["flipped"][s], 1)
                        if i >= 2:
                            for s in range(SLOTS):
                                pe.wait_ge(ev["probs"][s], nth(it, "probs", 4 * a + i - 2))
                                if a == 3 and i >= 3:
                                    pe.wait_ge(ev["onorm"][s], nth(it, "onorm", 3 + i - 3))
                                at = 512 * ((i - 2) % 2)
                                for j in range(4):
                                    h = 4 * (i - 2) + j
                                    to = depth * (j if a == 3 else h)
                                    last = pe.matmul(b[s][3][:, to:to + depth], probs[s][0:keys, at + T * j:at + T * j + T],
                                                     v[s][0:keys, depth * h:depth * h + depth], start=True, stop=True)
                                last.then_inc(ev["mixed"][s], 1)

                def o_flip(a):
                    for s in range(SLOTS):
                        pe.wait_ge(ev["onorm"][s], nth(it, "onorm", a))
                        pe.transpose(b[s][3][:, 256:384], o[s][:, :], ident).then_inc(ev["oflip"][s], 1)

                flip(0)
                project(0, 0, T)
                attend(0, T, vv, HD + 1)
                o_flip(0)
                for s in range(SLOTS):
                    pe.wait_ge(ev["oT"][s], nth(it, "oT", 0))
                    pe.matmul(b[s][3][:, 384:512], oT[s][:, :], w(0, "o"), start=True, stop=True).then_inc(ev["y"][s], 1)
                flip(1)
                project(1, 1, C)
                attend(1, C, vv, HD + 1)
                o_flip(1)
                for s in range(SLOTS):
                    pe.wait_ge(ev["oT"][s], nth(it, "oT", 1))
                    for c in range(2):
                        pe.matmul(b[s][3][:, D * c:D * c + D], w(1, "m1")[:, D * c:D * c + D], oT[s][:, :],
                                  start=True, stop=False)
                        last = pe.matmul(b[s][3][:, D * c:D * c + D], row("xm1")[:, D * c:D * c + D], k16("ones"),
                                         start=False, stop=True)
                    last.then_inc(ev["mlp"][s], 1)
                for s in range(SLOTS):
                    pe.wait_ge(ev["mlp_act"][s], nth(it, "mlp_act"))
                    for c in range(2):
                        pe.matmul(b[s][3][:, 384:512], mh[s][:, D * c:D * c + D], w(1, "m2")[:, D * c:D * c + D],
                                  start=(c == 0), stop=False)
                    pe.matmul(b[s][3][:, 384:512], k16("ones"), row("xm2"), start=False, stop=True)\
                        .then_inc(ev["y"][s], 1)
                flip(2)
                for s in range(SLOTS):
                    pe.wait_ge(ev["xT"][s], nth(it, "xT", 2))
                    pe.matmul(b[s][3][:, 128:128 + NE], xT[s][:, :], w(2, "gate"), start=True, stop=True)
                    for name, at in (("s1", 256), ("s3", 384)):
                        pe.matmul(b[s][3][:, at:at + 128], w(2, name), xT[s][:, :], start=True, stop=False)
                        last = pe.matmul(b[s][3][:, at:at + 128], row(name), k16("ones"), start=False, stop=True)
                    last.then_inc(ev["gate"][s], 1)

                def hidden(s, name, bias, c, to):
                    pe.matmul(to, w(2, name)[:, 128 * c:128 * c + 128], xT[s][:, :], start=True, stop=False)
                    return pe.matmul(to, row(bias)[:, 128 * c:128 * c + 128], k16("ones"), start=False, stop=True)

                for s in range(SLOTS):
                    for c in range(8):
                        last = hidden(s, "w1", "e1", c, b[s][c // 4][:, 128 * (c % 4):128 * (c % 4) + 128])
                    last.then_inc(ev["h1"][s], 1)
                for s in range(SLOTS):
                    for c in range(4):
                        hidden(s, "w3", "e3", c, b[s][2][:, 128 * c:128 * c + 128])
                    pe.wait_ge(ev["shared"][s], nth(it, "shared"))
                    pe.wait_ge(ev["masks"][s], nth(it, "masks"))
                    pe.transpose(b[s][3][:, 128:192].bitcast(BF16), mk[s][:, :], k16("ident")).then_inc(ev["mflip"][s], 1)
                for s in range(SLOTS):
                    pe.wait_ge(ev["maskT"][s], nth(it, "maskT"))
                    for c in range(4, 8):
                        last = hidden(s, "w3", "e3", c, b[s][3][:, 128 * (c - 4):128 * (c - 4) + 128])
                    last.then_inc(ev["h3"][s], 1)
                for j, name in enumerate(("spreadA", "spreadB")):
                    for s in range(SLOTS):
                        pe.wait_ge(ev["hidden"][s], nth(it, "hidden"))
                        for c in range(8):
                            last = pe.matmul(b[s][2 * j + c // 4][:, 128 * (c % 4):128 * (c % 4) + 128],
                                             k16("sel")[:, 128 * (8 * j + c):128 * (8 * j + c) + 128], mT[s][:, :],
                                             start=True, stop=True)
                        last.then_inc(ev[name][s], 1)
                for s in range(SLOTS):
                    pe.wait_ge(ev["square"][s], nth(it, "square"))
                    pe.wait_ge(ev["hA"][s], nth(it, "hA"))
                    pe.matmul(b[s][0][:, 128:256], sh[s][:, 128:256], w(2, "s2"), start=True, stop=False)
                    pe.matmul(b[s][0][:, 128:256], k16("ones"), row("s2"), start=False, stop=True)
                    for c in range(8):
                        pe.matmul(b[s][0][:, 2 * c:2 * c + 2], wide[s][:, 128 * c:128 * c + 128], k32("pair"),
                                  start=True, stop=True)
                    pe.matmul(b[s][0][:, 16:18], sh[s][:, 256:384], k32("ones"), start=True, stop=True)\
                        .then_inc(ev["norms"][s], 1)
                for s in range(SLOTS):
                    for j, name in enumerate("AB"):
                        if j == 1:
                            pe.wait_ge(ev["hB"][s], nth(it, "hB"))
                        to = b[s][1][:, D * j:D * j + D]
                        for c in range(8):
                            pe.matmul(to, big[s][:, 2048 + 1024 * j + 128 * c:2176 + 1024 * j + 128 * c],
                                      w(2, "w2")[:, 128 * c:128 * c + 128], start=(c == 0), stop=False)
                        pe.matmul(to, mT[s][:, :], row("e" + name), start=False, stop=True)
                        last = pe.matmul(b[s][1][:, 256 + D * j:256 + D * j + D], mT[s][:, :], row("t" + name),
                                         start=True, stop=True)
                    last.then_inc(ev["experts"][s], 1)
                flip(3)
                project(2, 3, T)
                attend(2, T, vv, HD + 1)
                o_flip(2)
                for s in range(SLOTS):
                    pe.wait_ge(ev["oT"][s], nth(it, "oT", 2))
                    pe.matmul(b[s][3][:, 384:512], oT[s][:, :], w(3, "o"), start=True, stop=False)
                    pe.matmul(b[s][3][:, 384:512], k16("ones"), row("ao"), start=False, stop=True)\
                        .then_inc(ev["y"][s], 1)
                flip(4)
                for s in range(SLOTS):
                    pe.wait_ge(ev["xT"][s], nth(it, "xT", 4))
                    for c in range(8):
                        last = pe.matmul(b[s][c // 4][:, 128 * (c % 4):128 * (c % 4) + 128],
                                         w(4, "q")[:, 128 * c:128 * c + 128], xT[s][:, :], start=True, stop=True)
                    last.then_inc(ev["lq"][s], 1)
                    for c in range(8):
                        last = pe.matmul(b[s][2 + c // 4][:, C * (c % 4):C * (c % 4) + C],
                                         w(4, "k", CD)[:, 128 * c:128 * c + 128], ctx_in[s][0:CD, :], start=True, stop=True)
                    last.then_inc(ev["lk"][s], 1)
                for s in range(SLOTS):
                    pe.wait_ge(ev["lqs"][s], nth(it, "lqs"))
                    for j in range(2):
                        last = pe.matmul(b[s][j][0:C, :], ctx_in[s][0:CD, :], w(4, "v", CD)[:, 512 * j:512 * j + 512],
                                         start=True, stop=True)
                    last.then_inc(ev["lv"][s], 1)
                attend(3, C, lv, LHD + 1)
                for s in range(SLOTS):
                    pe.wait_ge(ev["onorm"][s], nth(it, "onorm", 6))
                    for c in range(8):
                        last = pe.transpose(b[s][c // 4][:, 128 * (c % 4):128 * (c % 4) + 128],
                                            big[s][:, 1024 + 128 * c:1152 + 128 * c], ident)
                    last.then_inc(ev["oflip"][s], 1)
                for s in range(SLOTS):
                    pe.wait_ge(ev["oT"][s], nth(it, "oT", 3))
                    for c in range(8):
                        pe.matmul(b[s][3][:, 384:512], big[s][:, 2048 + 128 * c:2176 + 128 * c],
                                  w(4, "o")[:, 128 * c:128 * c + 128], start=(c == 0), stop=False)
                    pe.matmul(b[s][3][:, 384:512], k16("ones"), row("lo"), start=False, stop=True)\
                        .then_inc(ev["y"][s], 1)
                flip(5)
                for s in range(SLOTS):
                    pe.wait_ge(ev["xT"][s], nth(it, "xT", 5))
                    pe.matmul(b[s][3][:, 128:128 + NF], xT[s][:, :], w(5, "r"), start=True, stop=True)\
                        .then_inc(ev["flogits"][s], 1)
                for s in range(SLOTS):
                    pe.wait_ge(ev["fmasked"][s], nth(it, "fmasked"))
                    for e in range(NF):
                        pe.transpose(b[s][2][:, T * e:T * e + T], big[s][:, 3072 + D * e:3072 + D * e + D], ident)
                    pe.transpose(b[s][3][:, 128:192].bitcast(BF16), mk[s][:, :], k16("ident")).then_inc(ev["fflip"][s], 1)
                for s in range(SLOTS):
                    pe.wait_ge(ev["fT"][s], nth(it, "fT"))
                    for c in range(4):
                        to = b[s][0][:, 128 * c:128 * c + 128]
                        for e in range(NF):
                            pe.matmul(to, w(5, "w1")[:, FI * e + 128 * c:FI * e + 128 * c + 128],
                                      big[s][:, T * e:T * e + T], start=(e == 0), stop=False)
                        last = pe.matmul(to, row("f1")[:, 128 * c:128 * c + 128], mT[s][:, :], start=False, stop=True)
                    last.then_inc(ev["fh"][s], 1)
                for s in range(SLOTS):
                    pe.wait_ge(ev["fact"][s], nth(it, "fact"))
                    for c in range(4):
                        pe.matmul(b[s][3][:, 384:512], big[s][:, 512 + 128 * c:640 + 128 * c],
                                  w(5, "o")[:, 128 * c:128 * c + 128], start=(c == 0), stop=False)
                    pe.matmul(b[s][3][:, 384:512], k16("ones"), row("fo"), start=False, stop=True)\
                        .then_inc(ev["y"][s], 1)


CLEARED = 8 + 4 * SLOTS


def _bf16_parts(a):
    out = []
    for _ in range(3):
        hi = a.astype("bfloat16").astype(np.float32)
        out.append(hi)
        a = a - hi
    return out


def _constants():
    ccol, n16 = columns(CONST16)
    fcol, n32 = columns(CONST32)
    c16 = np.zeros((128, n16), np.float32)
    c32 = np.zeros((128, n32), np.float32)
    p = np.arange(128)
    c16[:, ccol["ident"]] = np.eye(128)
    c16[:, ccol["causal"]] = np.where(p[:, None] >= np.arange(T)[None, :], 0.0, NEG)
    slopes = (2.0 ** (-0.5 * (np.arange(H) + 1))).astype(np.float32)
    by_key = (slopes[:, None] * np.arange(T, dtype=np.float32)[None, :]).reshape(-1)
    unscale = np.float32(HD ** 0.5)
    for q, (a, s) in enumerate(zip(_bf16_parts(by_key * unscale), _bf16_parts(np.repeat(slopes, T) * unscale))):
        c16[32 * q, ccol["ones"]] = 1.0
        c16[32 * q, ccol["alibi_q"]] = 1.0
        c16[32 * q + 1, ccol["alibi_q"]] = -np.arange(T)
        c16[32 * q, ccol["alibi_k"]] = a
        c16[32 * q + 1, ccol["alibi_k"]] = s
    sel = c16[:, ccol["sel"]].reshape(128, 2, 8, 2, EI)
    for j in range(2):
        for e in range(NE):
            sel[NE * j + e, j, e // 2, e % 2, :] = 1.0
    c16[:, ccol["sel"]] = sel.reshape(128, -1)
    c32[:, fcol["ident"]] = np.eye(128)
    c32[:, fcol["head"]] = (p[:, None] % 32) // HD == np.arange(4)[None, :]
    c32[:, fcol["iota"]] = np.arange(NE)
    c32[:, fcol["iota_up"]] = np.arange(NE) + NE
    c32[:, fcol["origin"]] = np.arange(D) == 0
    c32[:, fcol["pair"]] = p[:, None] // EI == np.arange(2)[None, :]
    c32[:, fcol["ones"]] = 1.0
    return c16.astype("bfloat16"), c32


def _blank(table, n=128):
    cols, width = columns(table)
    return cols, np.zeros((n, width), np.float32)


def _chunks(a):
    return a.reshape(-1, 128, a.shape[1]).transpose(1, 0, 2).reshape(128, -1)


def _weights(i):
    out = []
    c, a = _blank(WEIGHTS[0])
    wqkv = i["L0_attn_Wqkv"]
    a[:, 0:3 * D] = wqkv
    a[:, c["o"]] = i["L0_attn_Wout"]
    out.append(a)
    c, a = _blank(WEIGHTS[1])
    a[:, c["q"]] = i["L0_xattn_Wq"]
    a[0:CD, c["k"]], a[CD, c["k"]] = i["L0_xattn_Wk"], i["L0_xattn_bk"]
    a[0:CD, c["v"]], a[CD, c["v"]] = i["L0_xattn_Wv"], i["L0_xattn_bv"]
    a[:, c["m1"]] = i["L0_xattn_W1"]
    a[:, c["m2"]] = _chunks(i["L0_xattn_W2"])
    out.append(a)
    c, a = _blank(WEIGHTS[2])
    a[:, c["gate"]] = i["L0_ffn_gate_w"].T
    for name, src in (("w1", "We1"), ("w3", "We3")):
        padded = np.zeros((NE, EI, D), np.float32)
        padded[:, 1:] = i["L0_ffn_" + src]
        a[:, c[name]] = padded.reshape(NE * EI, D).T
    w2 = np.zeros((NE, EI, D), np.float32)
    w2[:, 1:, 1:] = i["L0_ffn_We2"].transpose(0, 2, 1)[:, 1:]
    a[:, c["w2"]] = _chunks(w2.reshape(NE * EI, D))
    for name, src in (("s1", "Ws1"), ("s3", "Ws3")):
        padded = np.zeros((D, D), np.float32)
        padded[1:] = i["L0_ffn_" + src]
        a[:, c[name]] = padded.T
    s2 = np.zeros((D, D), np.float32)
    s2[1:, 1:] = i["L0_ffn_Ws2"].T[1:]
    a[:, c["s2"]] = s2
    t = np.zeros((D,), np.float32)
    t[1:] = i["L0_ffn_Ws2"][:, 0]
    a[:, c["s2t"]] = t
    out.append(a)
    c, a = _blank(WEIGHTS[3])
    a[:, 0:3 * D] = i["L1_attn_w_qkv"].T
    a[:, c["ent"].start] = i["L1_attn_w_ent"][0]
    a[:, c["o"]] = i["L1_attn_w_out"].T
    a[:, c["g"]] = i["L1_attn_ln_g"][:, None]
    a[:, c["b"]] = i["L1_attn_ln_b"][:, None]
    out.append(a)
    c, a = _blank(WEIGHTS[4])
    a[:, c["q"]] = i["L1_xattn_w_q"]
    a[0:CD, c["k"]] = i["L1_xattn_w_k"]
    a[0:CD, c["v"]] = i["L1_xattn_w_v"]
    a[:, c["o"]] = _chunks(i["L1_xattn_w_o"])
    out.append(a)
    c, a = _blank(WEIGHTS[5])
    a[:, c["r"]] = i["L1_ffn_W_router"]
    a[:, c["w1"]] = i["L1_ffn_W1"].transpose(1, 0, 2).reshape(D, NF * FI)
    a[:, c["o"]] = _chunks(i["L1_ffn_Wo"])
    a[:, c["g"]] = i["L1_ffn_ln_gamma"]
    a[:, c["b"]] = i["L1_ffn_ln_beta"]
    out.append(a)
    return out


def _rows(i):
    c, a = _blank(ROWS, 32)
    a[0, c["xq"]] = i["L0_xattn_bq"]
    a[0, c["xm1"]] = i["L0_xattn_b1"]
    a[0, c["xm2"]] = i["L0_xattn_b2"]
    for name in ("s1", "s3", "s2"):
        a[0, c[name].start + 1:c[name].stop] = i["L0_ffn_b" + name]
    for name in ("e1", "e3"):
        padded = np.zeros((NE, EI), np.float32)
        padded[:, 1:] = i["L0_ffn_b" + name]
        a[0, c[name]] = padded.reshape(-1)
    for j, name in enumerate("AB"):
        a[NE * j:NE * j + NE, c["e" + name].start + 1:c["e" + name].stop] = i["L0_ffn_be2"]
        a[NE * j:NE * j + NE, c["t" + name].start + 1:c["t" + name].stop] = i["L0_ffn_We2"][:, :, 0]
    a[0, c["q"].start:c["v"].stop] = i["L1_attn_b_qkv"]
    a[0, c["ent"].start] = i["L1_attn_b_ent"][0]
    a[0, c["ao"]] = i["L1_attn_b_out"]
    a[0, c["lo"]] = i["L1_xattn_b_o"]
    a[0, c["fo"]] = i["L1_ffn_bo"]
    a[0:NF, c["f1"]] = i["L1_ffn_b1"]
    return a


def kernel(**inputs):
    import concourse.bacc as _bacc
    from concourse.bass_utils import run_bass_kernel_spmd as _run

    i = {name: np.asarray(a) for name, a in inputs.items()}
    ctx = np.ones((B, CD + 1, C), np.float32)
    ctx[:, 0:CD] = i["ctx_768"].transpose(0, 2, 1)
    c16, c32 = _constants()
    arrays = {"x": np.ascontiguousarray(i["x"]), "ctx": ctx}
    for n, a in enumerate(_weights(i)):
        arrays[f"weights_{n}"] = np.ascontiguousarray(a)
    arrays["rows"] = _rows(i)
    arrays["c16"], arrays["c32"] = c16, c32

    nc = _bacc.Bacc("TRN2", target_bir_lowering=False, num_devices=1)
    ap = {n: nc.dram_tensor(n + "_dram", a.shape, mybir.dt.from_np(a.dtype), kind="ExternalInput").ap()
          for n, a in arrays.items()}
    out = nc.dram_tensor("out_dram", (B, T, D), F32, kind="ExternalOutput").ap()
    decoder(nc, ap["x"], ap["ctx"], [ap[f"weights_{n}"] for n in range(6)], ap["rows"], ap["c16"], ap["c32"], out)
    r = _run(nc, [{n + "_dram": a for n, a in arrays.items()}], core_ids=[0])
    return r.results[0]["out_dram"]
```

```python
from contextlib import ExitStack

import numpy as np

import concourse.bass as bass
from concourse import mybir

F32 = mybir.dt.float32
BF16 = mybir.dt.bfloat16
U32 = mybir.dt.uint32
ACT = mybir.ActivationFunctionType
ALU = mybir.AluOpType
AX = mybir.AxisListType

B, T, D = 16, 128, 128
C, CD = 120, 96
H, HD = 16, 8
LHD = 64
NE, EI = 16, 64
NF, FI = 4, 512
SLOTS = 2
TURNS = B // SLOTS
UNITS = H // 4
NEG = -1.0e30

WEIGHTS = [
    [("q", D), ("k", D), ("v", D), ("o", D)],
    [("q", D), ("k", D), ("v", D), ("m1", 2 * D), ("m2", 2 * D)],
    [("gate", NE), ("s1", D), ("s3", D), ("w1", NE * EI), ("w3", NE * EI), ("w2", NE * EI), ("s2", D), ("s2t", D)],
    [("q", D), ("k", D), ("v", D), ("ent", 2), ("o", D), ("g", 1), ("b", 1)],
    [("q", H * LHD), ("k", H * LHD), ("v", H * LHD), ("o", H * LHD)],
    [("r", NF), ("w1", NF * FI), ("o", FI), ("g", D), ("b", D)],
]
ROWS = [("xq", D), ("xm1", 2 * D), ("xm2", D),
        ("s1", D), ("s3", D), ("s2", D), ("e1", NE * EI), ("e3", NE * EI),
        ("eA", D), ("eB", D), ("tA", D), ("tB", D),
        ("q", D), ("k", D), ("v", D), ("ent", 2), ("ao", D), ("lo", D), ("fo", D), ("f1", FI)]
CONST16 = [("ident", 128), ("causal", T), ("ones", 128), ("alibi_q", T), ("alibi_k", H * T), ("sel", 16 * 128)]
CONST32 = [("ident", 128), ("head", 4), ("iota", NE), ("iota_up", NE), ("origin", D), ("pair", 2), ("ones", 2)]


def columns(table):
    at, out = 0, {}
    for name, n in table:
        out[name] = slice(at, at + n)
        at += n
    return out, at


_at = columns(ROWS)[0]
GROUPS = [slice(_at["xq"].start, _at["xm2"].stop), slice(_at["s1"].start, _at["tB"].stop),
          slice(_at["q"].start, _at["f1"].stop)]

SPLIT = 5

EVENTS = {
    "x_loaded": 1, "ctx_loaded": 1, "x_taken": 1, "out_ready": 1,
    "var": 8, "rstd": 8, "xn": 8, "xflip": 6, "xT": 6,
    "qkv": 3, "q": 12, "v": 3, "kx": 3,
    "scores": 16, "shifted": 16, "flipped": 16, "probs": 16, "mixed": 16,
    "onorm": 7, "oflip": 4, "oT": 4, "y": 5, "mlp": 1, "mlp_act": 1, "gate": 1, "gate_exp": 1, "key_gate": 1,
    "logits": 2, "top": 1, "gexp": 1, "masks": 1, "mflip": 1, "maskT": 1,
    "shared_silu": 1, "shared": 1, "h1": 1, "h3": 1, "silu": 1, "hidden": 1, "square": 1,
    "spreadA": 1, "spreadB": 1, "hA": 1, "hB": 1, "norms": 1, "experts": 1,
    "time_in": 1, "time": 1, "time_part": 1, "otime_in": 1, "otime": 1, "inner": 3, "rescale": 3,
    "lq": 1, "lqs": 1, "lk": 1, "lks": 2, "lv": 1, "lvs": 1,
    "flogits": 1, "fmasked": 1, "fflip": 1, "fT": 1, "fh": 1, "fact": 1,
}
DVE_LINKS = (36, 30)
POOL_LINKS = (5, 5)


TURNS_OF = {
    "pool": "1010101000001",
    "act": "010101000010101001100010101011010100001011011",
    "dve": "101101010010010100010010110101011001011100100100111001000011011",
    "pe": "0101001000000100010100111101011010010100001001001010110111110101010010100101101011",
}

def decoder(nc, x, ctx, wts, rows, c16, c32, out):
    wcol = [columns(t) for t in WEIGHTS]
    rcol, nrows = columns(ROWS)
    ccol, n16 = columns(CONST16)
    fcol, n32 = columns(CONST32)

    with ExitStack() as stack:
        def sb(name, shape, dt=F32):
            return stack.enter_context(nc.sbuf_tensor(name, shape, dt))

        def per_slot(name, shape, dt=F32):
            return [sb(f"{name}{s}", shape, dt) for s in range(SLOTS)]

        bank = [[stack.enter_context(nc.psum_tensor(f"bank{s}_{b}", [128, 512], F32)) for b in range(4)]
                for s in range(SLOTS)]
        ev = {n: [stack.enter_context(nc.semaphore(f"{n}_{s}")) for s in range(SLOTS)] for n in EVENTS}
        dve_order = [stack.enter_context(nc.semaphore(f"dve_order{layer}")) for layer in range(2)]
        pool_order = [stack.enter_context(nc.semaphore(f"pool_order{layer}")) for layer in range(2)]
        out_free = [stack.enter_context(nc.semaphore(f"out_free{s}")) for s in range(SLOTS)]
        w_loaded = [stack.enter_context(nc.semaphore(f"w_loaded{i}")) for i in range(6)]
        const_loaded = stack.enter_context(nc.semaphore("const_loaded"))
        rows_loaded = stack.enter_context(nc.semaphore("rows_loaded"))
        cleared = stack.enter_context(nc.semaphore("cleared"))
        parts_step = stack.enter_context(nc.semaphore("parts_step"))
        parts_ready = stack.enter_context(nc.semaphore("parts_ready"))

        W = [sb(f"weights{i}", [128, wcol[i][1]]) for i in range(6)]
        K16 = sb("const16", [128, n16], BF16)
        K32 = sb("const32", [128, n32])
        raw = sb("raw_rows", [128, nrows])
        part = sb("row_parts", [128, nrows], BF16)
        powers = sb("powers", [128, 8])

        def w(i, name, rows_=128):
            return W[i][0:rows_, wcol[i][0][name]]

        def k16(name):
            return K16[:, ccol[name]]

        def k32(name, p=128):
            return K32[0:p, fcol[name]]

        def row(name):
            return part[:, rcol[name]]

        x_in = per_slot("x_in", [128, D])
        ctx_in = per_slot("ctx_in", [CD + 1, C])
        res = per_slot("res", [128, D])
        x_out = per_slot("x_out", [128, D])
        stats = per_slot("stats", [128, 6])
        mv = per_slot("mean_var", [128, 2])
        rstd = per_slot("rstd", [128, 2])
        pad = per_slot("pad", [128, 1])
        xn = per_slot("xn", [128, D])
        xT = per_slot("xT", [128, T])
        xl = per_slot("xl", [128, D])
        qq = per_slot("q_quadrants", [128, UNITS * T])
        kx = per_slot("k_heads", [128, 4 * T])
        vv = per_slot("v_ones", [128, H * (HD + 1)])
        top = per_slot("top", [128, 2 * 4])
        shifted = per_slot("shifted", [128, 2 * 512])
        probs = per_slot("probs", [128, 2 * 512])
        rsum = per_slot("rsum", [128, H])
        o = per_slot("o", [128, D])
        oT = per_slot("oT", [128, D])
        mh = per_slot("mlp_hidden", [128, 2 * D])
        gate = per_slot("gate", [128, 2])
        lg = per_slot("lg", [128, NE])
        pr = per_slot("pr", [128, NE])
        sm = per_slot("small", [128, 32])
        best = per_slot("best", [128, 8])
        at_best = per_slot("at_best", [128, 8], U32)
        mk = per_slot("masks", [128, 128], BF16)
        mT = per_slot("masksT", [128, T], BF16)
        big = per_slot("big", [128, 4 * 1024])
        wide = per_slot("wide", [128, 2048])
        sh = per_slot("shared", [128, 3 * 128])
        lv = per_slot("lv", [128, H * (LHD + 1)])
        oe = per_slot("experts_out", [128, 3 * D])
        tw = per_slot("time_part", [128, 2 * D])
        z = per_slot("z", [128, D])
        yy = per_slot("y_state", [128, D])
        junk = per_slot("junk", [128, D])

        def nth(m, name, k=0, by=1):
            return m * (EVENTS[name] * by) + (k + 1) * by

        def walk(engine, turns, arrivals, layer0, layer1):
            alone(layer0(0, 0), arrivals)
            arrivals.get("layer 1", idle)()
            with engine.Fori(0, TURNS - 1) as i:
                both(turns, layer0(1, i), layer1(0, i))
                both(turns, layer0(0, i + 1), layer1(1, i))
            both(turns, layer0(1, TURNS - 1), layer1(0, TURNS - 1))
            alone(layer1(1, TURNS - 1), {})

        b = bank
        block = stack.enter_context(nc.Block())

        def idle():
            pass

        def alone(layer, arrivals):
            for name, step in layer.items():
                arrivals.get(name, idle)()
                step()

        def both(turns, layer0, layer1):
            steps = iter(layer0.values()), iter(layer1.values())
            for which in turns:
                next(steps[int(which)])()

        @block.sync
        def _(sp):
            sp.dma_start(x_in[0][:, :], x[0]).then_inc(ev["x_loaded"][0], 16)
            sp.dma_start(K32[:, :], c32).then_inc(const_loaded, 16)
            sp.dma_start(W[0][:, :], wts[0]).then_inc(w_loaded[0], 16)
            sp.dma_start(K16[:, :], c16).then_inc(const_loaded, 16)
            for p in range(3):
                sp.dma_start(raw[32 * p:32 * p + 32, :], rows).then_inc(rows_loaded, 16)
            sp.dma_start(ctx_in[0][:, :], ctx[0]).then_inc(ev["ctx_loaded"][0], 16)
            for i in (1, 2):
                sp.dma_start(W[i][:, :], wts[i]).then_inc(w_loaded[i], 16)
            sp.dma_start(x_in[1][:, :], x[1]).then_inc(ev["x_loaded"][1], 16)
            sp.dma_start(ctx_in[1][:, :], ctx[1]).then_inc(ev["ctx_loaded"][1], 16)
            for i in (3, 4, 5):
                sp.dma_start(W[i][:, :], wts[i]).then_inc(w_loaded[i], 16)

            def load(s, m, event, last_read, dst, src):
                sp.wait_ge(ev[last_read][s], nth(m, last_read))
                sp.dma_start(dst[s][:, :], src[bass.ds(SLOTS * m + SLOTS + s, 1)].rearrange("b t d -> (b t) d"))\
                    .then_inc(ev[event][s], 16)

            def store(s, m):
                sp.wait_ge(ev["out_ready"][s], nth(m, "out_ready"))
                sp.dma_start(out[bass.ds(SLOTS * m + s, 1)].rearrange("b t d -> (b t) d"), x_out[s][:, :])\
                    .then_inc(out_free[s], 16)

            with sp.Fori(0, TURNS - 1) as i:
                load(0, i, "x_loaded", "x_taken", x_in, x)
                load(1, i, "x_loaded", "x_taken", x_in, x)
                load(0, i, "ctx_loaded", "lv", ctx_in, ctx)
                store(0, i)
                load(1, i, "ctx_loaded", "lv", ctx_in, ctx)
                store(1, i)
            for s in range(SLOTS):
                sp.wait_ge(ev["out_ready"][s], TURNS)
                sp.dma_start(out[SLOTS * (TURNS - 1) + s], x_out[s][:, :]).then_inc(out_free[s], 16)
            for s in range(SLOTS):
                sp.wait_ge(out_free[s], 16 * (TURNS + 1))

        @block.gpsimd
        def _(pool):
            for j, value in enumerate([-0.5, 0.5, 1e-5, 1e-6, 1e-12, 1.0, 1.0, 1.0]):
                pool.memset(powers[:, j:j + 1], value).then_inc(cleared, 1)
            for s in range(SLOTS):
                pool.memset(qq[s][:, :], 0.0).then_inc(cleared, 1)
                pool.memset(vv[s][:, :], 1.0).then_inc(cleared, 1)
                pool.memset(mk[s][:, :], 0.0).then_inc(cleared, 1)
                pool.memset(lv[s][:, :], 1.0).then_inc(cleared, 1)
                pool.memset(x_out[s][:, :], 0.0).then_inc(out_free[s], 16)
            half = powers[:, 1:2]
            minus_half = powers[:, 0:1]
            epsilon = {1e-5: powers[:, 2:3], 1e-6: powers[:, 3:4], 1e-12: powers[:, 4:5]}
            pool.wait_ge(cleared, CLEARED)

            def parts(layer, s, m):
                n = [0]

                def link(ins):
                    n[0] += 1
                    ins.then_inc(pool_order[layer], 1)
                    pool.wait_ge(pool_order[layer], (SLOTS * m + s) * POOL_LINKS[layer] + n[0])

                def ln(k, eps):
                    pool.wait_ge(ev["var"][s], nth(m, "var", k))
                    link(pool.tensor_tensor(rstd[s][:, 1:2], mv[s][:, 1:2], epsilon[eps], ALU.add))
                    pool.tensor_tensor(rstd[s][:, 0:1], rstd[s][:, 1:2], minus_half, ALU.pow).then_inc(ev["rstd"][s], 1)

                def time(source, done, src, dst):
                    pool.wait_ge(ev[source][s], nth(m, source))
                    link(pool.tensor_tensor(sm[s][:, 12:15], sm[s][:, src], powers[:, 5:8], ALU.add))
                    pool.tensor_tensor(sm[s][:, dst], sm[s][:, 12:15], half.to_broadcast([128, 3]), ALU.pow)\
                        .then_inc(ev[done][s], 1)

                def rescale(k):
                    pool.wait_ge(ev["inner"][s], nth(m, "inner", k))
                    pool.tensor_tensor(sm[s][:, 18:19], sm[s][:, 17:18], minus_half, ALU.pow)\
                        .then_inc(ev["rescale"][s], 1)

                return ln, time, rescale

            def layer0(s, m):
                ln, time, rescale = parts(0, s, m)
                return {
                    "x0.stats": lambda: ln(0, 1e-5),
                    "x1.stats": lambda: ln(1, 1e-5),
                    "x2.stats": lambda: ln(2, 1e-5),
                    "e.norms": lambda: time("time_in", "time", slice(0, 3), slice(3, 6)),
                    "e.out": lambda: time("otime_in", "otime", slice(6, 9), slice(9, 12)),
                    "e.step0": lambda: rescale(0),
                    "e.step1": lambda: rescale(1),
                    "e.step2": lambda: rescale(2),
                }

            def layer1(s, m):
                ln, _, _ = parts(1, s, m)
                return {
                    "x3.stats": lambda: ln(3, 1e-5),
                    "x4.stats": lambda: ln(4, 1e-6),
                    "x5.stats": lambda: ln(5, 1e-5),
                    "x6.stats": lambda: ln(6, 1e-5),
                    "x7.stats": lambda: ln(7, 1e-12),
                }

            walk(pool, TURNS_OF["pool"], {}, layer0, layer1)

        @block.scalar
        def _(act):
            act.wait_ge(cleared, CLEARED)
            arrivals = {"layer 1": lambda: act.wait_ge(w_loaded[3], 16)}

            def parts(s, m):
                def flip_out(k):
                    act.wait_ge(ev["xflip"][s], nth(m, "xflip", k))
                    if k == 3:
                        act.activation(xT[s][:, :], b[s][3][:, 0:T], ACT.Identity, bias=w(3, "b"), scale=w(3, "g"))\
                            .then_inc(ev["xT"][s], 1)
                    else:
                        act.activation(xT[s][:, :], b[s][3][:, 0:T], ACT.Copy).then_inc(ev["xT"][s], 1)

                def q_out(a):
                    act.wait_ge(ev["qkv"][s], nth(m, "qkv", a))
                    if a == 2:
                        act.activation(gate[s][:, 0:1], b[s][3][:, 384:385], ACT.Exp, scale=-1.0)\
                            .then_inc(ev["gate_exp"][s], 1)
                    for i in range(UNITS):
                        act.activation(qq[s][32 * i:32 * i + 32, T * i:T * i + T],
                                       b[s][3][32 * i:32 * i + 32, 128:256], ACT.Copy).then_inc(ev["q"][s], 1)

                def v_out(a, keys):
                    if a == 2:
                        act.wait_ge(ev["key_gate"][s], nth(m, "key_gate"))
                    act.activation(vv[s][0:keys, :].rearrange("p (h d) -> p h d", d=HD + 1)[:, :, 0:HD],
                                   b[s][3][0:keys, 256:384].rearrange("p (h d) -> p h d", d=HD), ACT.Copy,
                                   scale=gate[s][:, 1:2] if a == 2 else 1.0).then_inc(ev["v"][s], 1)

                def exps(a, keys, scale, i):
                    act.wait_ge(ev["flipped"][s], nth(m, "flipped", 4 * a + i))
                    if i >= 2:
                        act.wait_ge(ev["mixed"][s], nth(m, "mixed", 4 * a + i - 2))
                    act.activation(probs[s][0:keys, 512 * (i % 2):512 * (i % 2) + 512], b[s][2][0:keys, :],
                                   ACT.Exp, scale=scale).then_inc(ev["probs"][s], 1)

                def attend(a, keys, scale):
                    return {f"a{a}.exp{i}": lambda i=i: exps(a, keys, scale, i) for i in range(UNITS)}

                def o_out(a):
                    act.wait_ge(ev["oflip"][s], nth(m, "oflip", a))
                    act.activation(oT[s][:, :], b[s][3][:, 256:384], ACT.Copy).then_inc(ev["oT"][s], 1)

                return flip_out, q_out, v_out, attend, o_out

            def layer0(s, m):
                flip_out, q_out, v_out, attend, o_out = parts(s, m)

                def mlp_relu():
                    act.wait_ge(ev["mlp"][s], nth(m, "mlp"))
                    act.activation(mh[s][:, :], b[s][3][:, 0:2 * D], ACT.Relu).then_inc(ev["mlp_act"][s], 1)

                def router():
                    act.wait_ge(ev["gate"][s], nth(m, "gate"))
                    act.activation(lg[s][:, :], b[s][3][:, 128:128 + NE], ACT.Copy).then_inc(ev["logits"][s], 1)

                def router_exp():
                    act.wait_ge(ev["top"][s], nth(m, "top"))
                    act.activation(pr[s][:, :], lg[s][:, :], ACT.Exp, bias=sm[s][:, 19:20],
                                   accum_out=sm[s][:, 20:21]).then_inc(ev["gexp"][s], 1)

                def shared_silu():
                    act.activation(sh[s][:, 0:128], b[s][3][:, 256:384], ACT.Silu).then_inc(ev["shared_silu"][s], 1)

                def silus():
                    act.wait_ge(ev["h1"][s], nth(m, "h1"))
                    act.activation(big[s][:, 0:512], b[s][0][:, :], ACT.Silu)
                    act.activation(big[s][:, 512:1024], b[s][1][:, :], ACT.Silu).then_inc(ev["silu"][s], 1)

                def masks_out():
                    act.wait_ge(ev["mflip"][s], nth(m, "mflip"))
                    act.activation(mT[s][:, :], b[s][3][:, 128:192].bitcast(BF16), ACT.Copy).then_inc(ev["maskT"][s], 1)

                def squares():
                    act.wait_ge(ev["hidden"][s], nth(m, "hidden"))
                    act.activation(sh[s][:, 256:384], sh[s][:, 128:256], ACT.Square)
                    act.activation(wide[s][:, 0:1024], big[s][:, 1024:2048], ACT.Square).then_inc(ev["square"][s], 1)

                def time_part():
                    act.wait_ge(ev["time"][s], nth(m, "time"))
                    for j in range(2):
                        ins = act.activation(tw[s][:, D * j:D * j + D], b[s][0][:, 256 + D * j:256 + D * j + D], ACT.Copy,
                                             scale=sm[s][:, 3 + j:4 + j])
                    ins.then_inc(ev["time_part"][s], 1)

                return {
                    "x0.norm": lambda: flip_out(0), "a0.q": lambda: q_out(0), "a0.v": lambda: v_out(0, T), **attend(0, T, HD ** -0.5),
                    "a0.norm": lambda: o_out(0),
                    "x1.norm": lambda: flip_out(1), "a1.q": lambda: q_out(1), "a1.v": lambda: v_out(1, C), **attend(1, C, HD ** -0.5),
                    "a1.norm": lambda: o_out(1), "a1.mlp": mlp_relu,
                    "x2.norm": lambda: flip_out(2), "e.gate": router, "e.h1": router_exp, "e.h3": shared_silu,
                    "e.silu": silus,
                    "e.flip": masks_out, "e.hidden": squares, "e.out": time_part,
                }

            def layer1(s, m):
                flip_out, q_out, v_out, attend, o_out = parts(s, m)

                def wide_q_out():
                    act.wait_ge(ev["lq"][s], nth(m, "lq"))
                    act.activation(big[s][:, 0:512], b[s][0][:, :], ACT.Copy)
                    act.activation(big[s][:, 512:1024], b[s][1][:, :], ACT.Copy).then_inc(ev["lqs"][s], 1)

                def wide_v_out():
                    act.wait_ge(ev["lv"][s], nth(m, "lv"))
                    for j in range(2):
                        ins = act.activation(
                            lv[s][0:C, :].rearrange("p (h d) -> p h d", d=LHD + 1)[:, 8 * j:8 * j + 8, 0:LHD],
                            b[s][2 + j][0:C, :].rearrange("p (h d) -> p h d", d=LHD), ACT.Copy)
                    ins.then_inc(ev["lvs"][s], 1)

                def wide_o_out():
                    act.wait_ge(ev["oflip"][s], nth(m, "oflip", 3))
                    act.activation(big[s][:, 2048:2560], b[s][0][:, :], ACT.Copy)
                    act.activation(big[s][:, 2560:3072], b[s][1][:, :], ACT.Copy).then_inc(ev["oT"][s], 1)

                def router():
                    act.wait_ge(ev["flogits"][s], nth(m, "flogits"))
                    act.activation(lg[s][:, 0:NF], b[s][3][:, 128:128 + NF], ACT.Copy).then_inc(ev["logits"][s], 1)

                def masked_out():
                    act.wait_ge(ev["fflip"][s], nth(m, "fflip"))
                    act.activation(big[s][:, 0:512], b[s][2][:, :], ACT.Copy)
                    act.activation(mT[s][:, :], b[s][3][:, 128:192].bitcast(BF16), ACT.Copy).then_inc(ev["fT"][s], 1)

                def gelu():
                    act.wait_ge(ev["fh"][s], nth(m, "fh"))
                    act.activation(big[s][:, 512:1024], b[s][0][:, :], ACT.Gelu).then_inc(ev["fact"][s], 1)

                return {
                    "x4.norm": lambda: flip_out(3), "a2.q": lambda: q_out(2), "a2.v": lambda: v_out(2, T), **attend(2, T, HD ** -0.5 / 0.1),
                    "a2.norm": lambda: o_out(2),
                    "x5.norm": lambda: flip_out(4), "l.qk": wide_q_out, "l.v": wide_v_out, **attend(3, C, LHD ** -0.5),
                    "l.norm": wide_o_out,
                    "x6.norm": lambda: flip_out(5), "f.route": router, "f.flip": masked_out, "f.hidden": gelu,
                }

            walk(act, TURNS_OF["act"], arrivals, layer0, layer1)

        @block.vector
        def _(dve):
            dve.memset(raw[96:128, :], 0.0).then_inc(cleared, 1)
            dve.wait_ge(cleared, CLEARED)
            dve.wait_ge(const_loaded, 32)
            def split(group, *steps):
                at = GROUPS[group]
                for step in steps:
                    if group == step == 0:
                        dve.wait_ge(rows_loaded, 48)
                    if step > 0:
                        dve.wait_ge(parts_step, (SPLIT - 1) * group + step)
                    p = (128, 64, 64, 32, 32)[step]
                    if step % 2 == 0:
                        ins = dve.tensor_copy(part[0:p, at], raw[0:p, at])
                    else:
                        ins = dve.tensor_tensor(raw[0:p, at], raw[0:p, at], part[0:p, at], ALU.subtract)
                    ins.then_inc(parts_ready if step == SPLIT - 1 else parts_step, 1)

            def layer1_arrives():
                dve.wait_ge(w_loaded[5], 16)

            def experts_arrive():
                dve.wait_ge(w_loaded[2], 16)
                split(2, 0, 1, 2, 3, 4)

            arrivals = {"a0.norm": lambda: split(0, 0, 1, 2, 3, 4), "a0.out": lambda: split(1, 0),
                        "a1.proj": lambda: split(1, 1), "a1.shift0": lambda: split(1, 2),
                        "a1.norm": lambda: split(1, 3), "a1.out": lambda: split(1, 4),
                        "e.out": experts_arrive, "layer 1": layer1_arrives}

            def parts(layer, s, m):
                n = [0]

                def link(ins):
                    n[0] += 1
                    ins.then_inc(dve_order[layer], 1)
                    dve.wait_ge(dve_order[layer], (SLOTS * m + s) * DVE_LINKS[layer] + n[0])

                def hold():
                    dve.memset(pad[s][:, :], 0.0)

                def ln_stats(k, src):
                    if k == 0:
                        dve.wait_ge(ev["x_loaded"][s], nth(m, "x_loaded", 0, 16))
                    link(dve.bn_stats(stats[s][:, :], src[s][:, :]))
                    hold()
                    dve.bn_aggr(mv[s][:, :], stats[s][:, :]).then_inc(ev["var"][s], 1)

                def ln(k, src, dst):
                    dve.wait_ge(ev["rstd"][s], nth(m, "rstd", k))
                    dve.tensor_scalar(dst[s][:, :], src[s][:, :], mv[s][:, 0:1], rstd[s][:, 0:1],
                                      ALU.subtract, ALU.mult).then_inc(ev["xn"][s], 1)

                def k_heads(a, keys):
                    dve.wait_ge(ev["qkv"][s], nth(m, "qkv", a))
                    dve.tensor_tensor(kx[s][:, 0:4 * keys].rearrange("p (j t) -> p j t", j=4),
                                      b[s][2][:, 0:keys].unsqueeze(1).to_broadcast([128, 4, keys]),
                                      k32("head").unsqueeze(2).to_broadcast([128, 4, keys]), ALU.mult)\
                        .then_inc(ev["kx"][s], 1)

                def shift(a, keys, i):
                    dve.wait_ge(ev["scores"][s], nth(m, "scores", 4 * a + i))
                    sc = b[s][i % 2][:, 0:4 * keys].rearrange("p (j t) -> p j t", j=4)
                    largest = top[s][:, 4 * (i % 2):4 * (i % 2) + 4]
                    link(dve.tensor_reduce(largest, sc, AX.X, ALU.max))
                    if i >= 2:
                        dve.wait_ge(ev["flipped"][s], nth(m, "flipped", 4 * a + i - 2))
                    dve.tensor_tensor(
                        shifted[s][:, 512 * (i % 2):512 * (i % 2) + 4 * keys].rearrange("p (j t) -> p j t", j=4),
                        sc, largest.unsqueeze(2).to_broadcast([128, 4, keys]), ALU.subtract)\
                        .then_inc(ev["shifted"][s], 1)

                def attend(a, keys):
                    return {f"a{a}.shift{i}": lambda i=i: shift(a, keys, i) for i in range(UNITS)}

                def o_norm(a):
                    dve.wait_ge(ev["mixed"][s], nth(m, "mixed", 4 * a + 3))
                    o4 = b[s][3][:, 0:H * (HD + 1)].rearrange("p (h d) -> p h d", d=HD + 1)
                    link(dve.reciprocal(rsum[s][:, :], o4[:, :, HD]))
                    dve.tensor_tensor(o[s][:, :].rearrange("p (h d) -> p h d", d=HD), o4[:, :, 0:HD],
                                      rsum[s][:, :].unsqueeze(2).to_broadcast([128, H, HD]), ALU.mult)\
                        .then_inc(ev["onorm"][s], 1)

                def add_y(k, to, scale, old):
                    dve.wait_ge(ev["y"][s], nth(m, "y", k))
                    link(dve.scalar_tensor_tensor(to[s][:, :], b[s][3][:, 384:512], scale, old[s][:, :],
                                                  ALU.mult, ALU.add))

                return n, link, hold, ln_stats, ln, k_heads, shift, attend, o_norm, add_y

            def layer0(s, m):
                n, link, hold, ln_stats, ln, k_heads, shift, attend, o_norm, add_y = parts(0, s, m)

                def take_x():
                    add_y(0, res, 1.0, x_in)
                    dve.memset(pad[s][:, :], 0.0).then_inc(ev["x_taken"][s], 1)

                def top_logit():
                    dve.wait_ge(ev["logits"][s], nth(m, "logits", 0))
                    link(dve.tensor_reduce(sm[s][:, 16:17], lg[s][:, :], AX.X, ALU.max))
                    dve.tensor_scalar(sm[s][:, 19:20], sm[s][:, 16:17], -1.0, None, ALU.mult).then_inc(ev["top"][s], 1)

                def route():
                    dve.wait_ge(ev["gexp"][s], nth(m, "gexp"))
                    link(dve.reciprocal(sm[s][:, 21:22], sm[s][:, 20:21]))
                    link(dve.tensor_scalar(pr[s][:, :], pr[s][:, :], sm[s][:, 21:22], None, ALU.mult))
                    hold()
                    link(dve.max(best[s][:, :], pr[s][:, :]))
                    hold()
                    link(dve.max_index(at_best[s][:, :], best[s][:, :], pr[s][:, :]))
                    link(dve.tensor_copy(sm[s][:, 22:24], at_best[s][:, 0:2]))
                    dve.tensor_tensor(sm[s][:, 24:25], sm[s][:, 22:23], sm[s][:, 23:24], ALU.min)
                    link(dve.tensor_tensor(sm[s][:, 25:26], sm[s][:, 22:23], sm[s][:, 23:24], ALU.max))
                    by_part = mk[s][:, :].rearrange("p (a c) -> p a c", a=4)
                    for j in range(2):
                        ins = dve.tensor_scalar(by_part[:, 0:3, NE * j:NE * j + NE],
                                                k32("iota").unsqueeze(1).to_broadcast([128, 3, NE]),
                                                sm[s][:, 24 + j:25 + j], None, ALU.is_equal)
                    ins.then_inc(ev["masks"][s], 1)

                def shared_hidden():
                    dve.wait_ge(ev["shared_silu"][s], nth(m, "shared_silu"))
                    dve.tensor_tensor(sh[s][:, 128:256], b[s][3][:, 384:512], sh[s][:, 0:128], ALU.mult)\
                        .then_inc(ev["shared"][s], 1)

                def chosen_weights():
                    dve.wait_ge(ev["masks"][s], nth(m, "masks"))
                    for j in range(2):
                        ins = dve.tensor_tensor_reduce(out=junk[s][:, NE * j:NE * j + NE], in0=mk[s][:, NE * j:NE * j + NE],
                                                       in1=pr[s][:, :], scale=1.0, scalar=0.0, op0=ALU.mult, op1=ALU.add,
                                                       accum_out=sm[s][:, 26 + j:27 + j])
                    link(ins)

                def hidden():
                    dve.wait_ge(ev["silu"][s], nth(m, "silu"))
                    dve.wait_ge(ev["h3"][s], nth(m, "h3"))
                    dve.tensor_tensor(big[s][:, 1024:1536], b[s][2][:, :], big[s][:, 0:512], ALU.mult)
                    dve.tensor_tensor(big[s][:, 1536:2048], b[s][3][:, :], big[s][:, 512:1024], ALU.mult)\
                        .then_inc(ev["hidden"][s], 1)

                def keep(j, spread, done):
                    dve.wait_ge(ev["hidden"][s], nth(m, "hidden"))
                    dve.wait_ge(ev[spread][s], nth(m, spread))
                    for c in range(2):
                        ins = dve.tensor_tensor(big[s][:, 2048 + 1024 * j + 512 * c:2560 + 1024 * j + 512 * c],
                                                b[s][2 * j + c][:, :], big[s][:, 1024 + 512 * c:1536 + 512 * c], ALU.mult)
                    ins.then_inc(ev[done][s], 1)

                def norms():
                    dve.wait_ge(ev["norms"][s], nth(m, "norms"))
                    for j in range(2):
                        dve.tensor_tensor_reduce(out=junk[s][:, NE * j + 32:NE * j + 32 + NE], in0=b[s][0][:, 0:NE],
                                                 in1=mk[s][:, NE * j:NE * j + NE], scale=1.0, scalar=0.0,
                                                 op0=ALU.mult, op1=ALU.add, accum_out=sm[s][:, j:j + 1])
                    dve.tensor_copy(sm[s][:, 2:3], b[s][0][:, NE:NE + 1]).then_inc(ev["time_in"][s], 1)

                def outputs():
                    dve.wait_ge(ev["time_part"][s], nth(m, "time_part"))
                    dve.scalar_tensor_tensor(oe[s][:, 2 * D:3 * D], w(2, "s2t"), sm[s][:, 5:6], b[s][0][:, 128:256],
                                             ALU.mult, ALU.add)
                    dve.wait_ge(ev["experts"][s], nth(m, "experts"))
                    link(dve.tensor_tensor(oe[s][:, 0:2 * D], b[s][1][:, 0:2 * D], tw[s][:, :], ALU.add))
                    for j in range(3):
                        ins = dve.tensor_tensor_reduce(out=(junk[s][:, :], z[s][:, :], yy[s][:, :])[j],
                                                       in0=oe[s][:, D * j:D * j + D], in1=oe[s][:, D * j:D * j + D],
                                                       scale=1.0, scalar=0.0, op0=ALU.mult, op1=ALU.add,
                                                       accum_out=sm[s][:, 6 + j:7 + j])
                    ins.then_inc(ev["otime_in"][s], 1)

                def onto(k):
                    if k == 0:
                        dve.wait_ge(ev["otime"][s], nth(m, "otime"))
                        link(dve.tensor_copy(oe[s][:, :].rearrange("p (j d) -> p j d", j=3)[:, :, 0], sm[s][:, 9:12]))
                        link(dve.scalar_tensor_tensor(z[s][:, :], oe[s][:, 0:D], sm[s][:, 26:27], k32("origin"),
                                                      ALU.mult, ALU.add))
                    else:
                        dve.wait_ge(ev["rescale"][s], nth(m, "rescale", k - 1))
                        link(dve.scalar_tensor_tensor(z[s][:, :], z[s][:, :], sm[s][:, 18:19], oe[s][:, D * k:D * k + D],
                                                      ALU.mult, ALU.add))
                    link(dve.tensor_tensor_reduce(out=junk[s][:, 1:D], in0=z[s][:, 1:D], in1=z[s][:, 1:D], scale=1.0,
                                                  scalar=0.0, op0=ALU.mult, op1=ALU.add, accum_out=sm[s][:, 15:16]))
                    link(dve.scalar_tensor_tensor(sm[s][:, 16:17], z[s][:, 0:1], z[s][:, 0:1], sm[s][:, 15:16],
                                                  ALU.mult, ALU.subtract))
                    dve.tensor_scalar(sm[s][:, 17:18], sm[s][:, 16:17], 1e-6, None, ALU.max).then_inc(ev["inner"][s], 1)
                    if k == 0:
                        link(dve.tensor_scalar(oe[s][:, D:2 * D], oe[s][:, D:2 * D], sm[s][:, 27:28], None, ALU.mult))

                def end():
                    dve.wait_ge(ev["rescale"][s], nth(m, "rescale", 2))
                    link(dve.scalar_tensor_tensor(res[s][:, :], z[s][:, :], sm[s][:, 18:19], res[s][:, :],
                                                  ALU.mult, ALU.add))
                    assert n[0] == DVE_LINKS[0], n

                return {
                    "x0.stats": lambda: ln_stats(0, x_in), "x0.norm": lambda: ln(0, x_in, xn),
                    "a0.proj": lambda: k_heads(0, T), **attend(0, T), "a0.norm": lambda: o_norm(0), "a0.out": take_x,
                    "x1.stats": lambda: ln_stats(1, res), "x1.norm": lambda: ln(1, res, xn),
                    "a1.proj": lambda: k_heads(1, C), **attend(1, C), "a1.norm": lambda: o_norm(1),
                    "a1.out": lambda: add_y(1, res, 1.0, res),
                    "x2.stats": lambda: ln_stats(2, res), "x2.norm": lambda: ln(2, res, xn),
                    "e.gate": top_logit, "e.h1": route, "e.h3": shared_hidden, "e.weights": chosen_weights,
                    "e.hidden": hidden,
                    "e.A": lambda: keep(0, "spreadA", "hA"), "e.B": lambda: keep(1, "spreadB", "hB"),
                    "e.norms": norms, "e.out": outputs, "e.step0": lambda: onto(0), "e.step1": lambda: onto(1),
                    "e.step2": lambda: onto(2), "e.end": end,
                }

            def layer1(s, m):
                n, link, hold, ln_stats, ln, k_heads, shift, attend, o_norm, add_y = parts(1, s, m)

                def inner_stats():
                    dve.wait_ge(ev["xn"][s], nth(m, "xn", 3))
                    ln_stats(4, xl)

                def gated_heads():
                    k_heads(2, T)
                    dve.wait_ge(ev["gate_exp"][s], nth(m, "gate_exp"))
                    link(dve.tensor_scalar(gate[s][:, 1:2], gate[s][:, 0:1], 1.0, None, ALU.add))
                    link(dve.reciprocal(gate[s][:, 0:1], gate[s][:, 1:2]))
                    dve.tensor_scalar(gate[s][:, 1:2], gate[s][:, 0:1], 0.1, 2.0, ALU.max, ALU.min)\
                        .then_inc(ev["key_gate"][s], 1)

                def wide_k():
                    dve.wait_ge(ev["lk"][s], nth(m, "lk"))
                    k4 = wide[s][:, 0:16 * C].rearrange("p (c e t) -> p c e t", c=8, e=2)
                    for c in range(2):
                        src = b[s][2 + c][:, 0:4 * C].rearrange("p (c t) -> p c t", c=4)
                        for e in range(2):
                            ins = dve.tensor_scalar(k4[:, 4 * c:4 * c + 4, e, :], src, k32("pair")[:, e:e + 1], None,
                                                    ALU.mult)
                        ins.then_inc(ev["lks"][s], 1)

                def wide_norm(i):
                    dve.wait_ge(ev["mixed"][s], nth(m, "mixed", 12 + i))
                    o4 = b[s][3][:, 0:4 * (LHD + 1)].rearrange("p (h d) -> p h d", d=LHD + 1)
                    link(dve.reciprocal(rsum[s][:, 0:4], o4[:, :, LHD]))
                    at = 1024 + 256 * i
                    dve.tensor_tensor(big[s][:, at:at + 256].rearrange("p (h d) -> p h d", d=LHD), o4[:, :, 0:LHD],
                                      rsum[s][:, 0:4].unsqueeze(2).to_broadcast([128, 4, LHD]), ALU.mult)\
                        .then_inc(ev["onorm"][s], 1)

                def route():
                    dve.wait_ge(ev["logits"][s], nth(m, "logits", 1))
                    link(dve.tensor_reduce(sm[s][:, 16:17], lg[s][:, 0:NF], AX.X, ALU.max))
                    link(dve.tensor_scalar(sm[s][:, 19:23], lg[s][:, 0:NF], sm[s][:, 16:17], None, ALU.is_equal))
                    link(dve.scalar_tensor_tensor(sm[s][:, 24:28], sm[s][:, 19:23], -float(NE), k32("iota_up")[:, 0:NF],
                                                  ALU.mult, ALU.add))
                    link(dve.tensor_reduce(sm[s][:, 16:17], sm[s][:, 24:28], AX.X, ALU.min))
                    link(dve.tensor_scalar(sm[s][:, 19:23], k32("iota")[:, 0:NF], sm[s][:, 16:17], None, ALU.is_equal))
                    by_part = mk[s][:, :].rearrange("p (a c) -> p a c", a=4)
                    dve.tensor_copy(by_part[:, 0:3, 0:NF], sm[s][:, 19:23].unsqueeze(1).to_broadcast([128, 3, NF]))
                    dve.tensor_tensor(big[s][:, 3072:3584].rearrange("p (e d) -> p e d", e=NF),
                                      xn[s][:, :].unsqueeze(1).to_broadcast([128, NF, D]),
                                      sm[s][:, 19:23].unsqueeze(2).to_broadcast([128, NF, D]), ALU.mult)\
                        .then_inc(ev["fmasked"][s], 1)

                def end():
                    dve.wait_ge(ev["xn"][s], nth(m, "xn", 7))
                    link(dve.tensor_tensor(z[s][:, :], yy[s][:, :], w(5, "g"), ALU.mult))
                    link(dve.tensor_tensor(yy[s][:, :], z[s][:, :], w(5, "b"), ALU.add))
                    dve.wait_ge(out_free[s], m * 16 + 16)
                    dve.tensor_tensor(x_out[s][:, :], yy[s][:, :], res[s][:, :], ALU.add).then_inc(ev["out_ready"][s], 1)
                    assert n[0] == DVE_LINKS[1], n

                return {
                    "x3.stats": lambda: ln_stats(3, res), "x3.norm": lambda: ln(3, res, xl),
                    "x4.stats": inner_stats, "x4.norm": lambda: ln(4, xl, xn),
                    "a2.proj": gated_heads, **attend(2, T), "a2.norm": lambda: o_norm(2),
                    "a2.out": lambda: add_y(2, res, 0.1, res),
                    "x5.stats": lambda: ln_stats(5, res), "x5.norm": lambda: ln(5, res, xn), "l.qk": wide_k,
                    "a3.shift0": lambda: shift(3, C, 0), "a3.shift1": lambda: shift(3, C, 1),
                    "a3.shift2": lambda: shift(3, C, 2), "l.norm0": lambda: wide_norm(0),
                    "a3.shift3": lambda: shift(3, C, 3), "l.norm1": lambda: wide_norm(1),
                    "l.norm2": lambda: wide_norm(2), "l.norm3": lambda: wide_norm(3),
                    "l.out": lambda: add_y(3, res, 1.0, res),
                    "x6.stats": lambda: ln_stats(6, res), "x6.norm": lambda: ln(6, res, xn), "f.route": route,
                    "f.out": lambda: add_y(4, z, 1.0, xn),
                    "x7.stats": lambda: ln_stats(7, z), "x7.norm": lambda: ln(7, z, yy), "f.end": end,
                }

            walk(dve, TURNS_OF["dve"], arrivals, layer0, layer1)

        @block.tensor
        def _(pe):
            ident = k32("ident")
            pe.wait_ge(const_loaded, 32)
            pe.wait_ge(w_loaded[0], 16)
            pe.wait_ge(cleared, CLEARED)

            def arrived(sublayers, groups):
                for i in sublayers:
                    pe.wait_ge(w_loaded[i], 16)
                pe.wait_ge(parts_ready, groups)

            arrivals = {"a1.proj": lambda: arrived([1], 1), "e.gate": lambda: arrived([2], 2),
                        "layer 1": lambda: arrived([3, 4, 5], 3)}

            def parts(s, m):
                def flip(k):
                    pe.wait_ge(ev["xn"][s], nth(m, "xn", (0, 1, 2, 4, 5, 6)[k]))
                    pe.transpose(b[s][3][:, 0:T], xn[s][:, :], ident).then_inc(ev["xflip"][s], 1)

                def project(a, i, keys):
                    pe.wait_ge(ev["xT"][s], nth(m, "xT", (0, 1, 3)[a]))
                    kvT, depth = xT[s][:, :], 128
                    if a == 1:
                        pe.wait_ge(ev["ctx_loaded"][s], nth(m, "ctx_loaded", 0, 16))
                        kvT, depth = ctx_in[s][:, :], CD + 1
                    pe.matmul(b[s][2][:, 0:keys], w(i, "k", depth), kvT, start=True, stop=(a != 2))
                    if a == 2:
                        pe.matmul(b[s][2][:, 0:keys], row("k"), k16("ones"), start=False, stop=True)
                    pe.matmul(b[s][3][:, 128:256], w(i, "q"), xT[s][:, :], start=True, stop=(a == 0))
                    if a > 0:
                        pe.matmul(b[s][3][:, 128:256], row(("", "xq", "q")[a]), k16("ones"), start=False, stop=True)
                    wv = w(i, "v", depth)
                    if a == 2:
                        wv = W[i][:, wcol[i][0]["v"].start:wcol[i][0]["ent"].stop]
                    last = pe.matmul(b[s][3][0:keys, 256:256 + wv.shape[1]], kvT, wv, start=True, stop=(a != 2))
                    if a == 2:
                        last = pe.matmul(b[s][3][:, 256:386], k16("ones"),
                                         part[:, rcol["v"].start:rcol["ent"].stop], start=False, stop=True)
                    last.then_inc(ev["qkv"][s], 1)

                def scores(a, keys, i):
                    if a < 3:
                        pe.wait_ge(ev["q"][s], nth(m, "q", 4 * a + i))
                    if i == 0 and a < 3:
                        pe.wait_ge(ev["kx"][s], nth(m, "kx", a))
                    if i == 0 and a == 3:
                        pe.wait_ge(ev["lqs"][s], nth(m, "lqs"))
                    if i % 2 == 0 and a == 3:
                        pe.wait_ge(ev["lks"][s], nth(m, "lks", i // 2))
                    if i >= 2:
                        pe.wait_ge(ev["shifted"][s], nth(m, "shifted", 4 * a + i - 2))
                    sc = b[s][i % 2]
                    if a == 3:
                        for c in range(2 * i, 2 * i + 2):
                            last = pe.matmul(sc[:, 2 * C * (c % 2):2 * C * (c % 2) + 2 * C],
                                             big[s][:, 128 * c:128 * c + 128], wide[s][:, 2 * C * c:2 * C * c + 2 * C],
                                             start=True, stop=True)
                    else:
                        last = pe.matmul(sc[:, 0:4 * keys], qq[s][:, T * i:T * i + T], kx[s][:, 0:4 * keys],
                                         start=True, stop=(a == 1))
                        if a != 1:
                            last = pe.matmul(sc[:, :], k16("ident"), k16("causal").unsqueeze(1).to_broadcast([128, 4, T]),
                                             start=False, stop=(a == 2))
                        if a == 0:
                            last = pe.matmul(sc[:, :], k16("alibi_q"), k16("alibi_k")[:, 4 * T * i:4 * T * i + 4 * T],
                                             start=False, stop=True)
                    last.then_inc(ev["scores"][s], 1)

                def flip_scores(a, keys, i):
                    pe.wait_ge(ev["shifted"][s], nth(m, "shifted", 4 * a + i))
                    if i == 0 and a == 3:
                        pe.wait_ge(ev["lvs"][s], nth(m, "lvs"))
                    if i >= 1:
                        pe.wait_ge(ev["probs"][s], nth(m, "probs", 4 * a + i - 1))
                    at = 512 * (i % 2)
                    for j in range(4):
                        last = pe.transpose(b[s][2][0:keys, T * j:T * j + T],
                                            shifted[s][:, at + keys * j:at + keys * j + keys], ident)
                    last.then_inc(ev["flipped"][s], 1)

                def mix(a, keys, i, v, depth):
                    pe.wait_ge(ev["probs"][s], nth(m, "probs", 4 * a + i))
                    if a < 3 and i == 0:
                        pe.wait_ge(ev["v"][s], nth(m, "v", a))
                    if a == 3 and i >= 1:
                        pe.wait_ge(ev["onorm"][s], nth(m, "onorm", 3 + i - 1))
                    at = 512 * (i % 2)
                    for j in range(4):
                        h = 4 * i + j
                        to = depth * (j if a == 3 else h)
                        last = pe.matmul(b[s][3][:, to:to + depth], probs[s][0:keys, at + T * j:at + T * j + T],
                                         v[s][0:keys, depth * h:depth * h + depth], start=True, stop=True)
                    last.then_inc(ev["mixed"][s], 1)

                def attend(a, keys, v, depth):
                    steps = {}
                    for i in range(UNITS + 2):
                        if i < UNITS:
                            steps[f"a{a}.scores{i}"] = lambda i=i: scores(a, keys, i)
                        if 1 <= i <= UNITS:
                            steps[f"a{a}.flip{i - 1}"] = lambda i=i: flip_scores(a, keys, i - 1)
                        if i >= 2:
                            steps[f"a{a}.mix{i - 2}"] = lambda i=i: mix(a, keys, i - 2, v, depth)
                    return steps

                def o_flip(a):
                    pe.wait_ge(ev["onorm"][s], nth(m, "onorm", a))
                    pe.transpose(b[s][3][:, 256:384], o[s][:, :], ident).then_inc(ev["oflip"][s], 1)

                def output(a, i, bias):
                    pe.wait_ge(ev["oT"][s], nth(m, "oT", a))
                    last = pe.matmul(b[s][3][:, 384:512], oT[s][:, :], w(i, "o"), start=True, stop=(bias is None))
                    if bias is not None:
                        last = pe.matmul(b[s][3][:, 384:512], k16("ones"), row(bias), start=False, stop=True)
                    last.then_inc(ev["y"][s], 1)

                def chunked_output(src, at, chunks, i, name, bias):
                    for c in range(chunks):
                        pe.matmul(b[s][3][:, 384:512], src[s][:, at + 128 * c:at + 128 * c + 128],
                                  w(i, name)[:, 128 * c:128 * c + 128], start=(c == 0), stop=False)
                    pe.matmul(b[s][3][:, 384:512], k16("ones"), row(bias), start=False, stop=True)\
                        .then_inc(ev["y"][s], 1)

                return flip, project, attend, o_flip, output, chunked_output

            def layer0(s, m):
                flip, project, attend, o_flip, output, chunked_output = parts(s, m)

                def mlp():
                    pe.wait_ge(ev["oT"][s], nth(m, "oT", 1))
                    for c in range(2):
                        pe.matmul(b[s][3][:, D * c:D * c + D], w(1, "m1")[:, D * c:D * c + D], oT[s][:, :],
                                  start=True, stop=False)
                        last = pe.matmul(b[s][3][:, D * c:D * c + D], row("xm1")[:, D * c:D * c + D], k16("ones"),
                                         start=False, stop=True)
                    last.then_inc(ev["mlp"][s], 1)

                def mlp_out():
                    pe.wait_ge(ev["mlp_act"][s], nth(m, "mlp_act"))
                    chunked_output(mh, 0, 2, 1, "m2", "xm2")

                def router():
                    pe.wait_ge(ev["xT"][s], nth(m, "xT", 2))
                    pe.matmul(b[s][3][:, 128:128 + NE], xT[s][:, :], w(2, "gate"), start=True, stop=True)
                    for name, at in (("s1", 256), ("s3", 384)):
                        pe.matmul(b[s][3][:, at:at + 128], w(2, name), xT[s][:, :], start=True, stop=False)
                        last = pe.matmul(b[s][3][:, at:at + 128], row(name), k16("ones"), start=False, stop=True)
                    last.then_inc(ev["gate"][s], 1)

                def hidden(name, bias, c, to):
                    pe.matmul(to, w(2, name)[:, 128 * c:128 * c + 128], xT[s][:, :], start=True, stop=False)
                    return pe.matmul(to, row(bias)[:, 128 * c:128 * c + 128], k16("ones"), start=False, stop=True)

                def h1():
                    for c in range(8):
                        last = hidden("w1", "e1", c, b[s][c // 4][:, 128 * (c % 4):128 * (c % 4) + 128])
                    last.then_inc(ev["h1"][s], 1)

                def h3_low():
                    for c in range(4):
                        hidden("w3", "e3", c, b[s][2][:, 128 * c:128 * c + 128])

                def flip_masks():
                    pe.wait_ge(ev["shared"][s], nth(m, "shared"))
                    pe.wait_ge(ev["masks"][s], nth(m, "masks"))
                    pe.transpose(b[s][3][:, 128:192].bitcast(BF16), mk[s][:, :], k16("ident")).then_inc(ev["mflip"][s], 1)

                def h3_high():
                    pe.wait_ge(ev["maskT"][s], nth(m, "maskT"))
                    for c in range(4, 8):
                        last = hidden("w3", "e3", c, b[s][3][:, 128 * (c - 4):128 * (c - 4) + 128])
                    last.then_inc(ev["h3"][s], 1)

                def spread(j, name):
                    pe.wait_ge(ev["hidden"][s], nth(m, "hidden"))
                    for c in range(8):
                        last = pe.matmul(b[s][2 * j + c // 4][:, 128 * (c % 4):128 * (c % 4) + 128],
                                         k16("sel")[:, 128 * (8 * j + c):128 * (8 * j + c) + 128], mT[s][:, :],
                                         start=True, stop=True)
                    last.then_inc(ev[name][s], 1)

                def norms():
                    pe.wait_ge(ev["square"][s], nth(m, "square"))
                    pe.wait_ge(ev["hA"][s], nth(m, "hA"))
                    pe.matmul(b[s][0][:, 128:256], sh[s][:, 128:256], w(2, "s2"), start=True, stop=False)
                    pe.matmul(b[s][0][:, 128:256], k16("ones"), row("s2"), start=False, stop=True)
                    for j, name in enumerate("AB"):
                        pe.matmul(b[s][0][:, 256 + D * j:256 + D * j + D], mT[s][:, :], row("t" + name),
                                  start=True, stop=True)
                    for c in range(8):
                        pe.matmul(b[s][0][:, 2 * c:2 * c + 2], wide[s][:, 128 * c:128 * c + 128], k32("pair"),
                                  start=True, stop=True)
                    pe.matmul(b[s][0][:, 16:18], sh[s][:, 256:384], k32("ones"), start=True, stop=True)\
                        .then_inc(ev["norms"][s], 1)

                def outputs(j, name):
                    if j == 1:
                        pe.wait_ge(ev["hB"][s], nth(m, "hB"))
                    to = b[s][1][:, D * j:D * j + D]
                    for c in range(8):
                        pe.matmul(to, big[s][:, 2048 + 1024 * j + 128 * c:2176 + 1024 * j + 128 * c],
                                  w(2, "w2")[:, 128 * c:128 * c + 128], start=(c == 0), stop=False)
                    last = pe.matmul(to, mT[s][:, :], row("e" + name), start=False, stop=True)
                    if j == 1:
                        last.then_inc(ev["experts"][s], 1)

                return {
                    "x0.norm": lambda: flip(0), "a0.proj": lambda: project(0, 0, T), **attend(0, T, vv, HD + 1),
                    "a0.norm": lambda: o_flip(0), "a0.out": lambda: output(0, 0, None),
                    "x1.norm": lambda: flip(1), "a1.proj": lambda: project(1, 1, C), **attend(1, C, vv, HD + 1),
                    "a1.norm": lambda: o_flip(1), "a1.mlp": mlp, "a1.out": mlp_out,
                    "x2.norm": lambda: flip(2), "e.gate": router, "e.h1": h1, "e.h3": h3_low, "e.flip": flip_masks,
                    "e.hidden": h3_high, "e.A": lambda: spread(0, "spreadA"), "e.B": lambda: spread(1, "spreadB"),
                    "e.norms": norms, "e.outA": lambda: outputs(0, "A"), "e.outB": lambda: outputs(1, "B"),
                }

            def layer1(s, m):
                flip, project, attend, o_flip, output, chunked_output = parts(s, m)

                def wide_kq():
                    pe.wait_ge(ev["xT"][s], nth(m, "xT", 4))
                    for c in range(8):
                        last = pe.matmul(b[s][2 + c // 4][:, C * (c % 4):C * (c % 4) + C],
                                         w(4, "k", CD)[:, 128 * c:128 * c + 128], ctx_in[s][0:CD, :], start=True, stop=True)
                    last.then_inc(ev["lk"][s], 1)
                    for c in range(8):
                        last = pe.matmul(b[s][c // 4][:, 128 * (c % 4):128 * (c % 4) + 128],
                                         w(4, "q")[:, 128 * c:128 * c + 128], xT[s][:, :], start=True, stop=True)
                    last.then_inc(ev["lq"][s], 1)

                def wide_v():
                    for j in range(2):
                        pe.wait_ge(ev["lks"][s], nth(m, "lks", j))
                        last = pe.matmul(b[s][2 + j][0:C, :], ctx_in[s][0:CD, :], w(4, "v", CD)[:, 512 * j:512 * j + 512],
                                         start=True, stop=True)
                    last.then_inc(ev["lv"][s], 1)

                def wide_flip():
                    pe.wait_ge(ev["onorm"][s], nth(m, "onorm", 6))
                    for c in range(8):
                        last = pe.transpose(b[s][c // 4][:, 128 * (c % 4):128 * (c % 4) + 128],
                                            big[s][:, 1024 + 128 * c:1152 + 128 * c], ident)
                    last.then_inc(ev["oflip"][s], 1)

                def wide_out():
                    pe.wait_ge(ev["oT"][s], nth(m, "oT", 3))
                    chunked_output(big, 2048, 8, 4, "o", "lo")

                def router():
                    pe.wait_ge(ev["xT"][s], nth(m, "xT", 5))
                    pe.matmul(b[s][3][:, 128:128 + NF], xT[s][:, :], w(5, "r"), start=True, stop=True)\
                        .then_inc(ev["flogits"][s], 1)

                def flip_masked():
                    pe.wait_ge(ev["fmasked"][s], nth(m, "fmasked"))
                    for e in range(NF):
                        pe.transpose(b[s][2][:, T * e:T * e + T], big[s][:, 3072 + D * e:3072 + D * e + D], ident)
                    pe.transpose(b[s][3][:, 128:192].bitcast(BF16), mk[s][:, :], k16("ident")).then_inc(ev["fflip"][s], 1)

                def hidden():
                    pe.wait_ge(ev["fT"][s], nth(m, "fT"))
                    for c in range(4):
                        to = b[s][0][:, 128 * c:128 * c + 128]
                        for e in range(NF):
                            pe.matmul(to, w(5, "w1")[:, FI * e + 128 * c:FI * e + 128 * c + 128],
                                      big[s][:, T * e:T * e + T], start=(e == 0), stop=False)
                        last = pe.matmul(to, row("f1")[:, 128 * c:128 * c + 128], mT[s][:, :], start=False, stop=True)
                    last.then_inc(ev["fh"][s], 1)

                def out():
                    pe.wait_ge(ev["fact"][s], nth(m, "fact"))
                    chunked_output(big, 512, 4, 5, "o", "fo")

                wide_attention = attend(3, C, lv, LHD + 1)
                return {
                    "x4.norm": lambda: flip(3), "a2.proj": lambda: project(2, 3, T), **attend(2, T, vv, HD + 1),
                    "a2.norm": lambda: o_flip(2), "a2.out": lambda: output(2, 3, "ao"),
                    "x5.norm": lambda: flip(4), "l.kq": wide_kq, "a3.scores0": wide_attention["a3.scores0"],
                    "l.v": wide_v, **wide_attention,
                    "l.norm": wide_flip, "l.out": wide_out,
                    "x6.norm": lambda: flip(5), "f.route": router, "f.flip": flip_masked, "f.hidden": hidden,
                    "f.out": out,
                }

            walk(pe, TURNS_OF["pe"], arrivals, layer0, layer1)


CLEARED = 9 + 4 * SLOTS


def _bf16_parts(a):
    out = []
    for _ in range(3):
        hi = a.astype("bfloat16").astype(np.float32)
        out.append(hi)
        a = a - hi
    return out


def _constants():
    ccol, n16 = columns(CONST16)
    fcol, n32 = columns(CONST32)
    c16 = np.zeros((128, n16), np.float32)
    c32 = np.zeros((128, n32), np.float32)
    p = np.arange(128)
    c16[:, ccol["ident"]] = np.eye(128)
    c16[:, ccol["causal"]] = np.where(p[:, None] >= np.arange(T)[None, :], 0.0, NEG)
    slopes = (2.0 ** (-0.5 * (np.arange(H) + 1))).astype(np.float32)
    by_key = (slopes[:, None] * np.arange(T, dtype=np.float32)[None, :]).reshape(-1)
    unscale = np.float32(HD ** 0.5)
    for q, (a, s) in enumerate(zip(_bf16_parts(by_key * unscale), _bf16_parts(np.repeat(slopes, T) * unscale))):
        c16[32 * q, ccol["ones"]] = 1.0
        c16[32 * q, ccol["alibi_q"]] = 1.0
        c16[32 * q + 1, ccol["alibi_q"]] = -np.arange(T)
        c16[32 * q, ccol["alibi_k"]] = a
        c16[32 * q + 1, ccol["alibi_k"]] = s
    sel = c16[:, ccol["sel"]].reshape(128, 2, 8, 2, EI)
    for j in range(2):
        for e in range(NE):
            sel[NE * j + e, j, e // 2, e % 2, :] = 1.0
    c16[:, ccol["sel"]] = sel.reshape(128, -1)
    c32[:, fcol["ident"]] = np.eye(128)
    c32[:, fcol["head"]] = (p[:, None] % 32) // HD == np.arange(4)[None, :]
    c32[:, fcol["iota"]] = np.arange(NE)
    c32[:, fcol["iota_up"]] = np.arange(NE) + NE
    c32[:, fcol["origin"]] = np.arange(D) == 0
    c32[:, fcol["pair"]] = p[:, None] // EI == np.arange(2)[None, :]
    c32[:, fcol["ones"]] = 1.0
    return c16.astype("bfloat16"), c32


def _blank(table, n=128):
    cols, width = columns(table)
    return cols, np.zeros((n, width), np.float32)


def _chunks(a):
    return a.reshape(-1, 128, a.shape[1]).transpose(1, 0, 2).reshape(128, -1)


def _weights(i):
    out = []
    c, a = _blank(WEIGHTS[0])
    wqkv = i["L0_attn_Wqkv"]
    a[:, 0:3 * D] = wqkv
    a[:, c["o"]] = i["L0_attn_Wout"]
    out.append(a)
    c, a = _blank(WEIGHTS[1])
    a[:, c["q"]] = i["L0_xattn_Wq"]
    a[0:CD, c["k"]], a[CD, c["k"]] = i["L0_xattn_Wk"], i["L0_xattn_bk"]
    a[0:CD, c["v"]], a[CD, c["v"]] = i["L0_xattn_Wv"], i["L0_xattn_bv"]
    a[:, c["m1"]] = i["L0_xattn_W1"]
    a[:, c["m2"]] = _chunks(i["L0_xattn_W2"])
    out.append(a)
    c, a = _blank(WEIGHTS[2])
    a[:, c["gate"]] = i["L0_ffn_gate_w"].T
    for name, src in (("w1", "We1"), ("w3", "We3")):
        padded = np.zeros((NE, EI, D), np.float32)
        padded[:, 1:] = i["L0_ffn_" + src]
        a[:, c[name]] = padded.reshape(NE * EI, D).T
    w2 = np.zeros((NE, EI, D), np.float32)
    w2[:, 1:, 1:] = i["L0_ffn_We2"].transpose(0, 2, 1)[:, 1:]
    a[:, c["w2"]] = _chunks(w2.reshape(NE * EI, D))
    for name, src in (("s1", "Ws1"), ("s3", "Ws3")):
        padded = np.zeros((D, D), np.float32)
        padded[1:] = i["L0_ffn_" + src]
        a[:, c[name]] = padded.T
    s2 = np.zeros((D, D), np.float32)
    s2[1:, 1:] = i["L0_ffn_Ws2"].T[1:]
    a[:, c["s2"]] = s2
    t = np.zeros((D,), np.float32)
    t[1:] = i["L0_ffn_Ws2"][:, 0]
    a[:, c["s2t"]] = t
    out.append(a)
    c, a = _blank(WEIGHTS[3])
    a[:, 0:3 * D] = i["L1_attn_w_qkv"].T
    a[:, c["ent"].start] = i["L1_attn_w_ent"][0]
    a[:, c["o"]] = i["L1_attn_w_out"].T
    a[:, c["g"]] = i["L1_attn_ln_g"][:, None]
    a[:, c["b"]] = i["L1_attn_ln_b"][:, None]
    out.append(a)
    c, a = _blank(WEIGHTS[4])
    a[:, c["q"]] = i["L1_xattn_w_q"]
    a[0:CD, c["k"]] = i["L1_xattn_w_k"]
    a[0:CD, c["v"]] = i["L1_xattn_w_v"]
    a[:, c["o"]] = _chunks(i["L1_xattn_w_o"])
    out.append(a)
    c, a = _blank(WEIGHTS[5])
    a[:, c["r"]] = i["L1_ffn_W_router"]
    a[:, c["w1"]] = i["L1_ffn_W1"].transpose(1, 0, 2).reshape(D, NF * FI)
    a[:, c["o"]] = _chunks(i["L1_ffn_Wo"])
    a[:, c["g"]] = i["L1_ffn_ln_gamma"]
    a[:, c["b"]] = i["L1_ffn_ln_beta"]
    out.append(a)
    return out


def _rows(i):
    c, a = _blank(ROWS, 32)
    a[0, c["xq"]] = i["L0_xattn_bq"]
    a[0, c["xm1"]] = i["L0_xattn_b1"]
    a[0, c["xm2"]] = i["L0_xattn_b2"]
    for name in ("s1", "s3", "s2"):
        a[0, c[name].start + 1:c[name].stop] = i["L0_ffn_b" + name]
    for name in ("e1", "e3"):
        padded = np.zeros((NE, EI), np.float32)
        padded[:, 1:] = i["L0_ffn_b" + name]
        a[0, c[name]] = padded.reshape(-1)
    for j, name in enumerate("AB"):
        a[NE * j:NE * j + NE, c["e" + name].start + 1:c["e" + name].stop] = i["L0_ffn_be2"]
        a[NE * j:NE * j + NE, c["t" + name].start + 1:c["t" + name].stop] = i["L0_ffn_We2"][:, :, 0]
    a[0, c["q"].start:c["v"].stop] = i["L1_attn_b_qkv"]
    a[0, c["ent"].start] = i["L1_attn_b_ent"][0]
    a[0, c["ao"]] = i["L1_attn_b_out"]
    a[0, c["lo"]] = i["L1_xattn_b_o"]
    a[0, c["fo"]] = i["L1_ffn_bo"]
    a[0:NF, c["f1"]] = i["L1_ffn_b1"]
    return a


def kernel(**inputs):
    import concourse.bacc as _bacc
    from concourse.bass_utils import run_bass_kernel_spmd as _run

    i = {name: np.asarray(a) for name, a in inputs.items()}
    ctx = np.ones((B, CD + 1, C), np.float32)
    ctx[:, 0:CD] = i["ctx_768"].transpose(0, 2, 1)
    c16, c32 = _constants()
    arrays = {"x": np.ascontiguousarray(i["x"]), "ctx": ctx}
    for n, a in enumerate(_weights(i)):
        arrays[f"weights_{n}"] = np.ascontiguousarray(a)
    arrays["rows"] = _rows(i)
    arrays["c16"], arrays["c32"] = c16, c32

    nc = _bacc.Bacc("TRN2", target_bir_lowering=False, num_devices=1)
    ap = {n: nc.dram_tensor(n + "_dram", a.shape, mybir.dt.from_np(a.dtype), kind="ExternalInput").ap()
          for n, a in arrays.items()}
    out = nc.dram_tensor("out_dram", (B, T, D), F32, kind="ExternalOutput").ap()
    decoder(nc, ap["x"], ap["ctx"], [ap[f"weights_{n}"] for n in range(6)], ap["rows"], ap["c16"], ap["c32"], out)
    r = _run(nc, [{n + "_dram": a for n, a in arrays.items()}], core_ids=[0])
    return r.results[0]["out_dram"]
```

```python
from contextlib import ExitStack

import numpy as np

import concourse.bass as bass
from concourse import mybir

F32 = mybir.dt.float32
BF16 = mybir.dt.bfloat16
U32 = mybir.dt.uint32
ACT = mybir.ActivationFunctionType
ALU = mybir.AluOpType
AX = mybir.AxisListType

B, T, D = 16, 128, 128
C, CD = 120, 96
H, HD = 16, 8
LHD = 64
NE, EI = 16, 64
NF, FI = 4, 512
SLOTS = 2
TURNS = B // SLOTS
UNITS = H // 4
NEG = -1.0e30

WEIGHTS = [
    [("q", D), ("k", D), ("v", D), ("o", D)],
    [("q", D), ("k", D), ("v", D), ("m1", 2 * D), ("m2", 2 * D), ("bq", 1), ("bm1", 2)],
    [("gate", NE), ("s1", D), ("s3", D), ("w1", NE * EI), ("w3", NE * EI), ("w2", NE * EI), ("s2", D), ("s2t", D),
     ("bs1", 1), ("bs3", 1), ("b1", 8), ("b3", 8)],
    [("q", D), ("k", D), ("v", D), ("ent", 2), ("o", D), ("g", 1), ("b", 1), ("bq", 1), ("bk", 1)],
    [("q", H * LHD), ("k", H * LHD), ("v", H * LHD), ("o", H * LHD)],
    [("r", NF), ("w1", NF * FI), ("o", FI), ("g", D), ("b", D)],
]
ROWS = [("xm2", D), ("s2", D), ("eA", D), ("eB", D), ("tA", D), ("tB", D),
        ("v", D), ("ent", 2), ("ao", D), ("lo", D), ("fo", D), ("f1", FI)]
CONST16 = [("ident", 128), ("causal", T), ("ones", 128), ("alibi_q", T), ("alibi_k", H * T), ("sel", 16 * 128)]
CONST32 = [("ident", 128), ("head", 4), ("iota", NE), ("iota_up", NE), ("origin", D), ("pair", 2), ("ones", 2)]


def columns(table):
    at, out = 0, {}
    for name, n in table:
        out[name] = slice(at, at + n)
        at += n
    return out, at


_at = columns(ROWS)[0]
GROUPS = [_at["xm2"], slice(_at["s2"].start, _at["tB"].stop), slice(_at["v"].start, _at["f1"].stop)]

SPLIT = 5

EVENTS = {
    "x_loaded": 1, "ctx_loaded": 1, "x_taken": 1, "out_ready": 1,
    "var": 8, "rstd": 8, "xn": 8, "xflip": 6, "xT": 6,
    "qkv": 3, "q": 12, "v": 3, "kx": 3,
    "scores": 16, "shifted": 16, "flipped": 16, "probs": 16, "mixed": 16,
    "onorm": 7, "oflip": 4, "oT": 4, "y": 5, "mlp": 1, "mlp_act": 1, "gate": 1, "gate_exp": 1, "key_gate": 1,
    "logits": 2, "top": 1, "gexp": 1, "masks": 1, "mflip": 1, "maskT": 1,
    "shared_silu": 1, "shared": 1, "h1": 1, "h3": 1, "silu": 1, "hidden": 1, "square": 1,
    "spreadA": 1, "spreadB": 1, "hA": 1, "hB": 1, "norms": 1, "experts": 1,
    "time_in": 1, "time": 1, "time_part": 1, "otime_in": 1, "otime": 1, "inner": 3, "rescale": 3,
    "lq": 1, "lqs": 1, "lk": 1, "lks": 2, "lv": 1, "lvs": 1,
    "flogits": 1, "fmasked": 1, "fflip": 1, "fT": 1, "fh": 1, "fact": 1,
}
LATE = [("e.out", "e.step0", "e.step1", "e.step2", "e.end"),
        ("f.hidden", "f.out", "x7.stats", "x7.norm", "f.end")]
DVE_LINKS = ((23, 13), (26, 4))
POOL_LINKS = ((4, 1), (4, 1))


TURNS_OF = {
    "pool": "1111101001010",
    "act": "001010010001010101010001010101101001000101101",
    "dve": "111111001100001001000110100010010110101011001011010011000111001",
    "pe": "0001010000100001000101001111010110100101000010010010101101111010110100101001010101",
}

def decoder(nc, x, ctx, wts, rows, c16, c32, out):
    wcol = [columns(t) for t in WEIGHTS]
    rcol, nrows = columns(ROWS)
    ccol, n16 = columns(CONST16)
    fcol, n32 = columns(CONST32)

    with ExitStack() as stack:
        def sb(name, shape, dt=F32):
            return stack.enter_context(nc.sbuf_tensor(name, shape, dt))

        def per_slot(name, shape, dt=F32):
            return [sb(f"{name}{s}", shape, dt) for s in range(SLOTS)]

        bank = [[stack.enter_context(nc.psum_tensor(f"bank{s}_{b}", [128, 512], F32)) for b in range(4)]
                for s in range(SLOTS)]
        ev = {n: [stack.enter_context(nc.semaphore(f"{n}_{s}")) for s in range(SLOTS)] for n in EVENTS}
        dve_order = [[stack.enter_context(nc.semaphore(f"dve_order{layer}_{late}")) for late in range(2)]
                     for layer in range(2)]
        pool_order = [[stack.enter_context(nc.semaphore(f"pool_order{layer}_{late}")) for late in range(2)]
                      for layer in range(2)]
        out_free = [stack.enter_context(nc.semaphore(f"out_free{s}")) for s in range(SLOTS)]
        w_loaded = [stack.enter_context(nc.semaphore(f"w_loaded{i}")) for i in range(6)]
        const_loaded = stack.enter_context(nc.semaphore("const_loaded"))
        rows_loaded = stack.enter_context(nc.semaphore("rows_loaded"))
        cleared = stack.enter_context(nc.semaphore("cleared"))
        parts_step = stack.enter_context(nc.semaphore("parts_step"))
        parts_ready = stack.enter_context(nc.semaphore("parts_ready"))

        W = [sb(f"weights{i}", [128, wcol[i][1]]) for i in range(6)]
        K16 = sb("const16", [128, n16], BF16)
        K32 = sb("const32", [128, n32])
        raw = sb("raw_rows", [128, nrows])
        part = sb("row_parts", [128, nrows], BF16)
        powers = sb("powers", [128, 8])

        def w(i, name, rows_=128):
            return W[i][0:rows_, wcol[i][0][name]]

        def k16(name):
            return K16[:, ccol[name]]

        def k32(name, p=128):
            return K32[0:p, fcol[name]]

        def row(name):
            return part[:, rcol[name]]

        x_in = per_slot("x_in", [128, D])
        ctx_in = per_slot("ctx_in", [CD + 1, C])
        res = per_slot("res", [128, D])
        x_out = per_slot("x_out", [128, D])
        stats = per_slot("stats", [128, 6])
        mv = per_slot("mean_var", [128, 2])
        rstd = per_slot("rstd", [128, 2])
        pad = per_slot("pad", [128, 1])
        xn = per_slot("xn", [128, D])
        xT = per_slot("xT", [128, T])
        xl = per_slot("xl", [128, D])
        qq = per_slot("q_quadrants", [128, UNITS * T])
        kx = per_slot("k_heads", [128, 4 * T])
        vv = per_slot("v_ones", [128, H * (HD + 1)])
        top = per_slot("top", [128, 2 * 4])
        shifted = per_slot("shifted", [128, 2 * 512])
        probs = per_slot("probs", [128, 2 * 512])
        rsum = per_slot("rsum", [128, H])
        o = per_slot("o", [128, D])
        oT = per_slot("oT", [128, D])
        mh = per_slot("mlp_hidden", [128, 2 * D])
        gate = per_slot("gate", [128, 2])
        lg = per_slot("lg", [128, NE])
        pr = per_slot("pr", [128, NE])
        sm = per_slot("small", [128, 32])
        best = per_slot("best", [128, 8])
        at_best = per_slot("at_best", [128, 8], U32)
        mk = per_slot("masks", [128, 128], BF16)
        mT = per_slot("masksT", [128, T], BF16)
        big = per_slot("big", [128, 4 * 1024])
        wide = per_slot("wide", [128, 2048])
        sh = per_slot("shared", [128, 3 * 128])
        lv = per_slot("lv", [128, H * (LHD + 1)])
        oe = per_slot("experts_out", [128, 3 * D])
        tw = per_slot("time_part", [128, 2 * D])
        z = per_slot("z", [128, D])
        yy = per_slot("y_state", [128, D])
        junk = per_slot("junk", [128, D])

        def nth(m, name, k=0, by=1):
            return m * (EVENTS[name] * by) + (k + 1) * by

        def walk(engine, turns, arrivals, layer0, layer1):
            def steps(layer, s, m, late):
                of_row = (layer0, layer1)[layer](s, 0 if m is None else m, late)
                return {name: idle if m is None else step for name, step in of_row.items()
                        if (name in LATE[layer]) == late}

            def first(s, last, m):
                return {**steps(1, s, last, True), **steps(0, s, m, False)}

            def second(s, m):
                return {**steps(0, s, m, True), **steps(1, s, m, False)}

            alone(steps(0, 0, 0, False), arrivals)
            arrivals.get("layer 1", idle)()
            both(turns, first(1, None, 0), second(0, 0))
            with engine.Fori(0, TURNS - 1) as i:
                both(turns, first(0, i, i + 1), second(1, i))
                both(turns, first(1, i, i + 1), second(0, i + 1))
            both(turns, first(0, TURNS - 1, None), second(1, TURNS - 1))
            alone(steps(1, 1, TURNS - 1, True), {})

        b = bank
        block = stack.enter_context(nc.Block())

        def idle():
            pass

        def alone(steps, arrivals):
            for name, step in steps.items():
                arrivals.get(name, idle)()
                step()

        def both(turns, first, second):
            steps = iter(first.values()), iter(second.values())
            for which in turns:
                next(steps[int(which)])()

        @block.sync
        def _(sp):
            sp.dma_start(x_in[0][:, :], x[0]).then_inc(ev["x_loaded"][0], 16)
            sp.dma_start(K32[:, :], c32).then_inc(const_loaded, 16)
            sp.dma_start(W[0][:, :], wts[0]).then_inc(w_loaded[0], 16)
            sp.dma_start(K16[:, :], c16).then_inc(const_loaded, 16)
            for p in range(3):
                sp.dma_start(raw[32 * p:32 * p + 32, :], rows).then_inc(rows_loaded, 16)
            sp.dma_start(ctx_in[0][:, :], ctx[0]).then_inc(ev["ctx_loaded"][0], 16)
            for i in (1, 2):
                sp.dma_start(W[i][:, :], wts[i]).then_inc(w_loaded[i], 16)
            sp.dma_start(x_in[1][:, :], x[1]).then_inc(ev["x_loaded"][1], 16)
            sp.dma_start(ctx_in[1][:, :], ctx[1]).then_inc(ev["ctx_loaded"][1], 16)
            for i in (3, 4, 5):
                sp.dma_start(W[i][:, :], wts[i]).then_inc(w_loaded[i], 16)

            def load(s, m, event, last_read, dst, src):
                sp.wait_ge(ev[last_read][s], nth(m, last_read))
                sp.dma_start(dst[s][:, :], src[bass.ds(SLOTS * m + SLOTS + s, 1)].rearrange("b t d -> (b t) d"))\
                    .then_inc(ev[event][s], 16)

            def store(s, m):
                sp.wait_ge(ev["out_ready"][s], nth(m, "out_ready"))
                sp.dma_start(out[bass.ds(SLOTS * m + s, 1)].rearrange("b t d -> (b t) d"), x_out[s][:, :])\
                    .then_inc(out_free[s], 16)

            with sp.Fori(0, TURNS - 1) as i:
                load(0, i, "x_loaded", "x_taken", x_in, x)
                load(1, i, "x_loaded", "x_taken", x_in, x)
                load(0, i, "ctx_loaded", "lv", ctx_in, ctx)
                store(0, i)
                load(1, i, "ctx_loaded", "lv", ctx_in, ctx)
                store(1, i)
            for s in range(SLOTS):
                sp.wait_ge(ev["out_ready"][s], TURNS)
                sp.dma_start(out[SLOTS * (TURNS - 1) + s], x_out[s][:, :]).then_inc(out_free[s], 16)
            for s in range(SLOTS):
                sp.wait_ge(out_free[s], 16 * (TURNS + 1))

        @block.gpsimd
        def _(pool):
            for j, value in enumerate([-0.5, 0.5, 1e-5, 1e-6, 1e-12, 1.0, 1.0, 1.0]):
                pool.memset(powers[:, j:j + 1], value).then_inc(cleared, 1)
            for s in range(SLOTS):
                pool.memset(qq[s][:, :], 0.0).then_inc(cleared, 1)
                pool.memset(vv[s][:, :], 1.0).then_inc(cleared, 1)
                pool.memset(mk[s][:, :], 0.0).then_inc(cleared, 1)
                pool.memset(lv[s][:, :], 1.0).then_inc(cleared, 1)
                pool.memset(x_out[s][:, :], 0.0).then_inc(out_free[s], 16)
            half = powers[:, 1:2]
            minus_half = powers[:, 0:1]
            epsilon = {1e-5: powers[:, 2:3], 1e-6: powers[:, 3:4], 1e-12: powers[:, 4:5]}
            pool.wait_ge(cleared, CLEARED)

            def parts(layer, late, s, m):
                n = [0]

                def link(ins):
                    n[0] += 1
                    ins.then_inc(pool_order[layer][late], 1)
                    pool.wait_ge(pool_order[layer][late], (SLOTS * m + s) * POOL_LINKS[layer][late] + n[0])

                def ln(k, eps):
                    pool.wait_ge(ev["var"][s], nth(m, "var", k))
                    link(pool.tensor_tensor(rstd[s][:, 1:2], mv[s][:, 1:2], epsilon[eps], ALU.add))
                    pool.tensor_tensor(rstd[s][:, 0:1], rstd[s][:, 1:2], minus_half, ALU.pow).then_inc(ev["rstd"][s], 1)

                def time(source, done, src, dst):
                    pool.wait_ge(ev[source][s], nth(m, source))
                    link(pool.tensor_tensor(sm[s][:, 12:15], sm[s][:, src], powers[:, 5:8], ALU.add))
                    pool.tensor_tensor(sm[s][:, dst], sm[s][:, 12:15], half.to_broadcast([128, 3]), ALU.pow)\
                        .then_inc(ev[done][s], 1)

                def rescale(k):
                    pool.wait_ge(ev["inner"][s], nth(m, "inner", k))
                    pool.tensor_tensor(sm[s][:, 18:19], sm[s][:, 17:18], minus_half, ALU.pow)\
                        .then_inc(ev["rescale"][s], 1)

                return ln, time, rescale

            def layer0(s, m, late):
                ln, time, rescale = parts(0, late, s, m)
                return {
                    "x0.stats": lambda: ln(0, 1e-5),
                    "x1.stats": lambda: ln(1, 1e-5),
                    "x2.stats": lambda: ln(2, 1e-5),
                    "e.norms": lambda: time("time_in", "time", slice(0, 3), slice(3, 6)),
                    "e.out": lambda: time("otime_in", "otime", slice(6, 9), slice(9, 12)),
                    "e.step0": lambda: rescale(0),
                    "e.step1": lambda: rescale(1),
                    "e.step2": lambda: rescale(2),
                }

            def layer1(s, m, late):
                ln, _, _ = parts(1, late, s, m)
                return {
                    "x3.stats": lambda: ln(3, 1e-5),
                    "x4.stats": lambda: ln(4, 1e-6),
                    "x5.stats": lambda: ln(5, 1e-5),
                    "x6.stats": lambda: ln(6, 1e-5),
                    "x7.stats": lambda: ln(7, 1e-12),
                }

            walk(pool, TURNS_OF["pool"], {}, layer0, layer1)

        @block.scalar
        def _(act):
            act.wait_ge(cleared, CLEARED)
            arrivals = {"a1.q": lambda: act.wait_ge(w_loaded[1], 16), "e.h3": lambda: act.wait_ge(w_loaded[2], 16),
                        "layer 1": lambda: act.wait_ge(w_loaded[3], 16)}

            def parts(s, m):
                def flip_out(k):
                    act.wait_ge(ev["xflip"][s], nth(m, "xflip", k))
                    if k == 3:
                        act.activation(xT[s][:, :], b[s][3][:, 0:T], ACT.Identity, bias=w(3, "b"), scale=w(3, "g"))\
                            .then_inc(ev["xT"][s], 1)
                    else:
                        act.activation(xT[s][:, :], b[s][3][:, 0:T], ACT.Copy).then_inc(ev["xT"][s], 1)

                def q_out(a):
                    act.wait_ge(ev["qkv"][s], nth(m, "qkv", a))
                    if a == 2:
                        act.activation(gate[s][:, 0:1], b[s][3][:, 384:385], ACT.Exp, scale=-1.0)\
                            .then_inc(ev["gate_exp"][s], 1)
                    for i in range(UNITS):
                        rows_ = slice(32 * i, 32 * i + 32)
                        act.activation(qq[s][rows_, T * i:T * i + T], b[s][3][rows_, 128:256], ACT.Identity,
                                       bias=0.0 if a == 0 else w((0, 1, 3)[a], "bq")[rows_, :]).then_inc(ev["q"][s], 1)

                def v_out(a, keys):
                    if a == 2:
                        act.wait_ge(ev["key_gate"][s], nth(m, "key_gate"))
                    act.activation(vv[s][0:keys, :].rearrange("p (h d) -> p h d", d=HD + 1)[:, :, 0:HD],
                                   b[s][3][0:keys, 256:384].rearrange("p (h d) -> p h d", d=HD), ACT.Copy,
                                   scale=gate[s][:, 1:2] if a == 2 else 1.0).then_inc(ev["v"][s], 1)

                def exps(a, keys, scale, i):
                    act.wait_ge(ev["flipped"][s], nth(m, "flipped", 4 * a + i))
                    if i >= 2:
                        act.wait_ge(ev["mixed"][s], nth(m, "mixed", 4 * a + i - 2))
                    act.activation(probs[s][0:keys, 512 * (i % 2):512 * (i % 2) + 512], b[s][2][0:keys, :],
                                   ACT.Exp, scale=scale).then_inc(ev["probs"][s], 1)

                def attend(a, keys, scale):
                    return {f"a{a}.exp{i}": lambda i=i: exps(a, keys, scale, i) for i in range(UNITS)}

                def o_out(a):
                    act.wait_ge(ev["oflip"][s], nth(m, "oflip", a))
                    act.activation(oT[s][:, :], b[s][3][:, 256:384], ACT.Copy).then_inc(ev["oT"][s], 1)

                return flip_out, q_out, v_out, attend, o_out

            def layer0(s, m, late):
                flip_out, q_out, v_out, attend, o_out = parts(s, m)

                def mlp_relu():
                    act.wait_ge(ev["mlp"][s], nth(m, "mlp"))
                    for c in range(2):
                        ins = act.activation(mh[s][:, D * c:D * c + D], b[s][3][:, D * c:D * c + D], ACT.Relu,
                                             bias=w(1, "bm1")[:, c:c + 1])
                    ins.then_inc(ev["mlp_act"][s], 1)

                def router():
                    act.wait_ge(ev["gate"][s], nth(m, "gate"))
                    act.activation(lg[s][:, :], b[s][3][:, 128:128 + NE], ACT.Copy).then_inc(ev["logits"][s], 1)

                def router_exp():
                    act.wait_ge(ev["top"][s], nth(m, "top"))
                    act.activation(pr[s][:, :], lg[s][:, :], ACT.Exp, bias=sm[s][:, 19:20],
                                   accum_out=sm[s][:, 20:21]).then_inc(ev["gexp"][s], 1)

                def shared_silu():
                    act.activation(sh[s][:, 0:128], b[s][3][:, 256:384], ACT.Silu, bias=w(2, "bs1")).then_inc(ev["shared_silu"][s], 1)

                def silus():
                    act.wait_ge(ev["h1"][s], nth(m, "h1"))
                    for c in range(8):
                        ins = act.activation(big[s][:, 128 * c:128 * c + 128],
                                             b[s][c // 4][:, 128 * (c % 4):128 * (c % 4) + 128], ACT.Silu,
                                             bias=w(2, "b1")[:, c:c + 1])
                    ins.then_inc(ev["silu"][s], 1)

                def masks_out():
                    act.wait_ge(ev["mflip"][s], nth(m, "mflip"))
                    act.activation(mT[s][:, :], b[s][3][:, 128:192].bitcast(BF16), ACT.Copy).then_inc(ev["maskT"][s], 1)

                def squares():
                    act.wait_ge(ev["hidden"][s], nth(m, "hidden"))
                    act.activation(sh[s][:, 256:384], sh[s][:, 128:256], ACT.Square)
                    act.activation(wide[s][:, 0:1024], big[s][:, 1024:2048], ACT.Square).then_inc(ev["square"][s], 1)

                def time_part():
                    act.wait_ge(ev["time"][s], nth(m, "time"))
                    for j in range(2):
                        ins = act.activation(tw[s][:, D * j:D * j + D], b[s][0][:, 256 + D * j:256 + D * j + D], ACT.Copy,
                                             scale=sm[s][:, 3 + j:4 + j])
                    ins.then_inc(ev["time_part"][s], 1)

                return {
                    "x0.norm": lambda: flip_out(0), "a0.q": lambda: q_out(0), "a0.v": lambda: v_out(0, T),
                    **attend(0, T, HD ** -0.5),
                    "a0.norm": lambda: o_out(0),
                    "x1.norm": lambda: flip_out(1), "a1.q": lambda: q_out(1), "a1.v": lambda: v_out(1, C),
                    **attend(1, C, HD ** -0.5),
                    "a1.norm": lambda: o_out(1), "a1.mlp": mlp_relu,
                    "x2.norm": lambda: flip_out(2), "e.gate": router, "e.h1": router_exp, "e.h3": shared_silu,
                    "e.silu": silus,
                    "e.flip": masks_out, "e.hidden": squares, "e.time": time_part,
                }

            def layer1(s, m, late):
                flip_out, q_out, v_out, attend, o_out = parts(s, m)

                def wide_q_out():
                    act.wait_ge(ev["lq"][s], nth(m, "lq"))
                    act.activation(big[s][:, 0:512], b[s][0][:, :], ACT.Copy)
                    act.activation(big[s][:, 512:1024], b[s][1][:, :], ACT.Copy).then_inc(ev["lqs"][s], 1)

                def wide_v_out():
                    act.wait_ge(ev["lv"][s], nth(m, "lv"))
                    for j in range(2):
                        ins = act.activation(
                            lv[s][0:C, :].rearrange("p (h d) -> p h d", d=LHD + 1)[:, 8 * j:8 * j + 8, 0:LHD],
                            b[s][2 + j][0:C, :].rearrange("p (h d) -> p h d", d=LHD), ACT.Copy)
                    ins.then_inc(ev["lvs"][s], 1)

                def wide_o_out():
                    act.wait_ge(ev["oflip"][s], nth(m, "oflip", 3))
                    act.activation(big[s][:, 2048:2560], b[s][0][:, :], ACT.Copy)
                    act.activation(big[s][:, 2560:3072], b[s][1][:, :], ACT.Copy).then_inc(ev["oT"][s], 1)

                def router():
                    act.wait_ge(ev["flogits"][s], nth(m, "flogits"))
                    act.activation(lg[s][:, 0:NF], b[s][3][:, 128:128 + NF], ACT.Copy).then_inc(ev["logits"][s], 1)

                def masked_out():
                    act.wait_ge(ev["fflip"][s], nth(m, "fflip"))
                    act.activation(big[s][:, 0:512], b[s][2][:, :], ACT.Copy)
                    act.activation(mT[s][:, :], b[s][3][:, 128:192].bitcast(BF16), ACT.Copy).then_inc(ev["fT"][s], 1)

                def gelu():
                    act.wait_ge(ev["fh"][s], nth(m, "fh"))
                    act.activation(big[s][:, 512:1024], b[s][0][:, :], ACT.Gelu).then_inc(ev["fact"][s], 1)

                return {
                    "x4.norm": lambda: flip_out(3), "a2.q": lambda: q_out(2), "a2.v": lambda: v_out(2, T),
                    **attend(2, T, HD ** -0.5 / 0.1),
                    "a2.norm": lambda: o_out(2),
                    "x5.norm": lambda: flip_out(4), "l.qk": wide_q_out, "l.v": wide_v_out, **attend(3, C, LHD ** -0.5),
                    "l.norm": wide_o_out,
                    "x6.norm": lambda: flip_out(5), "f.route": router, "f.flip": masked_out, "f.hidden": gelu,
                }

            walk(act, TURNS_OF["act"], arrivals, layer0, layer1)

        @block.vector
        def _(dve):
            dve.memset(raw[96:128, :], 0.0).then_inc(cleared, 1)
            dve.wait_ge(cleared, CLEARED)
            dve.wait_ge(const_loaded, 32)
            def split(group, *steps):
                at = GROUPS[group]
                for step in steps:
                    if group == step == 0:
                        dve.wait_ge(rows_loaded, 48)
                    if step > 0:
                        dve.wait_ge(parts_step, (SPLIT - 1) * group + step)
                    p = (128, 64, 64, 32, 32)[step]
                    if step % 2 == 0:
                        ins = dve.tensor_copy(part[0:p, at], raw[0:p, at])
                    else:
                        ins = dve.tensor_tensor(raw[0:p, at], raw[0:p, at], part[0:p, at], ALU.subtract)
                    ins.then_inc(parts_ready if step == SPLIT - 1 else parts_step, 1)

            def layer1_arrives():
                dve.wait_ge(w_loaded[3], 16)
                dve.wait_ge(w_loaded[5], 16)

            arrivals = {"a0.norm": lambda: split(0, 0, 1, 2, 3, 4), "a1.proj": lambda: split(1, 0, 1, 2),
                        "a1.norm": lambda: split(1, 3, 4), "e.h3": lambda: dve.wait_ge(w_loaded[2], 16),
                        "e.norms": lambda: split(2, 0, 1, 2, 3, 4), "layer 1": layer1_arrives}

            def parts(layer, late, s, m):
                n = [0]

                def link(ins):
                    n[0] += 1
                    ins.then_inc(dve_order[layer][late], 1)
                    dve.wait_ge(dve_order[layer][late], (SLOTS * m + s) * DVE_LINKS[layer][late] + n[0])

                def hold():
                    dve.memset(pad[s][:, :], 0.0)

                def ln_stats(k, src):
                    if k == 0:
                        dve.wait_ge(ev["x_loaded"][s], nth(m, "x_loaded", 0, 16))
                    link(dve.bn_stats(stats[s][:, :], src[s][:, :]))
                    hold()
                    dve.bn_aggr(mv[s][:, :], stats[s][:, :]).then_inc(ev["var"][s], 1)

                def ln(k, src, dst):
                    dve.wait_ge(ev["rstd"][s], nth(m, "rstd", k))
                    dve.tensor_scalar(dst[s][:, :], src[s][:, :], mv[s][:, 0:1], rstd[s][:, 0:1],
                                      ALU.subtract, ALU.mult).then_inc(ev["xn"][s], 1)

                def k_heads(a, keys):
                    dve.wait_ge(ev["qkv"][s], nth(m, "qkv", a))
                    dve.scalar_tensor_tensor(kx[s][:, 0:4 * keys].rearrange("p (j t) -> p j t", j=4),
                                             b[s][2][:, 0:keys].unsqueeze(1).to_broadcast([128, 4, keys]),
                                             w(3, "bk") if a == 2 else 0.0,
                                             k32("head").unsqueeze(2).to_broadcast([128, 4, keys]), ALU.add, ALU.mult)\
                        .then_inc(ev["kx"][s], 1)

                def shift(a, keys, i):
                    dve.wait_ge(ev["scores"][s], nth(m, "scores", 4 * a + i))
                    sc = b[s][i % 2][:, 0:4 * keys].rearrange("p (j t) -> p j t", j=4)
                    largest = top[s][:, 4 * (i % 2):4 * (i % 2) + 4]
                    link(dve.tensor_reduce(largest, sc, AX.X, ALU.max))
                    if i >= 2:
                        dve.wait_ge(ev["flipped"][s], nth(m, "flipped", 4 * a + i - 2))
                    dve.tensor_tensor(
                        shifted[s][:, 512 * (i % 2):512 * (i % 2) + 4 * keys].rearrange("p (j t) -> p j t", j=4),
                        sc, largest.unsqueeze(2).to_broadcast([128, 4, keys]), ALU.subtract)\
                        .then_inc(ev["shifted"][s], 1)

                def attend(a, keys):
                    return {f"a{a}.shift{i}": lambda i=i: shift(a, keys, i) for i in range(UNITS)}

                def o_norm(a):
                    dve.wait_ge(ev["mixed"][s], nth(m, "mixed", 4 * a + 3))
                    o4 = b[s][3][:, 0:H * (HD + 1)].rearrange("p (h d) -> p h d", d=HD + 1)
                    link(dve.reciprocal(rsum[s][:, :], o4[:, :, HD]))
                    dve.tensor_tensor(o[s][:, :].rearrange("p (h d) -> p h d", d=HD), o4[:, :, 0:HD],
                                      rsum[s][:, :].unsqueeze(2).to_broadcast([128, H, HD]), ALU.mult)\
                        .then_inc(ev["onorm"][s], 1)

                def add_y(k, to, scale, old):
                    dve.wait_ge(ev["y"][s], nth(m, "y", k))
                    link(dve.scalar_tensor_tensor(to[s][:, :], b[s][3][:, 384:512], scale, old[s][:, :],
                                                  ALU.mult, ALU.add))

                return n, link, hold, ln_stats, ln, k_heads, shift, attend, o_norm, add_y

            def layer0(s, m, late):
                n, link, hold, ln_stats, ln, k_heads, shift, attend, o_norm, add_y = parts(0, late, s, m)

                def take_x():
                    add_y(0, res, 1.0, x_in)
                    dve.memset(pad[s][:, :], 0.0).then_inc(ev["x_taken"][s], 1)

                def top_logit():
                    dve.wait_ge(ev["logits"][s], nth(m, "logits", 0))
                    link(dve.tensor_reduce(sm[s][:, 16:17], lg[s][:, :], AX.X, ALU.max))
                    dve.tensor_scalar(sm[s][:, 19:20], sm[s][:, 16:17], -1.0, None, ALU.mult).then_inc(ev["top"][s], 1)

                def route():
                    dve.wait_ge(ev["gexp"][s], nth(m, "gexp"))
                    link(dve.reciprocal(sm[s][:, 21:22], sm[s][:, 20:21]))
                    link(dve.tensor_scalar(pr[s][:, :], pr[s][:, :], sm[s][:, 21:22], None, ALU.mult))
                    hold()
                    link(dve.max(best[s][:, :], pr[s][:, :]))
                    hold()
                    link(dve.max_index(at_best[s][:, :], best[s][:, :], pr[s][:, :]))
                    link(dve.tensor_copy(sm[s][:, 22:24], at_best[s][:, 0:2]))
                    dve.tensor_tensor(sm[s][:, 24:25], sm[s][:, 22:23], sm[s][:, 23:24], ALU.min)
                    link(dve.tensor_tensor(sm[s][:, 25:26], sm[s][:, 22:23], sm[s][:, 23:24], ALU.max))
                    by_part = mk[s][:, :].rearrange("p (a c) -> p a c", a=4)
                    for j in range(2):
                        ins = dve.tensor_scalar(by_part[:, 0:3, NE * j:NE * j + NE],
                                                k32("iota").unsqueeze(1).to_broadcast([128, 3, NE]),
                                                sm[s][:, 24 + j:25 + j], None, ALU.is_equal)
                    ins.then_inc(ev["masks"][s], 1)

                def shared_hidden():
                    dve.wait_ge(ev["shared_silu"][s], nth(m, "shared_silu"))
                    dve.scalar_tensor_tensor(sh[s][:, 128:256], b[s][3][:, 384:512], w(2, "bs3"), sh[s][:, 0:128],
                                             ALU.add, ALU.mult)\
                        .then_inc(ev["shared"][s], 1)

                def chosen_weights():
                    dve.wait_ge(ev["masks"][s], nth(m, "masks"))
                    for j in range(2):
                        ins = dve.tensor_tensor_reduce(out=junk[s][:, NE * j:NE * j + NE], in0=mk[s][:, NE * j:NE * j + NE],
                                                       in1=pr[s][:, :], scale=1.0, scalar=0.0, op0=ALU.mult, op1=ALU.add,
                                                       accum_out=sm[s][:, 26 + j:27 + j])
                    link(ins)

                def hidden():
                    dve.wait_ge(ev["silu"][s], nth(m, "silu"))
                    dve.wait_ge(ev["h3"][s], nth(m, "h3"))
                    for c in range(8):
                        ins = dve.scalar_tensor_tensor(big[s][:, 1024 + 128 * c:1152 + 128 * c],
                                                       b[s][2 + c // 4][:, 128 * (c % 4):128 * (c % 4) + 128],
                                                       w(2, "b3")[:, c:c + 1], big[s][:, 128 * c:128 * c + 128],
                                                       ALU.add, ALU.mult)
                    ins.then_inc(ev["hidden"][s], 1)

                def keep(j, spread, done):
                    dve.wait_ge(ev["hidden"][s], nth(m, "hidden"))
                    dve.wait_ge(ev[spread][s], nth(m, spread))
                    for c in range(2):
                        ins = dve.tensor_tensor(big[s][:, 2048 + 1024 * j + 512 * c:2560 + 1024 * j + 512 * c],
                                                b[s][2 * j + c][:, :], big[s][:, 1024 + 512 * c:1536 + 512 * c], ALU.mult)
                    ins.then_inc(ev[done][s], 1)

                def norms():
                    dve.wait_ge(ev["norms"][s], nth(m, "norms"))
                    for j in range(2):
                        dve.tensor_tensor_reduce(out=junk[s][:, NE * j + 32:NE * j + 32 + NE], in0=b[s][0][:, 0:NE],
                                                 in1=mk[s][:, NE * j:NE * j + NE], scale=1.0, scalar=0.0,
                                                 op0=ALU.mult, op1=ALU.add, accum_out=sm[s][:, j:j + 1])
                    dve.tensor_copy(sm[s][:, 2:3], b[s][0][:, NE:NE + 1]).then_inc(ev["time_in"][s], 1)
                    assert n[0] == DVE_LINKS[0][False], n

                def outputs():
                    dve.wait_ge(ev["time_part"][s], nth(m, "time_part"))
                    dve.scalar_tensor_tensor(oe[s][:, 2 * D:3 * D], w(2, "s2t"), sm[s][:, 5:6], b[s][0][:, 128:256],
                                             ALU.mult, ALU.add)
                    dve.wait_ge(ev["experts"][s], nth(m, "experts"))
                    link(dve.tensor_tensor(oe[s][:, 0:2 * D], b[s][1][:, 0:2 * D], tw[s][:, :], ALU.add))
                    for j in range(3):
                        ins = dve.tensor_tensor_reduce(out=(junk[s][:, :], z[s][:, :], yy[s][:, :])[j],
                                                       in0=oe[s][:, D * j:D * j + D], in1=oe[s][:, D * j:D * j + D],
                                                       scale=1.0, scalar=0.0, op0=ALU.mult, op1=ALU.add,
                                                       accum_out=sm[s][:, 6 + j:7 + j])
                    ins.then_inc(ev["otime_in"][s], 1)

                def onto(k):
                    if k == 0:
                        dve.wait_ge(ev["otime"][s], nth(m, "otime"))
                        link(dve.tensor_copy(oe[s][:, :].rearrange("p (j d) -> p j d", j=3)[:, :, 0], sm[s][:, 9:12]))
                        link(dve.scalar_tensor_tensor(z[s][:, :], oe[s][:, 0:D], sm[s][:, 26:27], k32("origin"),
                                                      ALU.mult, ALU.add))
                    else:
                        dve.wait_ge(ev["rescale"][s], nth(m, "rescale", k - 1))
                        link(dve.scalar_tensor_tensor(z[s][:, :], z[s][:, :], sm[s][:, 18:19], oe[s][:, D * k:D * k + D],
                                                      ALU.mult, ALU.add))
                    link(dve.tensor_tensor_reduce(out=junk[s][:, 1:D], in0=z[s][:, 1:D], in1=z[s][:, 1:D], scale=1.0,
                                                  scalar=0.0, op0=ALU.mult, op1=ALU.add, accum_out=sm[s][:, 15:16]))
                    link(dve.scalar_tensor_tensor(sm[s][:, 16:17], z[s][:, 0:1], z[s][:, 0:1], sm[s][:, 15:16],
                                                  ALU.mult, ALU.subtract))
                    dve.tensor_scalar(sm[s][:, 17:18], sm[s][:, 16:17], 1e-6, None, ALU.max).then_inc(ev["inner"][s], 1)
                    if k == 0:
                        link(dve.tensor_scalar(oe[s][:, D:2 * D], oe[s][:, D:2 * D], sm[s][:, 27:28], None, ALU.mult))

                def end():
                    dve.wait_ge(ev["rescale"][s], nth(m, "rescale", 2))
                    link(dve.scalar_tensor_tensor(res[s][:, :], z[s][:, :], sm[s][:, 18:19], res[s][:, :],
                                                  ALU.mult, ALU.add))
                    assert n[0] == DVE_LINKS[0][True], n

                return {
                    "x0.stats": lambda: ln_stats(0, x_in), "x0.norm": lambda: ln(0, x_in, xn),
                    "a0.proj": lambda: k_heads(0, T), **attend(0, T), "a0.norm": lambda: o_norm(0), "a0.out": take_x,
                    "x1.stats": lambda: ln_stats(1, res), "x1.norm": lambda: ln(1, res, xn),
                    "a1.proj": lambda: k_heads(1, C), **attend(1, C), "a1.norm": lambda: o_norm(1),
                    "a1.out": lambda: add_y(1, res, 1.0, res),
                    "x2.stats": lambda: ln_stats(2, res), "x2.norm": lambda: ln(2, res, xn),
                    "e.gate": top_logit, "e.h1": route, "e.h3": shared_hidden, "e.weights": chosen_weights,
                    "e.hidden": hidden,
                    "e.A": lambda: keep(0, "spreadA", "hA"), "e.B": lambda: keep(1, "spreadB", "hB"),
                    "e.norms": norms, "e.out": outputs, "e.step0": lambda: onto(0), "e.step1": lambda: onto(1),
                    "e.step2": lambda: onto(2), "e.end": end,
                }

            def layer1(s, m, late):
                n, link, hold, ln_stats, ln, k_heads, shift, attend, o_norm, add_y = parts(1, late, s, m)

                def inner_stats():
                    dve.wait_ge(ev["xn"][s], nth(m, "xn", 3))
                    ln_stats(4, xl)

                def gated_heads():
                    k_heads(2, T)
                    dve.wait_ge(ev["gate_exp"][s], nth(m, "gate_exp"))
                    link(dve.tensor_scalar(gate[s][:, 1:2], gate[s][:, 0:1], 1.0, None, ALU.add))
                    link(dve.reciprocal(gate[s][:, 0:1], gate[s][:, 1:2]))
                    dve.tensor_scalar(gate[s][:, 1:2], gate[s][:, 0:1], 0.1, 2.0, ALU.max, ALU.min)\
                        .then_inc(ev["key_gate"][s], 1)

                def wide_k():
                    dve.wait_ge(ev["lk"][s], nth(m, "lk"))
                    k4 = wide[s][:, 0:16 * C].rearrange("p (c e t) -> p c e t", c=8, e=2)
                    for c in range(2):
                        src = b[s][2 + c][:, 0:4 * C].rearrange("p (c t) -> p c t", c=4)
                        for e in range(2):
                            ins = dve.tensor_scalar(k4[:, 4 * c:4 * c + 4, e, :], src, k32("pair")[:, e:e + 1], None,
                                                    ALU.mult)
                        ins.then_inc(ev["lks"][s], 1)

                def wide_norm(i):
                    dve.wait_ge(ev["mixed"][s], nth(m, "mixed", 12 + i))
                    o4 = b[s][3][:, 0:4 * (LHD + 1)].rearrange("p (h d) -> p h d", d=LHD + 1)
                    link(dve.reciprocal(rsum[s][:, 0:4], o4[:, :, LHD]))
                    at = 1024 + 256 * i
                    dve.tensor_tensor(big[s][:, at:at + 256].rearrange("p (h d) -> p h d", d=LHD), o4[:, :, 0:LHD],
                                      rsum[s][:, 0:4].unsqueeze(2).to_broadcast([128, 4, LHD]), ALU.mult)\
                        .then_inc(ev["onorm"][s], 1)

                def route():
                    dve.wait_ge(ev["logits"][s], nth(m, "logits", 1))
                    link(dve.tensor_reduce(sm[s][:, 16:17], lg[s][:, 0:NF], AX.X, ALU.max))
                    link(dve.tensor_scalar(sm[s][:, 19:23], lg[s][:, 0:NF], sm[s][:, 16:17], None, ALU.is_equal))
                    link(dve.scalar_tensor_tensor(sm[s][:, 24:28], sm[s][:, 19:23], -float(NE), k32("iota_up")[:, 0:NF],
                                                  ALU.mult, ALU.add))
                    link(dve.tensor_reduce(sm[s][:, 16:17], sm[s][:, 24:28], AX.X, ALU.min))
                    link(dve.tensor_scalar(sm[s][:, 19:23], k32("iota")[:, 0:NF], sm[s][:, 16:17], None, ALU.is_equal))
                    by_part = mk[s][:, :].rearrange("p (a c) -> p a c", a=4)
                    dve.tensor_copy(by_part[:, 0:3, 0:NF], sm[s][:, 19:23].unsqueeze(1).to_broadcast([128, 3, NF]))
                    dve.tensor_tensor(big[s][:, 3072:3584].rearrange("p (e d) -> p e d", e=NF),
                                      xn[s][:, :].unsqueeze(1).to_broadcast([128, NF, D]),
                                      sm[s][:, 19:23].unsqueeze(2).to_broadcast([128, NF, D]), ALU.mult)\
                        .then_inc(ev["fmasked"][s], 1)
                    assert n[0] == DVE_LINKS[1][False], n

                def end():
                    dve.wait_ge(ev["xn"][s], nth(m, "xn", 7))
                    link(dve.tensor_tensor(z[s][:, :], yy[s][:, :], w(5, "g"), ALU.mult))
                    link(dve.tensor_tensor(yy[s][:, :], z[s][:, :], w(5, "b"), ALU.add))
                    dve.wait_ge(out_free[s], m * 16 + 16)
                    dve.tensor_tensor(x_out[s][:, :], yy[s][:, :], res[s][:, :], ALU.add).then_inc(ev["out_ready"][s], 1)
                    assert n[0] == DVE_LINKS[1][True], n

                return {
                    "x3.stats": lambda: ln_stats(3, res), "x3.norm": lambda: ln(3, res, xl),
                    "x4.stats": inner_stats, "x4.norm": lambda: ln(4, xl, xn),
                    "a2.proj": gated_heads, **attend(2, T), "a2.norm": lambda: o_norm(2),
                    "a2.out": lambda: add_y(2, res, 0.1, res),
                    "x5.stats": lambda: ln_stats(5, res), "x5.norm": lambda: ln(5, res, xn), "l.qk": wide_k,
                    "a3.shift0": lambda: shift(3, C, 0), "a3.shift1": lambda: shift(3, C, 1),
                    "a3.shift2": lambda: shift(3, C, 2), "l.norm0": lambda: wide_norm(0),
                    "a3.shift3": lambda: shift(3, C, 3), "l.norm1": lambda: wide_norm(1),
                    "l.norm2": lambda: wide_norm(2), "l.norm3": lambda: wide_norm(3),
                    "l.out": lambda: add_y(3, res, 1.0, res),
                    "x6.stats": lambda: ln_stats(6, res), "x6.norm": lambda: ln(6, res, xn), "f.route": route,
                    "f.out": lambda: add_y(4, z, 1.0, xn),
                    "x7.stats": lambda: ln_stats(7, z), "x7.norm": lambda: ln(7, z, yy), "f.end": end,
                }

            walk(dve, TURNS_OF["dve"], arrivals, layer0, layer1)

        @block.tensor
        def _(pe):
            ident = k32("ident")
            pe.wait_ge(const_loaded, 32)
            pe.wait_ge(w_loaded[0], 16)
            pe.wait_ge(cleared, CLEARED)

            def arrived(sublayers, groups):
                for i in sublayers:
                    pe.wait_ge(w_loaded[i], 16)
                if groups:
                    pe.wait_ge(parts_ready, groups)

            arrivals = {"a1.proj": lambda: arrived([1], 0), "a1.out": lambda: arrived([], 1), "e.gate": lambda: arrived([2], 2),
                        "layer 1": lambda: arrived([3, 4, 5], 3)}

            def parts(s, m):
                def flip(k):
                    pe.wait_ge(ev["xn"][s], nth(m, "xn", (0, 1, 2, 4, 5, 6)[k]))
                    pe.transpose(b[s][3][:, 0:T], xn[s][:, :], ident).then_inc(ev["xflip"][s], 1)

                def project(a, i, keys):
                    pe.wait_ge(ev["xT"][s], nth(m, "xT", (0, 1, 3)[a]))
                    kvT, depth = xT[s][:, :], 128
                    if a == 1:
                        pe.wait_ge(ev["ctx_loaded"][s], nth(m, "ctx_loaded", 0, 16))
                        kvT, depth = ctx_in[s][:, :], CD + 1
                    pe.matmul(b[s][2][:, 0:keys], w(i, "k", depth), kvT, start=True, stop=True)
                    pe.matmul(b[s][3][:, 128:256], w(i, "q"), xT[s][:, :], start=True, stop=True)
                    wv = w(i, "v", depth)
                    if a == 2:
                        wv = W[i][:, wcol[i][0]["v"].start:wcol[i][0]["ent"].stop]
                    last = pe.matmul(b[s][3][0:keys, 256:256 + wv.shape[1]], kvT, wv, start=True, stop=(a != 2))
                    if a == 2:
                        last = pe.matmul(b[s][3][:, 256:386], k16("ones"),
                                         part[:, rcol["v"].start:rcol["ent"].stop], start=False, stop=True)
                    last.then_inc(ev["qkv"][s], 1)

                def scores(a, keys, i):
                    if a < 3:
                        pe.wait_ge(ev["q"][s], nth(m, "q", 4 * a + i))
                    if i == 0 and a < 3:
                        pe.wait_ge(ev["kx"][s], nth(m, "kx", a))
                    if i == 0 and a == 3:
                        pe.wait_ge(ev["lqs"][s], nth(m, "lqs"))
                    if i % 2 == 0 and a == 3:
                        pe.wait_ge(ev["lks"][s], nth(m, "lks", i // 2))
                    if i >= 2:
                        pe.wait_ge(ev["shifted"][s], nth(m, "shifted", 4 * a + i - 2))
                    sc = b[s][i % 2]
                    if a == 3:
                        for c in range(2 * i, 2 * i + 2):
                            last = pe.matmul(sc[:, 2 * C * (c % 2):2 * C * (c % 2) + 2 * C],
                                             big[s][:, 128 * c:128 * c + 128], wide[s][:, 2 * C * c:2 * C * c + 2 * C],
                                             start=True, stop=True)
                    else:
                        last = pe.matmul(sc[:, 0:4 * keys], qq[s][:, T * i:T * i + T], kx[s][:, 0:4 * keys],
                                         start=True, stop=(a == 1))
                        if a != 1:
                            last = pe.matmul(sc[:, :], k16("ident"), k16("causal").unsqueeze(1).to_broadcast([128, 4, T]),
                                             start=False, stop=(a == 2))
                        if a == 0:
                            last = pe.matmul(sc[:, :], k16("alibi_q"), k16("alibi_k")[:, 4 * T * i:4 * T * i + 4 * T],
                                             start=False, stop=True)
                    last.then_inc(ev["scores"][s], 1)

                def flip_scores(a, keys, i):
                    pe.wait_ge(ev["shifted"][s], nth(m, "shifted", 4 * a + i))
                    if i == 0 and a == 3:
                        pe.wait_ge(ev["lvs"][s], nth(m, "lvs"))
                    if i >= 1:
                        pe.wait_ge(ev["probs"][s], nth(m, "probs", 4 * a + i - 1))
                    at = 512 * (i % 2)
                    for j in range(4):
                        last = pe.transpose(b[s][2][0:keys, T * j:T * j + T],
                                            shifted[s][:, at + keys * j:at + keys * j + keys], ident)
                    last.then_inc(ev["flipped"][s], 1)

                def mix(a, keys, i, v, depth):
                    pe.wait_ge(ev["probs"][s], nth(m, "probs", 4 * a + i))
                    if a < 3 and i == 0:
                        pe.wait_ge(ev["v"][s], nth(m, "v", a))
                    if a == 3 and i >= 1:
                        pe.wait_ge(ev["onorm"][s], nth(m, "onorm", 3 + i - 1))
                    at = 512 * (i % 2)
                    for j in range(4):
                        h = 4 * i + j
                        to = depth * (j if a == 3 else h)
                        last = pe.matmul(b[s][3][:, to:to + depth], probs[s][0:keys, at + T * j:at + T * j + T],
                                         v[s][0:keys, depth * h:depth * h + depth], start=True, stop=True)
                    last.then_inc(ev["mixed"][s], 1)

                def attend(a, keys, v, depth):
                    steps = {}
                    for i in range(UNITS + 2):
                        if i < UNITS:
                            steps[f"a{a}.scores{i}"] = lambda i=i: scores(a, keys, i)
                        if 1 <= i <= UNITS:
                            steps[f"a{a}.flip{i - 1}"] = lambda i=i: flip_scores(a, keys, i - 1)
                        if i >= 2:
                            steps[f"a{a}.mix{i - 2}"] = lambda i=i: mix(a, keys, i - 2, v, depth)
                    return steps

                def o_flip(a):
                    pe.wait_ge(ev["onorm"][s], nth(m, "onorm", a))
                    pe.transpose(b[s][3][:, 256:384], o[s][:, :], ident).then_inc(ev["oflip"][s], 1)

                def output(a, i, bias):
                    pe.wait_ge(ev["oT"][s], nth(m, "oT", a))
                    last = pe.matmul(b[s][3][:, 384:512], oT[s][:, :], w(i, "o"), start=True, stop=(bias is None))
                    if bias is not None:
                        last = pe.matmul(b[s][3][:, 384:512], k16("ones"), row(bias), start=False, stop=True)
                    last.then_inc(ev["y"][s], 1)

                def chunked_output(src, at, chunks, i, name, bias):
                    for c in range(chunks):
                        pe.matmul(b[s][3][:, 384:512], src[s][:, at + 128 * c:at + 128 * c + 128],
                                  w(i, name)[:, 128 * c:128 * c + 128], start=(c == 0), stop=False)
                    pe.matmul(b[s][3][:, 384:512], k16("ones"), row(bias), start=False, stop=True)\
                        .then_inc(ev["y"][s], 1)

                return flip, project, attend, o_flip, output, chunked_output

            def layer0(s, m, late):
                flip, project, attend, o_flip, output, chunked_output = parts(s, m)

                def mlp():
                    pe.wait_ge(ev["oT"][s], nth(m, "oT", 1))
                    for c in range(2):
                        last = pe.matmul(b[s][3][:, D * c:D * c + D], w(1, "m1")[:, D * c:D * c + D], oT[s][:, :],
                                         start=True, stop=True)
                    last.then_inc(ev["mlp"][s], 1)

                def mlp_out():
                    pe.wait_ge(ev["mlp_act"][s], nth(m, "mlp_act"))
                    chunked_output(mh, 0, 2, 1, "m2", "xm2")

                def router():
                    pe.wait_ge(ev["xT"][s], nth(m, "xT", 2))
                    pe.matmul(b[s][3][:, 128:128 + NE], xT[s][:, :], w(2, "gate"), start=True, stop=True)
                    for name, at in (("s1", 256), ("s3", 384)):
                        last = pe.matmul(b[s][3][:, at:at + 128], w(2, name), xT[s][:, :], start=True, stop=True)
                    last.then_inc(ev["gate"][s], 1)

                def hidden(name, c, to):
                    return pe.matmul(to, w(2, name)[:, 128 * c:128 * c + 128], xT[s][:, :], start=True, stop=True)

                def h1():
                    for c in range(8):
                        last = hidden("w1", c, b[s][c // 4][:, 128 * (c % 4):128 * (c % 4) + 128])
                    last.then_inc(ev["h1"][s], 1)

                def h3_low():
                    for c in range(4):
                        hidden("w3", c, b[s][2][:, 128 * c:128 * c + 128])

                def flip_masks():
                    pe.wait_ge(ev["shared"][s], nth(m, "shared"))
                    pe.wait_ge(ev["masks"][s], nth(m, "masks"))
                    pe.transpose(b[s][3][:, 128:192].bitcast(BF16), mk[s][:, :], k16("ident")).then_inc(ev["mflip"][s], 1)

                def h3_high():
                    pe.wait_ge(ev["maskT"][s], nth(m, "maskT"))
                    for c in range(4, 8):
                        last = hidden("w3", c, b[s][3][:, 128 * (c - 4):128 * (c - 4) + 128])
                    last.then_inc(ev["h3"][s], 1)

                def spread(j, name):
                    pe.wait_ge(ev["hidden"][s], nth(m, "hidden"))
                    for c in range(8):
                        last = pe.matmul(b[s][2 * j + c // 4][:, 128 * (c % 4):128 * (c % 4) + 128],
                                         k16("sel")[:, 128 * (8 * j + c):128 * (8 * j + c) + 128], mT[s][:, :],
                                         start=True, stop=True)
                    last.then_inc(ev[name][s], 1)

                def norms():
                    pe.wait_ge(ev["square"][s], nth(m, "square"))
                    pe.wait_ge(ev["hA"][s], nth(m, "hA"))
                    pe.matmul(b[s][0][:, 128:256], sh[s][:, 128:256], w(2, "s2"), start=True, stop=False)
                    pe.matmul(b[s][0][:, 128:256], k16("ones"), row("s2"), start=False, stop=True)
                    for j, name in enumerate("AB"):
                        pe.matmul(b[s][0][:, 256 + D * j:256 + D * j + D], mT[s][:, :], row("t" + name),
                                  start=True, stop=True)
                    for c in range(8):
                        pe.matmul(b[s][0][:, 2 * c:2 * c + 2], wide[s][:, 128 * c:128 * c + 128], k32("pair"),
                                  start=True, stop=True)
                    pe.matmul(b[s][0][:, 16:18], sh[s][:, 256:384], k32("ones"), start=True, stop=True)\
                        .then_inc(ev["norms"][s], 1)

                def outputs(j, name):
                    if j == 1:
                        pe.wait_ge(ev["hB"][s], nth(m, "hB"))
                    to = b[s][1][:, D * j:D * j + D]
                    for c in range(8):
                        pe.matmul(to, big[s][:, 2048 + 1024 * j + 128 * c:2176 + 1024 * j + 128 * c],
                                  w(2, "w2")[:, 128 * c:128 * c + 128], start=(c == 0), stop=False)
                    last = pe.matmul(to, mT[s][:, :], row("e" + name), start=False, stop=True)
                    if j == 1:
                        last.then_inc(ev["experts"][s], 1)

                return {
                    "x0.norm": lambda: flip(0), "a0.proj": lambda: project(0, 0, T), **attend(0, T, vv, HD + 1),
                    "a0.norm": lambda: o_flip(0), "a0.out": lambda: output(0, 0, None),
                    "x1.norm": lambda: flip(1), "a1.proj": lambda: project(1, 1, C), **attend(1, C, vv, HD + 1),
                    "a1.norm": lambda: o_flip(1), "a1.mlp": mlp, "a1.out": mlp_out,
                    "x2.norm": lambda: flip(2), "e.gate": router, "e.h1": h1, "e.h3": h3_low, "e.flip": flip_masks,
                    "e.hidden": h3_high, "e.A": lambda: spread(0, "spreadA"), "e.B": lambda: spread(1, "spreadB"),
                    "e.norms": norms, "e.outA": lambda: outputs(0, "A"), "e.outB": lambda: outputs(1, "B"),
                }

            def layer1(s, m, late):
                flip, project, attend, o_flip, output, chunked_output = parts(s, m)

                def wide_kq():
                    pe.wait_ge(ev["xT"][s], nth(m, "xT", 4))
                    for c in range(8):
                        last = pe.matmul(b[s][2 + c // 4][:, C * (c % 4):C * (c % 4) + C],
                                         w(4, "k", CD)[:, 128 * c:128 * c + 128], ctx_in[s][0:CD, :], start=True, stop=True)
                    last.then_inc(ev["lk"][s], 1)
                    for c in range(8):
                        last = pe.matmul(b[s][c // 4][:, 128 * (c % 4):128 * (c % 4) + 128],
                                         w(4, "q")[:, 128 * c:128 * c + 128], xT[s][:, :], start=True, stop=True)
                    last.then_inc(ev["lq"][s], 1)

                def wide_v():
                    for j in range(2):
                        pe.wait_ge(ev["lks"][s], nth(m, "lks", j))
                        last = pe.matmul(b[s][2 + j][0:C, :], ctx_in[s][0:CD, :], w(4, "v", CD)[:, 512 * j:512 * j + 512],
                                         start=True, stop=True)
                    last.then_inc(ev["lv"][s], 1)

                def wide_flip():
                    pe.wait_ge(ev["onorm"][s], nth(m, "onorm", 6))
                    for c in range(8):
                        last = pe.transpose(b[s][c // 4][:, 128 * (c % 4):128 * (c % 4) + 128],
                                            big[s][:, 1024 + 128 * c:1152 + 128 * c], ident)
                    last.then_inc(ev["oflip"][s], 1)

                def wide_out():
                    pe.wait_ge(ev["oT"][s], nth(m, "oT", 3))
                    chunked_output(big, 2048, 8, 4, "o", "lo")

                def router():
                    pe.wait_ge(ev["xT"][s], nth(m, "xT", 5))
                    pe.matmul(b[s][3][:, 128:128 + NF], xT[s][:, :], w(5, "r"), start=True, stop=True)\
                        .then_inc(ev["flogits"][s], 1)

                def flip_masked():
                    pe.wait_ge(ev["fmasked"][s], nth(m, "fmasked"))
                    for e in range(NF):
                        pe.transpose(b[s][2][:, T * e:T * e + T], big[s][:, 3072 + D * e:3072 + D * e + D], ident)
                    pe.transpose(b[s][3][:, 128:192].bitcast(BF16), mk[s][:, :], k16("ident")).then_inc(ev["fflip"][s], 1)

                def hidden():
                    pe.wait_ge(ev["fT"][s], nth(m, "fT"))
                    for c in range(4):
                        to = b[s][0][:, 128 * c:128 * c + 128]
                        for e in range(NF):
                            pe.matmul(to, w(5, "w1")[:, FI * e + 128 * c:FI * e + 128 * c + 128],
                                      big[s][:, T * e:T * e + T], start=(e == 0), stop=False)
                        last = pe.matmul(to, row("f1")[:, 128 * c:128 * c + 128], mT[s][:, :], start=False, stop=True)
                    last.then_inc(ev["fh"][s], 1)

                def out():
                    pe.wait_ge(ev["fact"][s], nth(m, "fact"))
                    chunked_output(big, 512, 4, 5, "o", "fo")

                wide_attention = attend(3, C, lv, LHD + 1)
                return {
                    "x4.norm": lambda: flip(3), "a2.proj": lambda: project(2, 3, T), **attend(2, T, vv, HD + 1),
                    "a2.norm": lambda: o_flip(2), "a2.out": lambda: output(2, 3, "ao"),
                    "x5.norm": lambda: flip(4), "l.kq": wide_kq, "a3.scores0": wide_attention["a3.scores0"],
                    "l.v": wide_v, **wide_attention,
                    "l.norm": wide_flip, "l.out": wide_out,
                    "x6.norm": lambda: flip(5), "f.route": router, "f.flip": flip_masked, "f.hidden": hidden,
                    "f.out": out,
                }

            walk(pe, TURNS_OF["pe"], arrivals, layer0, layer1)


CLEARED = 9 + 4 * SLOTS


def _bf16_parts(a):
    out = []
    for _ in range(3):
        hi = a.astype("bfloat16").astype(np.float32)
        out.append(hi)
        a = a - hi
    return out


def _constants():
    ccol, n16 = columns(CONST16)
    fcol, n32 = columns(CONST32)
    c16 = np.zeros((128, n16), np.float32)
    c32 = np.zeros((128, n32), np.float32)
    p = np.arange(128)
    c16[:, ccol["ident"]] = np.eye(128)
    c16[:, ccol["causal"]] = np.where(p[:, None] >= np.arange(T)[None, :], 0.0, NEG)
    slopes = (2.0 ** (-0.5 * (np.arange(H) + 1))).astype(np.float32)
    by_key = (slopes[:, None] * np.arange(T, dtype=np.float32)[None, :]).reshape(-1)
    unscale = np.float32(HD ** 0.5)
    for q, (a, s) in enumerate(zip(_bf16_parts(by_key * unscale), _bf16_parts(np.repeat(slopes, T) * unscale))):
        c16[32 * q, ccol["ones"]] = 1.0
        c16[32 * q, ccol["alibi_q"]] = 1.0
        c16[32 * q + 1, ccol["alibi_q"]] = -np.arange(T)
        c16[32 * q, ccol["alibi_k"]] = a
        c16[32 * q + 1, ccol["alibi_k"]] = s
    sel = c16[:, ccol["sel"]].reshape(128, 2, 8, 2, EI)
    for j in range(2):
        for e in range(NE):
            sel[NE * j + e, j, e // 2, e % 2, :] = 1.0
    c16[:, ccol["sel"]] = sel.reshape(128, -1)
    c32[:, fcol["ident"]] = np.eye(128)
    c32[:, fcol["head"]] = (p[:, None] % 32) // HD == np.arange(4)[None, :]
    c32[:, fcol["iota"]] = np.arange(NE)
    c32[:, fcol["iota_up"]] = np.arange(NE) + NE
    c32[:, fcol["origin"]] = np.arange(D) == 0
    c32[:, fcol["pair"]] = p[:, None] // EI == np.arange(2)[None, :]
    c32[:, fcol["ones"]] = 1.0
    return c16.astype("bfloat16"), c32


def _blank(table, n=128):
    cols, width = columns(table)
    return cols, np.zeros((n, width), np.float32)


def _chunks(a):
    return a.reshape(-1, 128, a.shape[1]).transpose(1, 0, 2).reshape(128, -1)


def _weights(i):
    out = []
    c, a = _blank(WEIGHTS[0])
    wqkv = i["L0_attn_Wqkv"]
    a[:, 0:3 * D] = wqkv
    a[:, c["o"]] = i["L0_attn_Wout"]
    out.append(a)
    c, a = _blank(WEIGHTS[1])
    a[:, c["q"]] = i["L0_xattn_Wq"]
    a[0:CD, c["k"]], a[CD, c["k"]] = i["L0_xattn_Wk"], i["L0_xattn_bk"]
    a[0:CD, c["v"]], a[CD, c["v"]] = i["L0_xattn_Wv"], i["L0_xattn_bv"]
    a[:, c["m1"]] = i["L0_xattn_W1"]
    a[:, c["m2"]] = _chunks(i["L0_xattn_W2"])
    a[:, c["bq"]] = i["L0_xattn_bq"][:, None]
    a[:, c["bm1"]] = i["L0_xattn_b1"].reshape(2, D).T
    out.append(a)
    c, a = _blank(WEIGHTS[2])
    a[:, c["gate"]] = i["L0_ffn_gate_w"].T
    for name, src in (("w1", "We1"), ("w3", "We3")):
        padded = np.zeros((NE, EI, D), np.float32)
        padded[:, 1:] = i["L0_ffn_" + src]
        a[:, c[name]] = padded.reshape(NE * EI, D).T
    w2 = np.zeros((NE, EI, D), np.float32)
    w2[:, 1:, 1:] = i["L0_ffn_We2"].transpose(0, 2, 1)[:, 1:]
    a[:, c["w2"]] = _chunks(w2.reshape(NE * EI, D))
    for name, src in (("s1", "Ws1"), ("s3", "Ws3")):
        padded = np.zeros((D, D), np.float32)
        padded[1:] = i["L0_ffn_" + src]
        a[:, c[name]] = padded.T
    s2 = np.zeros((D, D), np.float32)
    s2[1:, 1:] = i["L0_ffn_Ws2"].T[1:]
    a[:, c["s2"]] = s2
    t = np.zeros((D,), np.float32)
    t[1:] = i["L0_ffn_Ws2"][:, 0]
    a[:, c["s2t"]] = t
    for name in ("s1", "s3"):
        a[1:, c["b" + name].start] = i["L0_ffn_b" + name]
    for name in ("1", "3"):
        padded = np.zeros((NE, EI), np.float32)
        padded[:, 1:] = i["L0_ffn_be" + name]
        a[:, c["b" + name]] = padded.reshape(NE * EI // 128, 128).T
    out.append(a)
    c, a = _blank(WEIGHTS[3])
    a[:, 0:3 * D] = i["L1_attn_w_qkv"].T
    a[:, c["ent"].start] = i["L1_attn_w_ent"][0]
    a[:, c["o"]] = i["L1_attn_w_out"].T
    a[:, c["g"]] = i["L1_attn_ln_g"][:, None]
    a[:, c["b"]] = i["L1_attn_ln_b"][:, None]
    a[:, c["bq"]] = i["L1_attn_b_qkv"][0:D, None]
    a[:, c["bk"]] = i["L1_attn_b_qkv"][D:2 * D, None]
    out.append(a)
    c, a = _blank(WEIGHTS[4])
    a[:, c["q"]] = i["L1_xattn_w_q"]
    a[0:CD, c["k"]] = i["L1_xattn_w_k"]
    a[0:CD, c["v"]] = i["L1_xattn_w_v"]
    a[:, c["o"]] = _chunks(i["L1_xattn_w_o"])
    out.append(a)
    c, a = _blank(WEIGHTS[5])
    a[:, c["r"]] = i["L1_ffn_W_router"]
    a[:, c["w1"]] = i["L1_ffn_W1"].transpose(1, 0, 2).reshape(D, NF * FI)
    a[:, c["o"]] = _chunks(i["L1_ffn_Wo"])
    a[:, c["g"]] = i["L1_ffn_ln_gamma"]
    a[:, c["b"]] = i["L1_ffn_ln_beta"]
    out.append(a)
    return out


def _rows(i):
    c, a = _blank(ROWS, 32)
    a[0, c["xm2"]] = i["L0_xattn_b2"]
    a[0, c["s2"].start + 1:c["s2"].stop] = i["L0_ffn_bs2"]
    for j, name in enumerate("AB"):
        a[NE * j:NE * j + NE, c["e" + name].start + 1:c["e" + name].stop] = i["L0_ffn_be2"]
        a[NE * j:NE * j + NE, c["t" + name].start + 1:c["t" + name].stop] = i["L0_ffn_We2"][:, :, 0]
    a[0, c["v"]] = i["L1_attn_b_qkv"][2 * D:]
    a[0, c["ent"].start] = i["L1_attn_b_ent"][0]
    a[0, c["ao"]] = i["L1_attn_b_out"]
    a[0, c["lo"]] = i["L1_xattn_b_o"]
    a[0, c["fo"]] = i["L1_ffn_bo"]
    a[0:NF, c["f1"]] = i["L1_ffn_b1"]
    return a


def kernel(**inputs):
    import concourse.bacc as _bacc
    from concourse.bass_utils import run_bass_kernel_spmd as _run

    i = {name: np.asarray(a) for name, a in inputs.items()}
    ctx = np.ones((B, CD + 1, C), np.float32)
    ctx[:, 0:CD] = i["ctx_768"].transpose(0, 2, 1)
    c16, c32 = _constants()
    arrays = {"x": np.ascontiguousarray(i["x"]), "ctx": ctx}
    for n, a in enumerate(_weights(i)):
        arrays[f"weights_{n}"] = np.ascontiguousarray(a)
    arrays["rows"] = _rows(i)
    arrays["c16"], arrays["c32"] = c16, c32

    nc = _bacc.Bacc("TRN2", target_bir_lowering=False, num_devices=1)
    ap = {n: nc.dram_tensor(n + "_dram", a.shape, mybir.dt.from_np(a.dtype), kind="ExternalInput").ap()
          for n, a in arrays.items()}
    out = nc.dram_tensor("out_dram", (B, T, D), F32, kind="ExternalOutput").ap()
    decoder(nc, ap["x"], ap["ctx"], [ap[f"weights_{n}"] for n in range(6)], ap["rows"], ap["c16"], ap["c32"], out)
    r = _run(nc, [{n + "_dram": a for n, a in arrays.items()}], core_ids=[0])
    return r.results[0]["out_dram"]
```
